# Optimizing a Trainium2 kernel written in Bass

```python
import numpy as np
import jax
import jax.numpy as jnp

def _softmax(x, axis=-1):
    return jax.nn.softmax(x, axis=axis)

def _gelu(x):
    return jax.nn.gelu(x, approximate=True)

def _silu(x):
    return jax.nn.silu(x)

def _sigmoid(x):
    return jax.nn.sigmoid(x)

def _layernorm(x, axis=-1, eps=1e-05):
    m = jnp.mean(x, axis=axis, keepdims=True)
    v = jnp.var(x, axis=axis, keepdims=True)
    return (x - m) / jnp.sqrt(v + eps)

def _scatter_add(tgt, idx, src, axis=0):
    return tgt.at[idx].add(src)

def _segment_sum(src, seg, n):
    return jax.ops.segment_sum(src, seg, n)
kernel_name = 'mk_decoder_postln_d1_seqx_r8_1b9ce9'

def setup_inputs(seed: int=0):
    np.random.seed(seed)
    _w = jnp.asarray

    def _rec_inputs():
        import jax
        import jax.numpy as jnp
        _rk = jax.random.key(seed)
        x = 7.22e-05 + 1 * jax.random.normal(jax.random.fold_in(_rk, 1), (32, 64, 512), jnp.float32)
        _lenS = 64 - jax.random.randint(jax.random.fold_in(_rk, 7), (32,), 0, max(1, 64 // 4) + 1, jnp.int32)
        _lenS2 = 64 - jax.random.randint(jax.random.fold_in(_rk, 8), (32,), 0, max(1, 64 // 4) + 1, jnp.int32)
        _ctx_4096P = jax.random.normal(jax.random.fold_in(_rk, 11), (32, 16, 512), jnp.float32)
        _ctx_4096c = jax.random.dirichlet(jax.random.fold_in(_rk, 511), 0.3 * jnp.ones((16,), jnp.float32), (32, 64))
        _ctx_4096t = jnp.einsum('bsk,bkd->bsd', _ctx_4096c, _ctx_4096P)
        _ctx_4096t = _ctx_4096t * jax.lax.rsqrt(jnp.mean(jnp.square(_ctx_4096t)) + 1e-12) * 0.953939
        ctx_4096 = 4.13588e-05 + 0.999923 * (_ctx_4096t + 0.3 * jax.random.normal(jax.random.fold_in(_rk, 611), (32, 64, 512), jnp.float32))
        _validS = jnp.arange(64)[None, :] < _lenS[:, None]
        _validS2 = jnp.arange(64)[None, :] < _lenS2[:, None]
        _causal = jnp.tril(jnp.ones((64, 64), dtype=bool))
        mask_BxSxS2_ff1 = jnp.where(jnp.ones((32, 64, 64), dtype=bool), 1.0, 0.0).astype(jnp.float32)
        return (x, ctx_4096, mask_BxSxS2_ff1)
    x, ctx_4096, mask_BxSxS2_ff1 = _rec_inputs()

    def _L0_attn_setup():
        import jax, jax.numpy as jnp
        import numpy as np
        import math
        B, L, D, H = (32, 64, 512, 32)
        HD = D // H
        key = jax.random.key(seed)
        ks = jax.random.split(key, 9)
        s = 1.0 / math.sqrt(D)
        return {'x': jax.random.normal(ks[0], (B, L, D), jnp.float32), 'Wq': jax.random.normal(ks[1], (D, D), jnp.float32) * s, 'bq': jax.random.normal(ks[2], (D,), jnp.float32) * s, 'Wk': jax.random.normal(ks[3], (D, D), jnp.float32) * s, 'bk': jax.random.normal(ks[4], (D,), jnp.float32) * s, 'Wv': jax.random.normal(ks[5], (D, D), jnp.float32) * s, 'bv': jax.random.normal(ks[6], (D,), jnp.float32) * s, 'Wo': jax.random.normal(ks[7], (D, D), jnp.float32) * s, 'bo': jax.random.normal(ks[8], (D,), jnp.float32) * s}
    _L0_attn_all = _L0_attn_setup()
    _L0_attn_in = {k: v for k, v in _L0_attn_all.items() if k in ('Wq', 'bq', 'Wk', 'bk', 'Wv', 'bv', 'Wo', 'bo')}
    del _L0_attn_all

    def _L0_xattn_setup():
        import jax, jax.numpy as jnp
        import numpy as np
        N_Q_HEADS = 32
        N_KV_HEADS = 8
        D_MODEL = 512
        D_K = 128
        D_V = 128
        ROPE_BASE = 10000.0

        def _rope(x):
            d = x.shape[-1]
            s = x.shape[2]
            inv_freq = 1.0 / ROPE_BASE ** (jnp.arange(0, d, 2, dtype=jnp.float32) / d)
            ang = jnp.arange(s, dtype=jnp.float32)[:, None] * inv_freq[None, :]
            cos = jnp.concatenate([jnp.cos(ang), jnp.cos(ang)], axis=-1)[None, None]
            sin = jnp.concatenate([jnp.sin(ang), jnp.sin(ang)], axis=-1)[None, None]
            x1, x2 = (x[..., :d // 2], x[..., d // 2:])
            rot = jnp.concatenate([-x2, x1], axis=-1)
            return x * cos + rot * sin
        key = jax.random.key(seed)
        ks = jax.random.split(key, 8)
        bs, s = (2, 128)
        inp = {'query': jax.random.normal(ks[0], (bs, s, D_MODEL), dtype=jnp.float32), 'key': jax.random.normal(ks[1], (bs, s, D_MODEL), dtype=jnp.float32), 'value': jax.random.normal(ks[2], (bs, s, D_MODEL), dtype=jnp.float32), 'mask': jnp.ones((bs, s, s), dtype=jnp.float32), 'wq': jax.random.normal(ks[3], (D_MODEL, N_Q_HEADS * D_K), dtype=jnp.float32) * 0.02, 'wk': jax.random.normal(ks[4], (D_MODEL, N_KV_HEADS * D_K), dtype=jnp.float32) * 0.02, 'wv': jax.random.normal(ks[5], (D_MODEL, N_KV_HEADS * D_V), dtype=jnp.float32) * 0.02, 'wo': jax.random.normal(ks[6], (N_Q_HEADS * D_V, D_MODEL), dtype=jnp.float32) * 0.02}
        return inp
    _L0_xattn_all = _L0_xattn_setup()
    _L0_xattn_in = {k: v for k, v in _L0_xattn_all.items() if k in ('wq', 'wk', 'wv', 'wo')}
    del _L0_xattn_all

    def _L0_ffn_setup():
        import jax, jax.numpy as jnp
        import numpy as np
        H = 512
        I = 256
        E = 16
        TOPK = 4
        SI = 256
        key = jax.random.key(seed)
        ks = jax.random.split(key, 9)
        s = 0.02
        return {'hidden_states': jax.random.normal(ks[0], (2, 256, H), dtype=jnp.float32), 'gate_w': jax.random.normal(ks[1], (E, H), dtype=jnp.float32) * s, 'bias': jnp.zeros((E,), dtype=jnp.float32), 'Wg': jax.random.normal(ks[2], (E, I, H), dtype=jnp.float32) * s, 'Wu': jax.random.normal(ks[3], (E, I, H), dtype=jnp.float32) * s, 'Wd': jax.random.normal(ks[4], (E, H, I), dtype=jnp.float32) * s, 'Sg': jax.random.normal(ks[5], (SI, H), dtype=jnp.float32) * s, 'Su': jax.random.normal(ks[6], (SI, H), dtype=jnp.float32) * s, 'Sd': jax.random.normal(ks[7], (H, SI), dtype=jnp.float32) * s}
    _L0_ffn_all = _L0_ffn_setup()
    _L0_ffn_in = {k: v for k, v in _L0_ffn_all.items() if k in ('gate_w', 'bias', 'Wg', 'Wu', 'Wd', 'Sg', 'Su', 'Sd')}
    del _L0_ffn_all
    return {'x': x, 'ctx_4096': ctx_4096, 'mask_BxSxS2_ff1': mask_BxSxS2_ff1, 'L0_attn_Wq': _L0_attn_in['Wq'], 'L0_attn_bq': _L0_attn_in['bq'], 'L0_attn_Wk': _L0_attn_in['Wk'], 'L0_attn_bk': _L0_attn_in['bk'], 'L0_attn_Wv': _L0_attn_in['Wv'], 'L0_attn_bv': _L0_attn_in['bv'], 'L0_attn_Wo': _L0_attn_in['Wo'], 'L0_attn_bo': _L0_attn_in['bo'], 'L0_xattn_wq': _L0_xattn_in['wq'], 'L0_xattn_wk': _L0_xattn_in['wk'], 'L0_xattn_wv': _L0_xattn_in['wv'], 'L0_xattn_wo': _L0_xattn_in['wo'], 'L0_ffn_gate_w': _L0_ffn_in['gate_w'], 'L0_ffn_bias': _L0_ffn_in['bias'], 'L0_ffn_Wg': _L0_ffn_in['Wg'], 'L0_ffn_Wu': _L0_ffn_in['Wu'], 'L0_ffn_Wd': _L0_ffn_in['Wd'], 'L0_ffn_Sg': _L0_ffn_in['Sg'], 'L0_ffn_Su': _L0_ffn_in['Su'], 'L0_ffn_Sd': _L0_ffn_in['Sd']}

def reference(x, ctx_4096, mask_BxSxS2_ff1, L0_attn_Wq, L0_attn_bq, L0_attn_Wk, L0_attn_bk, L0_attn_Wv, L0_attn_bv, L0_attn_Wo, L0_attn_bo, L0_xattn_wq, L0_xattn_wk, L0_xattn_wv, L0_xattn_wo, L0_ffn_gate_w, L0_ffn_bias, L0_ffn_Wg, L0_ffn_Wu, L0_ffn_Wd, L0_ffn_Sg, L0_ffn_Su, L0_ffn_Sd):
    import jax
    import jax.numpy as jnp

    def _L0_attn_ref(x, Wq, bq, Wk, bk, Wv, bv, Wo, bo):
        import jax, jax.numpy as jnp
        import numpy as np
        import math
        B, L, D, H = (32, 64, 512, 32)
        HD = D // H
        b, l, d = x.shape
        h, hd = (H, HD)
        q = (x @ Wq.T + bq).reshape(b, l, h, hd).transpose(0, 2, 1, 3)
        k = (x @ Wk.T + bk).reshape(b, l, h, hd).transpose(0, 2, 1, 3)
        v = (x @ Wv.T + bv).reshape(b, l, h, hd).transpose(0, 2, 1, 3)
        scores = jnp.einsum('bhqd,bhkd->bhqk', q, k) / math.sqrt(hd)
        causal = jnp.tril(jnp.ones((l, l), bool))
        scores = jnp.where(causal, scores, -jnp.inf)
        att = jax.nn.softmax(scores, axis=-1)
        out = jnp.einsum('bhqk,bhkd->bhqd', att, v)
        out = out.transpose(0, 2, 1, 3).reshape(b, l, d)
        return out @ Wo.T + bo

    def _L0_xattn_ref(query, key, value, mask, wq, wk, wv, wo):
        import jax, jax.numpy as jnp
        import numpy as np
        N_Q_HEADS = 32
        N_KV_HEADS = 8
        D_MODEL = 512
        D_K = 128
        D_V = 128
        ROPE_BASE = 10000.0

        def _rope(x):
            d = x.shape[-1]
            s = x.shape[2]
            inv_freq = 1.0 / ROPE_BASE ** (jnp.arange(0, d, 2, dtype=jnp.float32) / d)
            ang = jnp.arange(s, dtype=jnp.float32)[:, None] * inv_freq[None, :]
            cos = jnp.concatenate([jnp.cos(ang), jnp.cos(ang)], axis=-1)[None, None]
            sin = jnp.concatenate([jnp.sin(ang), jnp.sin(ang)], axis=-1)[None, None]
            x1, x2 = (x[..., :d // 2], x[..., d // 2:])
            rot = jnp.concatenate([-x2, x1], axis=-1)
            return x * cos + rot * sin
        bs, s, _ = query.shape
        g = N_Q_HEADS // N_KV_HEADS
        q = (query @ wq).reshape(bs, s, N_Q_HEADS, D_K).transpose(0, 2, 1, 3)
        k = (key @ wk).reshape(bs, s, N_KV_HEADS, D_K).transpose(0, 2, 1, 3)
        v = (value @ wv).reshape(bs, s, N_KV_HEADS, D_V).transpose(0, 2, 1, 3)
        q = _rope(q)
        k = _rope(k)
        scale = jnp.sqrt(jnp.float32(D_K))
        qg = q.reshape(bs, N_KV_HEADS, g, s, D_K)
        scores = jnp.einsum('bhgqd,bhkd->bhgqk', qg, k) / scale
        masked = jnp.where(mask[:, None, None].astype(bool), scores, -1000000000.0)
        w = jax.nn.softmax(masked, axis=-1)
        out = jnp.einsum('bhgqk,bhkd->bhgqd', w, v)
        out = out.reshape(bs, N_Q_HEADS, s, D_V).transpose(0, 2, 1, 3).reshape(bs, s, N_Q_HEADS * D_V)
        return out @ wo

    def _L0_ffn_ref(hidden_states, gate_w, bias, Wg, Wu, Wd, Sg, Su, Sd):
        import jax, jax.numpy as jnp
        import numpy as np
        H = 512
        I = 256
        E = 16
        TOPK = 4
        SI = 256
        orig_shape = hidden_states.shape
        x = hidden_states.reshape(-1, orig_shape[-1])
        scores = jax.nn.sigmoid(x @ gate_w.T) + bias
        topk_w, topk_idx = jax.lax.top_k(scores, TOPK)
        topk_w = topk_w / (jnp.sum(topk_w, axis=-1, keepdims=True) + 1e-20)
        cw = jnp.sum(jax.nn.one_hot(topk_idx, E, dtype=x.dtype) * topk_w[..., None], axis=1)
        g = jnp.einsum('th,eih->eti', x, Wg)
        u = jnp.einsum('th,eih->eti', x, Wu)
        z = jax.nn.silu(g) * u
        zw = z * cw.T[:, :, None]
        out = jnp.einsum('eti,ehi->th', zw, Wd)
        out = out + jax.nn.silu(x @ Sg.T) * (x @ Su.T) @ Sd.T
        return out.reshape(orig_shape)
    x = _layernorm(x + _L0_attn_ref(x, L0_attn_Wq, L0_attn_bq, L0_attn_Wk, L0_attn_bk, L0_attn_Wv, L0_attn_bv, L0_attn_Wo, L0_attn_bo), axis=-1)
    x = _layernorm(x + _L0_xattn_ref(x, ctx_4096, ctx_4096, mask_BxSxS2_ff1, L0_xattn_wq, L0_xattn_wk, L0_xattn_wv, L0_xattn_wo), axis=-1)
    x = _layernorm(x + _L0_ffn_ref(x, L0_ffn_gate_w, L0_ffn_bias, L0_ffn_Wg, L0_ffn_Wu, L0_ffn_Wd, L0_ffn_Sg, L0_ffn_Su, L0_ffn_Sd), axis=-1)
    return x

_drawn_inputs = setup_inputs


def setup_inputs(seed=0):
    import zlib

    import numpy as np

    out = dict(_drawn_inputs(seed))
    spreads = {'L0_ffn_bias': (0.0, 0.531)}
    factors = {'L0_attn_bq': 5.375,
     'L0_attn_bk': 8.0,
     'L0_xattn_wq': 2.867,
     'L0_xattn_wk': 2.872,
     'L0_ffn_gate_w': 4.333,
     'L0_ffn_Wg': 3.305,
     'L0_ffn_Wu': 3.248,
     'L0_ffn_Wd': 3.241}
    for name, (base, spread) in spreads.items():
        noise = np.random.default_rng([zlib.crc32(name.encode()), seed]).standard_normal(out[name].shape)
        drawn = base * np.exp(spread * noise) if base else spread * noise
        out[name] = jnp.asarray(drawn.astype(out[name].dtype))
    for name, factor in factors.items():
        out[name] = (out[name] * factor).astype(out[name].dtype)
    return out
```

```python
import concourse.bass as bass
from concourse import mybir
from contextlib import ExitStack

F32, F16, U32 = mybir.dt.float32, mybir.dt.float16, mybir.dt.uint32
ALU, ACT, AX = mybir.AluOpType, mybir.ActivationFunctionType, mybir.AxisListType

B, S, D = 32, 64, 512
T = B * S
P = 128
NT = T // P
TQ = 4
NQ = NT // TQ
QT = TQ * P
KD = D // P
H1, HD1 = 32, 16
HG = P // HD1
H2, HKV, HD2 = 32, 8, 128
GQ = H2 // HKV
NE, TOPK, FI = 16, 4, 256
IB = FI // P
EPS = 1e-5
WS = 64.0
OS = 16.0
BIG = 3.0e38


class Timeline:

    def __init__(self, sem, body, rounds, post=()):
        self.sem, self.body, self.rounds, self.post = sem, list(body), rounds, list(post)
        self.index = {k: n for n, k in enumerate(self.body)}
        self.post_index = {k: n for n, k in enumerate(self.post)}
        assert len(self.index) == len(self.body)
        self.cursor = 0

    def start(self, eng):
        eng.sem_inc(self.sem, len(self.body))

    def mark(self, instruction, name, step):
        order = self.post if step.i is None else self.body
        key = name if step.i is None else (step.q, name)
        assert order[self.cursor] == key, (order[self.cursor], key)
        self.cursor = (self.cursor + 1) % len(order)
        instruction.then_inc(self.sem, 1)

    def value(self, name, step, back=0):
        n = len(self.body)
        if step.i is None:
            if back == 0:
                return (self.rounds + 1) * n + self.post_index[name] + 1
            return self.rounds * n + self.index[(NQ - back, name)] + 1
        q = step.q - back
        if q >= 0:
            return step.i * n + n + self.index[(q, name)] + 1
        return step.i * n + self.index[(q + NQ, name)] + 1


class Step:

    def __init__(self, i, q):
        self.i, self.q = i, q


def events(per_step, extra=()):
    out = []
    for q in range(NQ):
        for name in per_step:
            out.append((q, name))
            for qq, after, names in extra:
                if qq == q and after == name:
                    out += [(q, x) for x in names]
    return out


def build(nc, x, xT, cT, maskf, wqT, bq, wkT, bk, wvT, bv, woT, bo, xwq, xwk, xwv, xwo,
          gwT, gbias, egu, ed, causal, cosT, sinT, parity, eye, iota, out):
    top = ExitStack()
    with top:
        def sb(name, shape, dt=F32, where=top):
            return where.enter_context(nc.sbuf_tensor(name, shape, dt))

        def sem(name):
            return top.enter_context(nc.semaphore(name))

        bank = [top.enter_context(nc.psum_tensor(f"bank{n}", [P, 512], F32)) for n in range(8)]

        acc = sb("acc", [P, NT, D])
        xh = sb("xh", [P, KD, T], F16)
        xl = sb("xl", [P, KD, T], F16)
        ident = sb("ident", [P, P])
        mv = sb("mv", [P, NT, 2])
        rstd = sb("rstd", [P, NT, 1])
        eps = sb("eps", [P, 1])

        s_met = sem("waits_met")

        def met(eng):
            eng.sem_inc(s_met, 1)

        def load_split(tag, src, hi, lo, first=None):
            with ExitStack() as ctx:
                raw = [sb(f"{tag}_raw{j}", [P, KD, QT], where=ctx) for j in range(2)]
                s_raw = [sem(f"{tag}_s_raw{j}") for j in range(2)]
                s_hi, s_lo = sem(f"{tag}_s_hi"), sem(f"{tag}_s_lo")
                view = src.rearrange("(k p) t -> p k t", p=P)
                block = ctx.enter_context(nc.Block())

                @block.sync
                def _(sp):
                    for n in range(NQ):
                        if n >= 2:
                            sp.wait_ge(s_lo, n - 1)
                        sp.dma_start(raw[n % 2][:, :, :], view[:, :, n * QT:(n + 1) * QT]).then_inc(s_raw[n % 2], 16)

                @block.scalar
                def _(act):
                    for n in range(NQ):
                        act.wait_ge(s_raw[n % 2], 16 * (n // 2 + 1))
                        act.activation(hi[:, :, n * QT:(n + 1) * QT], raw[n % 2][:, :, :], ACT.Copy).then_inc(s_hi, 1)

                @block.vector
                def _(dve):
                    for n in range(NQ):
                        dve.wait_ge(s_hi, n + 1)
                        dve.tensor_tensor(lo[:, :, n * QT:(n + 1) * QT], raw[n % 2][:, :, :],
                                          hi[:, :, n * QT:(n + 1) * QT], ALU.subtract).then_inc(s_lo, 1)

                @block.gpsimd
                def _(pool):
                    if first:
                        first(pool)

        def load_constants(pool):
            s_c, s_o = sem("s_const"), sem("s_const_bo")
            pool.memset(eps[:, :], EPS).then_inc(s_o, 1)
            pool.dma_start(ident[:, :], eye).then_inc(s_c, 16)
            pool.dma_start(acc[:, :, :], x.rearrange("(t p) d -> p t d", p=P)).then_inc(s_c, 16)
            pool.wait_ge(s_c, 32)
            with nc.sbuf_tensor("bo_rows", [P, D], F32) as bo_rows:
                pool.dma_start(bo_rows[:, :], bo.rearrange("(a n) -> a n", a=1).to_broadcast([P, D]))\
                    .then_inc(s_c, 16)
                pool.wait_ge(s_c, 48)
                pool.tensor_tensor(acc[:, :, :], acc[:, :, :],
                                   bo_rows[:, :].rearrange("p (a n) -> p a n", a=1).to_broadcast([P, NT, D]),
                                   ALU.add).then_inc(s_o, 1)
                pool.wait_ge(s_o, 2)

        def layernorm(tag, last):
            with ExitStack() as ctx:
                st = sb(f"{tag}_st", [P, 2, 6], where=ctx)
                s_st, s_ag, s_sq, s_rs = sem(f"{tag}_st"), sem(f"{tag}_ag"), sem(f"{tag}_sq"), sem(f"{tag}_rs")
                block = ctx.enter_context(nc.Block())

                @block.vector
                def _(dve):
                    for t in range(NT):
                        if t >= 2:
                            dve.wait_ge(s_ag, t - 1)
                        dve.bn_stats(st[:, t % 2, :], acc[:, t, :]).then_inc(s_st, 1)
                        dve.wait_ge(s_st, t + 1)
                        dve.bn_aggr(mv[:, t, :], st[:, t % 2, :]).then_inc(s_ag, 1)
                    dve.wait_ge(s_sq, 1)
                    dve.reciprocal(rstd[:, :, :], rstd[:, :, :]).then_inc(s_rs, 1)
                    dve.wait_ge(s_rs, 1)

                @block.scalar
                def _(act):
                    act.wait_ge(s_ag, NT)
                    act.activation(rstd[:, :, :], mv[:, :, 1:2], ACT.Sqrt, bias=eps[:, :]).then_inc(s_sq, 1)

            with ExitStack() as ctx:
                xn = [sb(f"{tag}_xn{j}", [P, D], where=ctx) for j in range(TQ)]
                s_out = [sem(f"{tag}_s_out{j}") for j in range(TQ)] if last else None
                dve_t = Timeline(sem(f"{tag}_dve"), [(0, f"{w}{j}") for j in range(TQ) for w in
                                                     (("norm",) if last else ("norm", "lo"))], NQ)
                act_t = Timeline(sem(f"{tag}_act"), [(0, f"hi{j}") for j in range(TQ)], NQ)
                pe_t = Timeline(sem(f"{tag}_pe"), [(0, f"turn{j}") for j in range(TQ)], NQ)
                pool_t = Timeline(sem(f"{tag}_pool"), [(0, f"back{j}") for j in range(TQ)], NQ)

                class Round(Step):
                    pass

                def before(tl, name, r):
                    return r.i * len(tl.body) + tl.index[(0, name)] + 1

                block = ctx.enter_context(nc.Block())

                @block.vector
                def _(dve):
                    dve_t.start(dve)
                    with dve.Fori(0, NQ) as i:
                        r = Round(i, 0)
                        for j in range(TQ):
                            if last:
                                dve.wait_ge(s_out[j], i * 16 + 16)
                            else:
                                dve.wait_ge(pool_t.sem, before(pool_t, f"back{j}", r))
                                dve.wait_ge(pe_t.sem, before(pe_t, f"turn{j}", r))
                            dve_t.mark(dve.tensor_scalar(xn[j][:, :], acc[:, i * TQ + j, :], mv[:, i * TQ + j, 0:1],
                                                         rstd[:, i * TQ + j, 0:1], ALU.subtract, ALU.mult),
                                       f"norm{j}", r)
                            if not last:
                                dve.wait_ge(act_t.sem, act_t.value(f"hi{j}", r))
                                tok = bass.ds(i * QT + j * P, P)
                                dve_t.mark(dve.tensor_tensor(xl[:, :, tok], bank[j][:, :].rearrange("p (k t) -> p k t", k=KD),
                                                             xh[:, :, tok], ALU.subtract), f"lo{j}", r)

                if last:
                    @block.sync
                    def _(sp):
                        for j in range(TQ):
                            sp.sem_inc(s_out[j], 16)
                        with sp.Fori(0, NQ) as i:
                            r = Round(i, 0)
                            for j in range(TQ):
                                sp.wait_ge(dve_t.sem, dve_t.value(f"norm{j}", r))
                                met(sp)
                                sp.dma_start(out[bass.ds(i * QT + j * P, P), :], xn[j][:, :]).then_inc(s_out[j], 16)
                        for j in range(TQ):
                            sp.wait_ge(s_out[j], 16 * (NQ + 1))
                else:
                    @block.tensor
                    def _(pe):
                        pe_t.start(pe)
                        with pe.Fori(0, NQ) as i:
                            r = Round(i, 0)
                            for j in range(TQ):
                                pe.wait_ge(dve_t.sem, dve_t.value(f"norm{j}", r))
                                pe.wait_ge(dve_t.sem, before(dve_t, f"lo{j}", r))
                                for k in range(KD):
                                    mm = pe.transpose(bank[j][:, k * P:(k + 1) * P], xn[j][:, k * P:(k + 1) * P], ident[:, :])
                                pe_t.mark(mm, f"turn{j}", r)

                    @block.scalar
                    def _(act):
                        act_t.start(act)
                        with act.Fori(0, NQ) as i:
                            r = Round(i, 0)
                            for j in range(TQ):
                                act.wait_ge(pe_t.sem, pe_t.value(f"turn{j}", r))
                                act_t.mark(act.activation(xh[:, :, bass.ds(i * QT + j * P, P)],
                                                          bank[j][:, :].rearrange("p (k t) -> p k t", k=KD), ACT.Copy),
                                           f"hi{j}", r)

                    @block.gpsimd
                    def _(pool):
                        pool_t.start(pool)
                        with pool.Fori(0, NQ) as i:
                            r = Round(i, 0)
                            for j in range(TQ):
                                pool.wait_ge(dve_t.sem, dve_t.value(f"norm{j}", r))
                                met(pool)
                                pool_t.mark(pool.tensor_copy(acc[:, i * TQ + j, :], xn[j][:, :]), f"back{j}", r)

        def three_pass(pe, out_ap, pairs, start=True, stop=True):
            n = len(pairs)
            for m, (ah, al, bh, bl) in enumerate(pairs):
                pe.matmul(out_ap, ah, bh, start=start and m == 0, stop=False)
                pe.matmul(out_ap, ah, bl, start=False, stop=False)
                mm = pe.matmul(out_ap, al, bh, start=False, stop=stop and m == n - 1)
            return mm

        def self_attention():
            NG = H1 // HG
            with ExitStack() as ctx:
                def b(name, shape, dt=F32):
                    return sb("sa_" + name, shape, dt, ctx)
                raw_f, wf_h, wf_l = b("raw_f", [P, KD, 3 * P]), b("wf_h", [P, KD, 3 * P], F16), b("wf_l", [P, KD, 3 * P], F16)
                raw_o, wo_h, wo_l = b("raw_o", [P, D]), b("wo_h", [P, D], F16), b("wo_l", [P, D], F16)
                rawb, bias_c, bv_row = b("rawb", [P, 2 + P]), b("bias_c", [P, 3]), b("bv_row", [P, P])
                par = b("par", [P, 2])
                parw = b("parw", [P, 2])
                caus = b("caus", [P, S])
                qT, kx = b("qT", [P, QT]), b("kx", [P, 2, QT])
                sc = b("sc", [P, 4, TQ, 2, S])
                mx, sm, rs = b("mx", [P, 4, 8]), b("sm", [P, 4, 8]), b("rs", [P, 4, TQ, 2])
                v, vs = b("v", [P, TQ, P]), b("vs", [P, TQ, P])
                pt = b("pt", [P, 4, TQ, P])
                at = b("at", [P, TQ, P])
                oh, ol = b("oh", [P, QT], F16), b("ol", [P, QT], F16)
                s_rf, s_ro, s_cn = sem("sa_s_rf"), sem("sa_s_ro"), sem("sa_s_cn")

                SB = [bank[2], bank[3]]
                PTB = [bank[4], bank[5]]
                PVB = [bank[6], bank[7]]
                uses = ["k", "q", "oT", "v", "w0", "w1", "w2", "w3"]
                PE = Timeline(sem("sa_pe"), events(["k", "q", "pt0", "pt1", "pt2", "pt3", "pv0", "pv1", "s0", "s1", "s2",
                                                    "s3", "oT", "v", "w0", "w1", "w2", "w3"]), NG,
                              ["pt0", "pt1", "pt2", "pt3", "pv0", "pv1", "oT", "w0", "w1", "w2", "w3"])
                AC = Timeline(sem("sa_act"), events(["ke", "ko", "qe", "pe0", "pe1", "pe2", "pe3", "oh", "ex0", "ex1", "ex2",
                                                     "ex3"], [(3, "oh", ["wfh"]), (0, "ex3", ["woh"])]), NG,
                              ["pe0", "pe1", "pe2", "pe3", "oh"])
                DV = Timeline(sem("sa_dve"), events(["no0", "no1", "mn0", "mx0", "sb0", "mn1", "mx1", "sb1", "mn2", "mx2", "sb2",
                                                     "mn3", "ol", "v", "vs", "mx3", "sb3", "w0", "w1", "w2", "w3", "sum", "rc"],
                                                    [(3, "vs", ["wfl", "bc0", "bc1"]), (0, "w3", ["wol"])]), NG,
                              ["no0", "no1", "ol", "w0", "w1", "w2", "w3"])
                freed = {"k": (AC, "ko"), "q": (AC, "qe"), "oT": (DV, "ol"), "v": (DV, "v"),
                         "w0": (DV, "w0"), "w1": (DV, "w1"), "w2": (DV, "w2"), "w3": (DV, "w3")}
                s_pre_a, s_pre_v, s_zero = sem("sa_pre_a"), sem("sa_pre_v"), sem("sa_zero")
                block = ctx.enter_context(nc.Block())

                def gbank(pe, name, st):
                    n = uses.index(name)
                    prev, back = (uses[n - 2], 0) if n >= 2 else (uses[n - 2], 1)
                    tl, ev = freed[prev]
                    if st.i is None and prev in ("q", "v"):
                        ev2 = tl.value(ev, st, 1)
                    elif st.i is None and prev == "k":
                        ev2 = tl.value(ev, st, 1)
                    else:
                        ev2 = tl.value(ev, st, back)
                    pe.wait_ge(tl.sem, ev2)
                    return bank[n % 2]

                @block.sync
                def _(sp):
                    def front_weights(g):
                        for n, w in enumerate((wqT, wkT, wvT)):
                            sp.dma_start(raw_f[:, :, n * P:(n + 1) * P],
                                         w.rearrange("(k p) n -> p k n", p=P)[:, :, bass.ds(g * P, P)]).then_inc(s_rf, 16)
                        for n, w in enumerate((bq, bk)):
                            sp.dma_start(rawb[:, n:n + 1], w.rearrange("(p a) -> p a", a=1)[bass.ds(g * P, P), :]).then_inc(s_rf, 16)
                        sp.dma_start(rawb[:, 2:2 + P],
                                     bv.rearrange("(a n) -> a n", a=1)[:, bass.ds(g * P, P)].to_broadcast([P, P])).then_inc(s_rf, 16)
                    sp.dma_start(caus[:, :], causal).then_inc(s_cn, 16)
                    sp.dma_start(par[:, :], parity).then_inc(s_cn, 16)
                    front_weights(0)
                    sp.dma_start(raw_o[:, :], woT[0:P, :]).then_inc(s_ro, 16)
                    sp.wait_ge(s_pre_v, 3)
                    with sp.Fori(0, NG) as i:
                        nxt = (i + 1) % NG
                        front_weights(nxt)
                        sp.wait_ge(DV.sem, DV.value("wol", Step(i, 0)))
                        met(sp)
                        sp.dma_start(raw_o[:, :], woT[bass.ds(nxt * P, P), :]).then_inc(s_ro, 16)
                        sp.wait_ge(DV.sem, DV.value("bc1", Step(i, 3)))
                        met(sp)
                    sp.wait_ge(s_ro, 16 * (NG + 1))

                def split_front_hi(act):
                    return act.activation(wf_h[:, :, :], raw_f[:, :, :], ACT.Copy, scale=WS)

                def split_front_lo(dve):
                    return dve.scalar_tensor_tensor(wf_l[:, :, :].rearrange("p a b -> p (a b)"),
                                                    raw_f[:, :, :].rearrange("p a b -> p (a b)"), WS,
                                                    wf_h[:, :, :].rearrange("p a b -> p (a b)"), ALU.mult, ALU.subtract)

                @block.gpsimd
                def _(pool):
                    for z in (sc, v, vs, wo_h, wo_l, rs):
                        pool.memset(z[:], 0.0)
                    pool.memset(qT[0:1, 0:1], 0.0).then_inc(s_zero, 1)

                @block.scalar
                def _(act):
                    act.wait_ge(s_rf, 96)
                    split_front_hi(act).then_inc(s_pre_a, 1)
                    AC.start(act)
                    act.wait_ge(s_pre_v, 3)

                    def back(st):
                        for j in range(4):
                            act.wait_ge(PE.sem, PE.value(f"pt{j}", st))
                            act.wait_ge(PE.sem, PE.value("pv1", st, 1))
                            AC.mark(act.activation(pt[:, j, :, :].rearrange("p a b -> p (a b)"), PTB[j % 2][:, :], ACT.Copy),
                                    f"pe{j}", st)
                        act.wait_ge(PE.sem, PE.value("oT", st))
                        act.wait_ge(PE.sem, PE.value("w3", st, 1))
                        AC.mark(act.activation(oh[:, :], bank[0][:, :], ACT.Copy), "oh", st)

                    with act.Fori(0, NG) as i:
                        for q in range(NQ):
                            st = Step(i, q)
                            act.wait_ge(PE.sem, PE.value("k", st))
                            act.wait_ge(PE.sem, PE.value("s3", st, 1))
                            if q == 0:
                                act.wait_ge(DV.sem, DV.value("bc1", st, 1))
                            for e in range(2):
                                AC.mark(act.activation(kx[:, e, :], bank[0][:, :], ACT.Identity, bias=bias_c[:, 1 + e:2 + e],
                                                       scale=parw[:, e:e + 1]), ("ke", "ko")[e], st)
                            act.wait_ge(PE.sem, PE.value("q", st))
                            AC.mark(act.activation(qT[:, :], bank[1][:, :], ACT.Identity, bias=bias_c[:, 0:1], scale=1 / WS), "qe", st)
                            back(st)
                            if q == 3:
                                act.wait_ge(s_rf, i * 96 + 192)
                                act.wait_ge(PE.sem, PE.value("v", st))
                                AC.mark(split_front_hi(act), "wfh", st)
                            for j in range(4):
                                act.wait_ge(DV.sem, DV.value(f"sb{j}", st))
                                s2 = sc[:, j, :, :, :].rearrange("p a b c -> p (a b c)")
                                AC.mark(act.activation(s2, s2, ACT.Exp, scale=float(HD1) ** -0.5), f"ex{j}", st)
                            if q == 0:
                                act.wait_ge(s_ro, i * 16 + 16)
                                act.wait_ge(PE.sem, PE.value("w3", st))
                                AC.mark(act.activation(wo_h[:, :], raw_o[:, :], ACT.Copy, scale=WS), "woh", st)
                    back(Step(None, 0))

                @block.vector
                def _(dve):
                    dve.wait_ge(s_cn, 32)
                    dve.tensor_scalar(parw[:, :], par[:, :], 1 / WS, None, ALU.mult)
                    dve.wait_ge(s_pre_a, 1)
                    split_front_lo(dve).then_inc(s_pre_v, 1)

                    def biases(done0, done1):
                        done0(dve.tensor_scalar(bias_c[:, 1:3], par[:, 0:2], rawb[:, 1:2], None, ALU.mult))
                        dve.tensor_copy(bv_row[:, :], rawb[:, 2:2 + P])
                        done1(dve.tensor_copy(bias_c[:, 0:1], rawb[:, 0:1]))
                    dve.wait_ge(s_rf, 96)
                    biases(lambda m: m.then_inc(s_pre_v, 1), lambda m: m.then_inc(s_pre_v, 1))
                    dve.wait_ge(s_pre_v, 3)
                    DV.start(dve)

                    def back_norm(st):
                        for e in range(2):
                            dve.wait_ge(PE.sem, PE.value(f"pv{e}", st))
                            if e == 0:
                                dve.wait_ge(DV.sem, DV.value("rc", st, 1))
                                dve.wait_ge(PE.sem, PE.value("oT", st, 1))
                            DV.mark(dve.tensor_tensor(at[:, :, :].rearrange("p t (j e d) -> p t j e d", j=4, e=2)[:, :, :, e, :],
                                                      PVB[e][:, 0:256].rearrange("p (t j d) -> p t j d", t=TQ, j=4),
                                                      rs[:, :, :, e:e + 1].rearrange("p j t a -> p t j a")
                                                      .to_broadcast([P, TQ, 4, HD1]), ALU.mult), f"no{e}", st)

                    def back_lo(st):
                        dve.wait_ge(AC.sem, AC.value("oh", st))
                        DV.mark(dve.tensor_tensor(ol[:, :], bank[0][:, :], oh[:, :], ALU.subtract), "ol", st)

                    def back_add(st):
                        for t in range(TQ):
                            dve.wait_ge(PE.sem, PE.value(f"w{t}", st))
                            row = acc[:, t + TQ * ((st.q - 1) % NQ if st.i is not None else NQ - 1), :]
                            DV.mark(dve.scalar_tensor_tensor(row, bank[t % 2][:, :], 1 / WS, row, ALU.mult, ALU.add), f"w{t}", st)

                    def smax(st, j, part):
                        s3 = sc[:, j, :, :, :].rearrange("p a b c -> p (a b) c")
                        if part == "mn":
                            dve.wait_ge(PE.sem, PE.value(f"s{j}", st))
                            DV.mark(dve.tensor_tensor(s3, SB[j % 2][:, :].rearrange("p (a c) -> p a c", a=8),
                                                      caus[:, :].rearrange("p (a c) -> p a c", a=1).to_broadcast([P, 8, S]),
                                                      ALU.min), f"mn{j}", st)
                        elif part == "mx":
                            dve.wait_ge(DV.sem, DV.value(f"mn{j}", st))
                            DV.mark(dve.tensor_reduce(mx[:, j, :], s3, AX.X, ALU.max), f"mx{j}", st)
                        else:
                            dve.wait_ge(DV.sem, DV.value(f"mx{j}", st))
                            DV.mark(dve.tensor_tensor(s3, s3, mx[:, j, :].rearrange("p (a c) -> p a c", c=1)
                                                      .to_broadcast([P, 8, S]), ALU.subtract), f"sb{j}", st)

                    with dve.Fori(0, NG) as i:
                        for q in range(NQ):
                            st = Step(i, q)
                            back_norm(st)
                            for j in range(3):
                                for part in ("mn", "mx", "sb"):
                                    smax(st, j, part)
                            smax(st, 3, "mn")
                            back_lo(st)
                            dve.wait_ge(PE.sem, PE.value("v", st))
                            DV.mark(dve.scalar_tensor_tensor(v[:, :, :], bank[1][:, :].rearrange("p (t n) -> p t n", t=TQ), 1 / WS,
                                                             bv_row[:, :].rearrange("p (a n) -> p a n", a=1).to_broadcast([P, TQ, P]),
                                                             ALU.mult, ALU.add), "v", st)
                            dve.wait_ge(DV.sem, DV.value("v", st))
                            dve.tensor_copy(vs[0:64, :, :], v[64:128, :, :])
                            DV.mark(dve.tensor_copy(vs[64:128, :, :], v[0:64, :, :]), "vs", st)
                            if q == 3:
                                dve.wait_ge(AC.sem, AC.value("wfh", st))
                                DV.mark(split_front_lo(dve), "wfl", st)
                                dve.wait_ge(s_rf, i * 96 + 192)
                                biases(lambda m: DV.mark(m, "bc0", st), lambda m: DV.mark(m, "bc1", st))
                            smax(st, 3, "mx")
                            smax(st, 3, "sb")
                            back_add(st)
                            if q == 0:
                                dve.wait_ge(AC.sem, AC.value("woh", st))
                                DV.mark(dve.scalar_tensor_tensor(wo_l[:, :], raw_o[:, :], WS, wo_h[:, :], ALU.mult, ALU.subtract),
                                        "wol", st)
                            dve.wait_ge(AC.sem, AC.value("ex3", st))
                            DV.mark(dve.tensor_reduce(sm[:, :, :], sc[:, :, :, :, :].rearrange("p j a b c -> p j (a b) c"), AX.X,
                                                      ALU.add), "sum", st)
                            dve.wait_ge(DV.sem, DV.value("sum", st))
                            DV.mark(dve.reciprocal(rs[:, :, :, :].rearrange("p j t e -> p j (t e)"), sm[:, :, :]), "rc", st)
                    st = Step(None, 0)
                    back_norm(st)
                    back_lo(st)
                    back_add(st)

                @block.tensor
                def _(pe):
                    PE.start(pe)
                    pe.wait_ge(s_zero, 1)
                    pe.wait_ge(s_pre_v, 3)

                    def feature_major(name, st, col):
                        o = gbank(pe, name, st)
                        tok = slice(st.q * QT, (st.q + 1) * QT)
                        PE.mark(three_pass(pe, o[:, :], [(wf_h[:, k, col:col + P], wf_l[:, k, col:col + P], xh[:, k, tok],
                                                          xl[:, k, tok]) for k in range(KD)]), name, st)

                    def back_pv(st):
                        for j in range(4):
                            if j == 0:
                                pe.wait_ge(AC.sem, AC.value("ex3", st, 1))
                            if j < 2:
                                pe.wait_ge(AC.sem, AC.value(f"pe{j + 2}", st, 1))
                            else:
                                pe.wait_ge(AC.sem, AC.value(f"pe{j - 2}", st))
                            for t in range(TQ):
                                mm = pe.transpose(PTB[j % 2][:, t * P:(t + 1) * P],
                                                  sc[:, j, t, :, :].rearrange("p e k -> p (e k)"), ident[:, :])
                            PE.mark(mm, f"pt{j}", st)
                        pe.wait_ge(AC.sem, AC.value("pe3", st))
                        pe.wait_ge(DV.sem, DV.value("vs", st, 1))
                        for e in range(2):
                            pe.wait_ge(DV.sem, DV.value(f"no{e}", st, 1))
                            met(pe)
                            rows = slice(64 * e, 64 * e + 64)
                            for t in range(TQ):
                                for b2 in range(2):
                                    val = v if b2 == e else vs
                                    for j in range(4):
                                        c = (2 * j + e) * HD1
                                        mm = pe.matmul(PVB[e][64 * b2:64 * b2 + 64, (4 * t + j) * HD1:(4 * t + j + 1) * HD1],
                                                       pt[rows, j, t, 64 * b2:64 * b2 + 64], val[rows, t, c:c + HD1],
                                                       start=True, stop=True)
                            PE.mark(mm, f"pv{e}", st)

                    def back_turn(st):
                        o = gbank(pe, "oT", st)
                        pe.wait_ge(DV.sem, DV.value("no1", st))
                        for t in range(TQ):
                            mm = pe.transpose(o[:, t * P:(t + 1) * P], at[:, t, :], ident[:, :])
                        PE.mark(mm, "oT", st)

                    def back_out(st):
                        pe.wait_ge(DV.sem, DV.value("ol", st))
                        if st.q == 1:
                            pe.wait_ge(DV.sem, DV.value("wol", st, 1))
                        for t in range(TQ):
                            o = gbank(pe, f"w{t}", st)
                            tok = slice(t * P, (t + 1) * P)
                            PE.mark(three_pass(pe, o[:, :], [(oh[:, tok], ol[:, tok], wo_h[:, :], wo_l[:, :])]), f"w{t}", st)

                    with pe.Fori(0, NG) as i:
                        for q in range(NQ):
                            st = Step(i, q)
                            if q == 0:
                                pe.wait_ge(DV.sem, DV.value("wfl", st, 1))
                            feature_major("k", st, P)
                            feature_major("q", st, 0)
                            back_pv(st)
                            pe.wait_ge(AC.sem, AC.value("qe", st))
                            for j in range(4):
                                if j < 2:
                                    pe.wait_ge(DV.sem, DV.value(f"mn{j + 2}", st, 1))
                                else:
                                    pe.wait_ge(DV.sem, DV.value(f"mn{j - 2}", st))
                                r = slice(32 * j, 32 * j + 32)
                                for t in range(TQ):
                                    for b2 in range(2):
                                        tok = slice(t * P + b2 * 64, t * P + b2 * 64 + 64)
                                        mm = pe.matmul(SB[j % 2][64 * b2:64 * b2 + 64, t * P:(t + 1) * P], qT[r, tok],
                                                       kx[r, :, tok], start=True, stop=True)
                                PE.mark(mm, f"s{j}", st)
                            back_turn(st)
                            o = gbank(pe, "v", st)
                            for t in range(TQ):
                                tok = slice(q * QT + t * P, q * QT + (t + 1) * P)
                                mm = three_pass(pe, o[:, t * P:(t + 1) * P],
                                                [(xh[:, k, tok], xl[:, k, tok], wf_h[:, k, 2 * P:3 * P], wf_l[:, k, 2 * P:3 * P])
                                                 for k in range(KD)])
                            PE.mark(mm, "v", st)
                            back_out(st)
                    st = Step(None, 0)
                    back_pv(st)
                    back_turn(st)
                    back_out(st)

        def cross_attention():
            NG = HKV
            FW = GQ * HD2 + 2 * HD2
            with ExitStack() as ctx:
                def b(name, shape, dt=F32):
                    return sb("xa_" + name, shape, dt, ctx)
                ch, cl = b("ch", [P, KD, T], F16), b("cl", [P, KD, T], F16)
                load_split("ctx", cT, ch, cl)
                raw_f, wf_h, wf_l = b("raw_f", [P, KD, FW]), b("wf_h", [P, KD, FW], F16), b("wf_l", [P, KD, FW], F16)
                raw_o, wo_h, wo_l = b("raw_o", [P, GQ, D]), b("wo_h", [P, GQ, D], F16), b("wo_l", [P, GQ, D], F16)
                bound = b("bound", [P, B, S])
                cs, sn = b("cs", [P, S]), b("sn", [P, S])
                NR = 1 + GQ
                x0 = [b(f"x0_{r}", [P, QT]) for r in range(2)]
                xs = [b(f"xs_{r}", [P, QT]) for r in range(2)]
                rk = b("rk", [P, QT])
                rq = b("rq", [P, GQ // 2, 2 * TQ, 2, S])
                sc = b("sc", [P, 2, TQ, 2, S])
                mx, sm, rs = b("mx", [P, 2, 8]), b("sm", [P, 2, 8]), b("rs", [P, 2, 8])
                v, pt = b("v", [P, TQ, P]), b("pt", [P, 2, TQ, P])
                oh, ol = b("oh", [P, GQ, QT], F16), b("ol", [P, GQ, QT], F16)
                s_rf, s_ro, s_cn, s_bd = sem("xa_s_rf"), sem("xa_s_ro"), sem("xa_s_cn"), sem("xa_s_bd")
                SB, PTB, PVB = [bank[2], bank[3]], [bank[4], bank[5]], [bank[6], bank[7]]
                names = [f"r{r}" for r in range(NR)]
                uses = names + ["v", "w0", "w1", "w2", "w3"]
                PE = Timeline(sem("xa_pe"), events(names + ["pt0", "pt1", "pv0", "pv1", "pv2", "pv3", "s0", "s1", "v",
                                                            "w0", "w1", "w2", "w3"]), NG,
                              ["pt0", "pt1", "pv0", "pv1", "pv2", "pv3", "w0", "w1", "w2", "w3"])
                AC = Timeline(sem("xa_act"), events(names + ["pe0", "pe1", "hi0", "hi1", "hi2", "hi3", "v", "ex0", "ex1"],
                                                    [(3, "v", ["wfh"]), (0, "ex1", ["woh"])]), NG,
                              ["pe0", "pe1", "hi0", "hi1", "hi2", "hi3"])
                rope_order = []
                for r in range(NR + 1):
                    rope_order += ([f"cm{r}"] if r < NR else []) + ([f"ra{r - 1}"] if r else [])
                DV = Timeline(sem("xa_dve"), events(rope_order + ["lo0", "lo1", "lo2", "lo3", "mn0", "mx0", "sb0", "mn1", "mx1",
                                                                  "sb1", "w0", "w1", "w2", "w3", "sum", "rc"],
                                                    [(3, "sb1", ["wfl"]), (0, "w3", ["wol"])]), NG,
                              ["lo0", "lo1", "lo2", "lo3", "w0", "w1", "w2", "w3"])
                PO = Timeline(sem("xa_pool"), events([f"sm{r}" for r in range(NR)] + ["nm"]), NG)
                freed = {n: (AC, n) for n in names + ["v"]}
                freed.update({f"w{t}": (DV, f"w{t}") for t in range(TQ)})
                s_pre_a, s_pre_v, s_zero = sem("xa_pre_a"), sem("xa_pre_v"), sem("xa_zero")
                block = ctx.enter_context(nc.Block())

                def heads(o, tp, b2):
                    return o[:, :, :].rearrange("p h (t b s) -> p t b h s", t=TQ, b=2)[:, 2 * tp:2 * tp + 2, b2, :, :]

                def gbank(pe, name, st):
                    n = uses.index(name)
                    prev = uses[n - 2]
                    tl, ev = freed[prev]
                    back = 1 if n < 2 or (st.i is None and not prev.startswith("w")) else 0
                    pe.wait_ge(tl.sem, tl.value(ev, st, back))
                    return bank[n % 2]

                @block.sync
                def _(sp):
                    def front_weights(g):
                        c = 0
                        for w, n in ((xwq, GQ * HD2), (xwk, HD2), (xwv, HD2)):
                            sp.dma_start(raw_f[:, :, c:c + n],
                                         w.rearrange("(k p) n -> p k n", p=P)[:, :, bass.ds(g * n, n)]).then_inc(s_rf, 16)
                            c += n

                    def out_weights(g):
                        sp.dma_start(raw_o[:, :, :], xwo[bass.ds(g * GQ * HD2, GQ * HD2), :]
                                     .rearrange("(h p) n -> p h n", p=P)).then_inc(s_ro, 16)
                    front_weights(0)
                    for h in range(2):
                        sp.dma_start(bound[64 * h:64 * h + 64, :, :], maskf.rearrange("b q k -> q b k")).then_inc(s_cn, 16)
                    sp.dma_start(cs[:, :], cosT).then_inc(s_cn, 16)
                    sp.dma_start(sn[:, :], sinT).then_inc(s_cn, 16)
                    out_weights(0)
                    sp.wait_ge(s_pre_v, 1)
                    with sp.Fori(0, NG) as i:
                        nxt = (i + 1) % NG
                        front_weights(nxt)
                        sp.wait_ge(DV.sem, DV.value("wol", Step(i, 0)))
                        met(sp)
                        out_weights(nxt)
                        sp.wait_ge(DV.sem, DV.value("wfl", Step(i, 3)))
                        met(sp)
                    sp.wait_ge(s_ro, 16 * (NG + 1))

                def split_front_hi(act):
                    return act.activation(wf_h[:, :, :], raw_f[:, :, :], ACT.Copy, scale=WS)

                def split_front_lo(dve):
                    return dve.scalar_tensor_tensor(wf_l[:, :, :].rearrange("p a b -> p (a b)"),
                                                    raw_f[:, :, :].rearrange("p a b -> p (a b)"), WS,
                                                    wf_h[:, :, :].rearrange("p a b -> p (a b)"), ALU.mult, ALU.subtract)

                @block.gpsimd
                def _(pool):
                    for z in (sc, v, wo_h, wo_l):
                        pool.memset(z[:], 0.0)
                    pool.memset(rs[:, :, :], 0.0).then_inc(s_zero, 1)
                    PO.start(pool)
                    with pool.Fori(0, NG) as i:
                        for q in range(NQ):
                            st = Step(i, q)
                            for r in range(NR):
                                pool.wait_ge(AC.sem, AC.value(f"r{r}", st))
                                xr = xs[r % 2][:, :].rearrange("p (a s) -> p a s", s=S)
                                PO.mark(pool.tensor_tensor(xr, xr, sn[:, :].rearrange("p (a s) -> p a s", a=1)
                                                           .to_broadcast([P, QT // S, S]), ALU.mult), f"sm{r}", st)
                            pool.wait_ge(DV.sem, DV.value("rc", st))
                            s4 = sc[:, :, :, :, :].rearrange("p h t b k -> p (h t b) k")
                            PO.mark(pool.tensor_tensor(s4, s4, rs[:, :, :].rearrange("p h (t a) -> p (h t) a", a=1)
                                                       .to_broadcast([P, 16, S]), ALU.mult), "nm", st)

                @block.scalar
                def _(act):
                    act.wait_ge(s_rf, 48)
                    split_front_hi(act).then_inc(s_pre_a, 1)
                    AC.start(act)
                    act.wait_ge(s_zero, 1)

                    def back(st):
                        for h in range(2):
                            act.wait_ge(PE.sem, PE.value(f"pt{h}", st))
                            act.wait_ge(PE.sem, PE.value("pv3", st, 1))
                            AC.mark(act.activation(pt[:, h, :, :].rearrange("p a b -> p (a b)"), PTB[h][:, :], ACT.Copy),
                                    f"pe{h}", st)
                        for c in range(4):
                            tp, b2 = c // 2, c % 2
                            act.wait_ge(PE.sem, PE.value(f"pv{c}", st))
                            act.wait_ge(PE.sem, PE.value("w3", st, 1))
                            AC.mark(act.activation(heads(oh, tp, b2), PVB[b2][:, :].rearrange("p (t h s) -> p t h s", t=2, h=GQ),
                                                   ACT.Copy), f"hi{c}", st)

                    with act.Fori(0, NG) as i:
                        for q in range(NQ):
                            st = Step(i, q)
                            for r in range(NR):
                                act.wait_ge(PE.sem, PE.value(f"r{r}", st))
                                if r < 2:
                                    act.wait_ge(DV.sem, DV.value(f"ra{NR - 1}", st, 1))
                                else:
                                    act.wait_ge(DV.sem, DV.value(f"ra{r - 2}", st))
                                src = bank[r % 2]
                                act.activation(x0[r % 2][:, :], src[:, :], ACT.Copy)
                                act.activation(xs[r % 2][0:64, :], src[64:128, :], ACT.Copy)
                                AC.mark(act.activation(xs[r % 2][64:128, :], src[0:64, :], ACT.Copy), f"r{r}", st)
                            back(st)
                            act.wait_ge(PE.sem, PE.value("v", st))
                            AC.mark(act.activation(v[:, :, :].rearrange("p t n -> p (t n)"), bank[uses.index("v") % 2][:, :],
                                                   ACT.Copy, scale=OS / WS), "v", st)
                            if q == 3:
                                act.wait_ge(s_rf, i * 48 + 96)
                                AC.mark(split_front_hi(act), "wfh", st)
                            for h in range(2):
                                act.wait_ge(DV.sem, DV.value(f"sb{h}", st))
                                s2 = sc[:, h, :, :, :].rearrange("p a b c -> p (a b c)")
                                AC.mark(act.activation(s2, s2, ACT.Exp, scale=float(HD2) ** -0.5), f"ex{h}", st)
                            if q == 0:
                                act.wait_ge(s_ro, i * 16 + 16)
                                act.wait_ge(PE.sem, PE.value("w3", st))
                                AC.mark(act.activation(wo_h[:, :, :], raw_o[:, :, :], ACT.Copy, scale=WS), "woh", st)
                    back(Step(None, 0))

                @block.vector
                def _(dve):
                    dve.wait_ge(s_pre_a, 1)
                    split_front_lo(dve).then_inc(s_pre_v, 1)
                    dve.wait_ge(s_cn, 64)
                    bd = bound[:, :, :].rearrange("p b k -> p (b k)")
                    dve.tensor_scalar(bd, bd, 0.0, 0.0, ALU.is_equal, ALU.is_equal).then_inc(s_bd, 1)
                    dve.wait_ge(s_bd, 1)
                    dve.tensor_scalar(bd, bd, BIG, -1e9 * float(HD2) ** 0.5, ALU.mult, ALU.add).then_inc(s_bd, 1)
                    dve.wait_ge(s_bd, 2)
                    DV.start(dve)

                    def back_lo(st):
                        for c in range(4):
                            tp, b2 = c // 2, c % 2
                            dve.wait_ge(AC.sem, AC.value(f"hi{c}", st))
                            DV.mark(dve.tensor_tensor(heads(ol, tp, b2), PVB[b2][:, :].rearrange("p (t h s) -> p t h s", t=2, h=GQ),
                                                      heads(oh, tp, b2), ALU.subtract), f"lo{c}", st)

                    def back_add(st):
                        for t in range(TQ):
                            dve.wait_ge(PE.sem, PE.value(f"w{t}", st))
                            row = acc[:, t + TQ * ((st.q - 1) % NQ if st.i is not None else NQ - 1), :]
                            DV.mark(dve.scalar_tensor_tensor(row, bank[uses.index(f"w{t}") % 2][:, :], 1 / (WS * OS), row,
                                                             ALU.mult, ALU.add), f"w{t}", st)

                    def cosine(st, r):
                        dve.wait_ge(AC.sem, AC.value(f"r{r}", st))
                        xr = x0[r % 2][:, :].rearrange("p (a s) -> p a s", s=S)
                        DV.mark(dve.tensor_tensor(xr, xr, cs[:, :].rearrange("p (a s) -> p a s", a=1)
                                                  .to_broadcast([P, QT // S, S]), ALU.mult), f"cm{r}", st)

                    def rotate(st, r):
                        dve.wait_ge(PO.sem, PO.value(f"sm{r}", st))
                        dve.wait_ge(DV.sem, DV.value(f"cm{r}", st))
                        if r == 0:
                            dve.wait_ge(PE.sem, PE.value("s1", st, 1))
                        o = rk[:, :].rearrange("p (a s) -> p a s", s=S) if r == 0 else rq[:, (r - 1) // 2, :, (r - 1) % 2, :]
                        DV.mark(dve.tensor_tensor(o, x0[r % 2][:, :].rearrange("p (a s) -> p a s", s=S),
                                                  xs[r % 2][:, :].rearrange("p (a s) -> p a s", s=S), ALU.add), f"ra{r}", st)

                    with dve.Fori(0, NG) as i:
                        for q in range(NQ):
                            st = Step(i, q)
                            for r in range(NR + 1):
                                if r < NR:
                                    cosine(st, r)
                                if r:
                                    rotate(st, r - 1)
                            back_lo(st)
                            for h in range(2):
                                s3 = sc[:, h, :, :, :].rearrange("p a b c -> p (a b) c")
                                bnd = bound[:, 2 * TQ * q:2 * TQ * (q + 1), :]
                                dve.wait_ge(PE.sem, PE.value(f"s{h}", st))
                                DV.mark(dve.tensor_tensor(s3, SB[h][:, :].rearrange("p (a c) -> p a c", a=8), bnd, ALU.min),
                                        f"mn{h}", st)
                                dve.wait_ge(DV.sem, DV.value(f"mn{h}", st))
                                DV.mark(dve.tensor_reduce(mx[:, h, :], s3, AX.X, ALU.max), f"mx{h}", st)
                                dve.wait_ge(DV.sem, DV.value(f"mx{h}", st))
                                DV.mark(dve.tensor_tensor(s3, s3, mx[:, h, :].rearrange("p (a c) -> p a c", c=1)
                                                          .to_broadcast([P, 8, S]), ALU.subtract), f"sb{h}", st)
                            if q == 3:
                                dve.wait_ge(AC.sem, AC.value("wfh", st))
                                DV.mark(split_front_lo(dve), "wfl", st)
                            back_add(st)
                            if q == 0:
                                dve.wait_ge(AC.sem, AC.value("woh", st))
                                DV.mark(dve.scalar_tensor_tensor(wo_l[:, :, :].rearrange("p a b -> p (a b)"),
                                                                 raw_o[:, :, :].rearrange("p a b -> p (a b)"), WS,
                                                                 wo_h[:, :, :].rearrange("p a b -> p (a b)"),
                                                                 ALU.mult, ALU.subtract), "wol", st)
                            dve.wait_ge(AC.sem, AC.value("ex1", st))
                            DV.mark(dve.tensor_reduce(sm[:, :, :], sc[:, :, :, :, :].rearrange("p h t b k -> p h (t b) k"), AX.X,
                                                      ALU.add), "sum", st)
                            dve.wait_ge(DV.sem, DV.value("sum", st))
                            DV.mark(dve.reciprocal(rs[:, :, :], sm[:, :, :]), "rc", st)
                    st = Step(None, 0)
                    back_lo(st)
                    back_add(st)

                @block.tensor
                def _(pe):
                    PE.start(pe)
                    pe.wait_ge(s_zero, 1)
                    pe.wait_ge(s_pre_v, 1)

                    def back_pv(st):
                        pe.wait_ge(PO.sem, PO.value("nm", st, 1))
                        for h in range(2):
                            pe.wait_ge(AC.sem, AC.value(f"pe{h}", st, 1))
                            for t in range(TQ):
                                mm = pe.transpose(PTB[h][:, t * P:(t + 1) * P],
                                                  sc[:, h, t, :, :].rearrange("p b k -> p (b k)"), ident[:, :])
                            PE.mark(mm, f"pt{h}", st)
                        pe.wait_ge(AC.sem, AC.value("pe1", st))
                        pe.wait_ge(AC.sem, AC.value("v", st, 1))
                        for c in range(4):
                            tp, b2 = c // 2, c % 2
                            if c < 2:
                                pe.wait_ge(DV.sem, DV.value(f"lo{c + 2}", st, 1))
                            else:
                                pe.wait_ge(DV.sem, DV.value(f"lo{c - 2}", st))
                            rows = slice(64 * b2, 64 * b2 + 64)
                            for t2 in range(2):
                                t = 2 * tp + t2
                                mm = pe.matmul(PVB[b2][:, t2 * 256:(t2 + 1) * 256], v[rows, t, :], pt[rows, :, t, :],
                                               start=True, stop=True)
                            PE.mark(mm, f"pv{c}", st)

                    def back_out(st):
                        pe.wait_ge(DV.sem, DV.value("lo3", st))
                        if st.q == 1:
                            pe.wait_ge(DV.sem, DV.value("wol", st, 1))
                        for t in range(TQ):
                            o = gbank(pe, f"w{t}", st)
                            tok = slice(t * P, (t + 1) * P)
                            PE.mark(three_pass(pe, o[:, :], [(oh[:, h, tok], ol[:, h, tok], wo_h[:, h, :], wo_l[:, h, :])
                                                             for h in range(GQ)]), f"w{t}", st)

                    with pe.Fori(0, NG) as i:
                        for q in range(NQ):
                            st = Step(i, q)
                            if q == 0:
                                pe.wait_ge(DV.sem, DV.value("wfl", st, 1))
                            tok = slice(q * QT, (q + 1) * QT)
                            for r in range(NR):
                                o = gbank(pe, f"r{r}", st)
                                c = GQ * HD2 if r == 0 else (r - 1) * HD2
                                ah, al = (ch, cl) if r == 0 else (xh, xl)
                                PE.mark(three_pass(pe, o[:, :], [(wf_h[:, k, c:c + P], wf_l[:, k, c:c + P], ah[:, k, tok],
                                                                  al[:, k, tok]) for k in range(KD)]), f"r{r}", st)
                            back_pv(st)
                            for h in range(2):
                                pe.wait_ge(DV.sem, DV.value(f"mn{h}", st, 1))
                                if h == 0:
                                    pe.wait_ge(DV.sem, DV.value(f"ra{NR - 1}", st))
                                for bb in range(2 * TQ):
                                    tk = slice(64 * bb, 64 * bb + 64)
                                    mm = pe.matmul(SB[h][:, tk], rq[:, h, bb, :, :].rearrange("p a s -> p (a s)"), rk[:, tk],
                                                   start=True, stop=True)
                                PE.mark(mm, f"s{h}", st)
                            o = gbank(pe, "v", st)
                            c = (GQ + 1) * HD2
                            for t in range(TQ):
                                tk = slice(q * QT + t * P, q * QT + (t + 1) * P)
                                mm = three_pass(pe, o[:, t * P:(t + 1) * P],
                                                [(ch[:, k, tk], cl[:, k, tk], wf_h[:, k, c:c + P], wf_l[:, k, c:c + P])
                                                 for k in range(KD)])
                            PE.mark(mm, "v", st)
                            back_out(st)
                    st = Step(None, 0)
                    back_pv(st)
                    back_out(st)

        cw = sb("cw", [P, NT, NE + 1])

        def router():
            with ExitStack() as ctx:
                def b(name, shape, dt=F32):
                    return sb("ro_" + name, shape, dt, ctx)
                raw, gh, gl = b("raw", [P, KD, NE]), b("gh", [P, KD, NE], F16), b("gl", [P, KD, NE], F16)
                bi, io = b("bi", [P, NE]), b("io", [P, NE])
                sg = b("sg", [P, NT, NE])
                top8, idx, idf = b("top8", [P, NT, 8]), b("idx", [P, NT, 8], U32), b("idf", [P, NT, 8])
                tot, rt, w4 = b("tot", [P, NT]), b("rt", [P, NT]), b("w4", [P, NT, TOPK])
                one, hit = b("one", [P, NT, NE]), b("hit", [P, NT, NE])
                s_in, s_g, s_mm, s_a, s_v = sem("ro_in"), sem("ro_g"), sem("ro_mm"), sem("ro_a"), sem("ro_v")
                block = ctx.enter_context(nc.Block())

                @block.sync
                def _(sp):
                    sp.dma_start(raw[:, :, :], gwT.rearrange("(k p) n -> p k n", p=P)).then_inc(s_in, 16)
                    sp.dma_start(bi[:, :], gbias.rearrange("(a n) -> a n", a=1).to_broadcast([P, NE])).then_inc(s_in, 16)
                    sp.dma_start(io[:, :], iota).then_inc(s_in, 16)

                @block.tensor
                def _(pe):
                    pe.wait_ge(s_g, 2)
                    for t in range(NT):
                        tok = slice(t * P, (t + 1) * P)
                        mm = three_pass(pe, bank[0][:, t * NE:(t + 1) * NE],
                                        [(xh[:, k, tok], xl[:, k, tok], gh[:, k, :], gl[:, k, :]) for k in range(KD)])
                    mm.then_inc(s_mm, 1)

                @block.scalar
                def _(act):
                    act.wait_ge(s_mm, 1)
                    act.activation(sg[:, :, :].rearrange("p t e -> p (t e)"), bank[0][:, 0:NT * NE], ACT.Exp,
                                   scale=-1 / WS).then_inc(s_a, 1)

                @block.vector
                def _(dve):
                    n = [0]

                    def then(m):
                        n[0] += 1
                        m.then_inc(s_v, 1)
                        dve.wait_ge(s_v, n[0])
                    dve.wait_ge(s_in, 48)
                    dve.tensor_scalar(gh[:, :, :], raw[:, :, :], WS, None, ALU.mult).then_inc(s_g, 1)
                    dve.wait_ge(s_g, 1)
                    dve.scalar_tensor_tensor(gl[:, :, :].rearrange("p k n -> p (k n)"), raw[:, :, :].rearrange("p k n -> p (k n)"), WS,
                                             gh[:, :, :].rearrange("p k n -> p (k n)"), ALU.mult, ALU.subtract).then_inc(s_g, 1)
                    dve.wait_ge(s_a, 1)
                    then(dve.tensor_scalar(sg[:, :, :], sg[:, :, :], 1.0, None, ALU.add))
                    then(dve.reciprocal(sg[:, :, :], sg[:, :, :]))
                    then(dve.tensor_tensor(sg[:, :, :], sg[:, :, :], bi[:, :].rearrange("p (a e) -> p a e", a=1)
                                           .to_broadcast([P, NT, NE]), ALU.add))
                    for t in range(NT):
                        m = dve.max(top8[:, t, :], sg[:, t, :])
                    then(m)
                    for t in range(NT):
                        m = dve.max_index(idx[:, t, :], top8[:, t, :], sg[:, t, :])
                    dve.tensor_reduce(tot[:, :], top8[:, :, 0:TOPK], AX.X, ALU.add)
                    then(m2 := dve.memset(cw[:, :, :], 0.0))
                    dve.tensor_copy(idf[:, :, :], idx[:, :, :])
                    then(dve.tensor_scalar(tot[:, :], tot[:, :], 1e-20, None, ALU.add))
                    then(dve.reciprocal(rt[:, :], tot[:, :]))
                    dve.memset(cw[:, :, NE:NE + 1], 1.0)
                    then(dve.tensor_tensor(w4[:, :, :], top8[:, :, 0:TOPK], rt[:, :].rearrange("p (t a) -> p t a", a=1)
                                           .to_broadcast([P, NT, TOPK]), ALU.mult))
                    for j in range(TOPK):
                        then(dve.tensor_tensor(one[:, :, :], io[:, :].rearrange("p (a e) -> p a e", a=1).to_broadcast([P, NT, NE]),
                                               idf[:, :, j:j + 1].to_broadcast([P, NT, NE]), ALU.is_equal))
                        then(dve.tensor_tensor(hit[:, :, :], one[:, :, :], w4[:, :, j:j + 1].to_broadcast([P, NT, NE]), ALU.mult))
                        then(dve.tensor_tensor(cw[:, :, 0:NE], cw[:, :, 0:NE], hit[:, :, :], ALU.add))
                    then(dve.tensor_scalar(cw[:, :, :], cw[:, :, :], 1 / (WS * OS), None, ALU.mult))

        def experts():
            NG = NE + 1
            with ExitStack() as ctx:
                def b(name, shape, dt=F32):
                    return sb("mo_" + name, shape, dt, ctx)
                raw_f, wf_h, wf_l = b("raw_f", [P, KD, 2 * FI]), b("wf_h", [P, KD, 2 * FI], F16), b("wf_l", [P, KD, 2 * FI], F16)
                raw_o, wo_h, wo_l = b("raw_o", [P, IB, D]), b("wo_h", [P, IB, D], F16), b("wo_l", [P, IB, D], F16)
                cwe = b("cwe", [P, NT])
                sg = b("sg", [P, IB, QT])
                z = b("z", [P, IB, QT])
                zh = [b(f"zh{j}", [P, IB, QT], F16) for j in range(2)]
                zl = [b(f"zl{j}", [P, IB, QT], F16) for j in range(2)]
                s_rf, s_ro = sem("mo_s_rf"), sem("mo_s_ro")
                PE = Timeline(sem("mo_pe"), events(["g0", "u0", "g1", "u1", "y0", "y1", "y2", "y3"]), NG, ["y0", "y1", "y2", "y3"])
                AC = Timeline(sem("mo_act"), events(["si0", "si1"], [(3, "si1", ["wfh"]), (0, "si1", ["woh"])]), NG)
                DV = Timeline(sem("mo_dve"), events(["z0", "z1", "y0", "y1", "y2", "y3"], [(3, "z1", ["wfl"]), (0, "y3", ["wol", "cw"])]),
                              NG, ["y0", "y1", "y2", "y3"])
                PO = Timeline(sem("mo_pool"), events(["zh0", "zl0", "zh1", "zl1"]), NG)
                s_pre_a, s_pre_v, s_zero = sem("mo_pre_a"), sem("mo_pre_v"), sem("mo_zero")
                block = ctx.enter_context(nc.Block())

                @block.sync
                def _(sp):
                    def front_weights(g):
                        sp.dma_start(raw_f[:, :, :], egu[bass.ds(g * D, D), :].rearrange("(k p) n -> p k n", p=P)).then_inc(s_rf, 16)

                    def out_weights(g):
                        sp.dma_start(raw_o[:, :, :], ed[bass.ds(g * FI, FI), :].rearrange("(k p) n -> p k n", p=P)).then_inc(s_ro, 16)
                    front_weights(0)
                    out_weights(0)
                    sp.wait_ge(s_pre_v, 1)
                    with sp.Fori(0, NG) as i:
                        nxt = (i + 1) % NG
                        front_weights(nxt)
                        sp.wait_ge(DV.sem, DV.value("wol", Step(i, 0)))
                        met(sp)
                        out_weights(nxt)
                        sp.wait_ge(DV.sem, DV.value("wfl", Step(i, 3)))
                        met(sp)
                    sp.wait_ge(s_ro, 16 * (NG + 1))

                def split_front_hi(act):
                    return act.activation(wf_h[:, :, :], raw_f[:, :, :], ACT.Copy, scale=WS)

                def split_front_lo(dve):
                    return dve.scalar_tensor_tensor(wf_l[:, :, :].rearrange("p a b -> p (a b)"),
                                                    raw_f[:, :, :].rearrange("p a b -> p (a b)"), WS,
                                                    wf_h[:, :, :].rearrange("p a b -> p (a b)"), ALU.mult, ALU.subtract)

                @block.gpsimd
                def _(pool):
                    for m in (zh[1], zl[1], wo_h, wo_l):
                        pool.memset(m[:], 0.0)
                    pool.memset(cwe[:, :], 0.0).then_inc(s_zero, 1)
                    PO.start(pool)
                    with pool.Fori(0, NG) as i:
                        for q in range(NQ):
                            st = Step(i, q)
                            for n in range(IB):
                                pool.wait_ge(DV.sem, DV.value(f"z{n}", st))
                                pool.wait_ge(PE.sem, PE.value("y3", st, 1))
                                met(pool)
                                PO.mark(pool.tensor_copy(zh[q % 2][:, n, :], z[:, n, :]), f"zh{n}", st)
                                pool.wait_ge(PO.sem, PO.value(f"zh{n}", st))
                                PO.mark(pool.tensor_tensor(zl[q % 2][:, n, :], z[:, n, :], zh[q % 2][:, n, :], ALU.subtract),
                                        f"zl{n}", st)

                @block.scalar
                def _(act):
                    act.wait_ge(s_rf, 16)
                    split_front_hi(act).then_inc(s_pre_a, 1)
                    AC.start(act)
                    act.wait_ge(s_zero, 1)
                    with act.Fori(0, NG) as i:
                        for q in range(NQ):
                            st = Step(i, q)
                            for n in range(IB):
                                act.wait_ge(PE.sem, PE.value(f"g{n}", st))
                                act.wait_ge(DV.sem, DV.value(f"z{n}", st, 1))
                                AC.mark(act.activation(sg[:, n, :], bank[2 * n][:, :], ACT.Silu, scale=1 / WS), f"si{n}", st)
                            if q == 3:
                                act.wait_ge(s_rf, i * 16 + 32)
                                act.wait_ge(PE.sem, PE.value("u1", st))
                                AC.mark(split_front_hi(act), "wfh", st)
                            if q == 0:
                                act.wait_ge(s_ro, i * 16 + 16)
                                act.wait_ge(PE.sem, PE.value("y3", st))
                                AC.mark(act.activation(wo_h[:, :, :], raw_o[:, :, :], ACT.Copy, scale=WS), "woh", st)

                @block.vector
                def _(dve):
                    dve.wait_ge(s_pre_a, 1)
                    split_front_lo(dve).then_inc(s_pre_v, 1)
                    dve.wait_ge(s_zero, 1)
                    DV.start(dve)

                    def back_add(st):
                        for t in range(TQ):
                            tile = t + TQ * ((st.q - 1) % NQ if st.i is not None else NQ - 1)
                            dve.wait_ge(PE.sem, PE.value(f"y{t}", st))
                            DV.mark(dve.scalar_tensor_tensor(acc[:, tile, :], bank[4 + t][:, :], cwe[:, tile:tile + 1],
                                                             acc[:, tile, :], ALU.mult, ALU.add), f"y{t}", st)

                    with dve.Fori(0, NG) as i:
                        for q in range(NQ):
                            st = Step(i, q)
                            for n in range(IB):
                                dve.wait_ge(PE.sem, PE.value(f"u{n}", st))
                                dve.wait_ge(AC.sem, AC.value(f"si{n}", st))
                                dve.wait_ge(PO.sem, PO.value(f"zl{n}", st, 1))
                                DV.mark(dve.scalar_tensor_tensor(z[:, n, :], bank[2 * n + 1][:, :], OS / WS, sg[:, n, :],
                                                                 ALU.mult, ALU.mult), f"z{n}", st)
                            if q == 3:
                                dve.wait_ge(AC.sem, AC.value("wfh", st))
                                DV.mark(split_front_lo(dve), "wfl", st)
                            if q == 1:
                                dve.wait_ge(DV.sem, DV.value("cw", st, 1))
                            back_add(st)
                            if q == 0:
                                dve.wait_ge(AC.sem, AC.value("woh", st))
                                DV.mark(dve.scalar_tensor_tensor(wo_l[:, :, :].rearrange("p a b -> p (a b)"),
                                                                 raw_o[:, :, :].rearrange("p a b -> p (a b)"), WS,
                                                                 wo_h[:, :, :].rearrange("p a b -> p (a b)"),
                                                                 ALU.mult, ALU.subtract), "wol", st)
                                dve.wait_ge(DV.sem, DV.value("y3", st))
                                DV.mark(dve.tensor_copy(cwe[:, :].rearrange("p (t a) -> p t a", a=1), cw[:, :, bass.ds(i, 1)]),
                                        "cw", st)
                    back_add(Step(None, 0))

                @block.tensor
                def _(pe):
                    PE.start(pe)
                    pe.wait_ge(s_zero, 1)
                    pe.wait_ge(s_pre_v, 1)

                    def back_out(st):
                        par = (st.q - 1) % 2 if st.i is not None else (NQ - 1) % 2
                        if st.q == 1:
                            pe.wait_ge(DV.sem, DV.value("wol", st, 1))
                        pe.wait_ge(PO.sem, PO.value("zl1", st, 1))
                        for t in range(TQ):
                            pe.wait_ge(DV.sem, DV.value(f"y{t}", st, 1))
                            tok = slice(t * P, (t + 1) * P)
                            PE.mark(three_pass(pe, bank[4 + t][:, :], [(zh[par][:, n, tok], zl[par][:, n, tok], wo_h[:, n, :],
                                                                        wo_l[:, n, :]) for n in range(IB)]), f"y{t}", st)

                    with pe.Fori(0, NG) as i:
                        for q in range(NQ):
                            st = Step(i, q)
                            if q == 0:
                                pe.wait_ge(DV.sem, DV.value("wfl", st, 1))
                            tok = slice(q * QT, (q + 1) * QT)
                            for n in range(IB):
                                for u, name in enumerate(("g", "u")):
                                    if u == 0:
                                        pe.wait_ge(AC.sem, AC.value(f"si{n}", st, 1))
                                    else:
                                        pe.wait_ge(DV.sem, DV.value(f"z{n}", st, 1))
                                    c = u * FI + n * P
                                    PE.mark(three_pass(pe, bank[2 * n + u][:, :],
                                                       [(wf_h[:, k, c:c + P], wf_l[:, k, c:c + P], xh[:, k, tok], xl[:, k, tok])
                                                        for k in range(KD)]), f"{name}{n}", st)
                            back_out(st)
                    back_out(Step(None, 0))

        load_split("x", xT, xh, xl, load_constants)
        self_attention()
        layernorm("ln1", False)
        cross_attention()
        layernorm("ln2", False)
        router()
        experts()
        layernorm("ln3", True)


def kernel(**inputs):
    import numpy as np
    import concourse.bacc as bacc
    from concourse.bass_utils import run_bass_kernel_spmd

    f = {k: np.asarray(v) for k, v in inputs.items()}
    x = f["x"].reshape(T, D)
    half = HD2 // 2
    inv = (np.float32(1.0) / np.power(np.float32(10000.0), np.arange(0, HD2, 2, dtype=np.float32) / np.float32(HD2))).astype(np.float32)
    ang = (np.arange(S, dtype=np.float32)[None, :] * inv[:, None]).astype(np.float32)
    cos, sin = np.cos(ang) / np.float32(WS), np.sin(ang) / np.float32(WS)
    pos = np.arange(P) % S
    arrays = {
        "x": x,
        "xT": x.T,
        "cT": f["ctx_4096"].reshape(T, D).T,
        "maskf": f["mask_BxSxS2_ff1"],
        "wqT": f["L0_attn_Wq"].T, "bq": f["L0_attn_bq"],
        "wkT": f["L0_attn_Wk"].T, "bk": f["L0_attn_bk"],
        "wvT": f["L0_attn_Wv"].T, "bv": f["L0_attn_bv"],
        "woT": f["L0_attn_Wo"].T, "bo": f["L0_attn_bo"],
        "xwq": f["L0_xattn_wq"], "xwk": f["L0_xattn_wk"], "xwv": f["L0_xattn_wv"], "xwo": f["L0_xattn_wo"],
        "gwT": f["L0_ffn_gate_w"].T, "gbias": f["L0_ffn_bias"],
        "egu": np.concatenate([np.concatenate([f["L0_ffn_Wg"], f["L0_ffn_Sg"][None]]).transpose(0, 2, 1),
                               np.concatenate([f["L0_ffn_Wu"], f["L0_ffn_Su"][None]]).transpose(0, 2, 1)], axis=2)
        .reshape((NE + 1) * D, 2 * FI),
        "ed": np.concatenate([f["L0_ffn_Wd"], f["L0_ffn_Sd"][None]]).transpose(0, 2, 1).reshape((NE + 1) * FI, D),
        "causal": np.where(np.arange(S)[None, :] <= pos[:, None], np.float32(BIG), np.float32(-1e30)).astype(np.float32),
        "cosT": np.concatenate([cos, cos]).astype(np.float32),
        "sinT": np.concatenate([-sin, sin]).astype(np.float32),
        "parity": np.stack([(np.arange(P) // HD1) % 2 == e for e in range(2)], axis=1).astype(np.float32),
        "eye": np.eye(P, dtype=np.float32),
        "iota": np.broadcast_to(np.arange(NE, dtype=np.float32), (P, NE)),
    }
    nc = bacc.Bacc("TRN2", target_bir_lowering=False, num_devices=1)
    given, args = {}, []
    for name, a in arrays.items():
        a = np.ascontiguousarray(a)
        given[f"in_{name}"] = a
        args.append(nc.dram_tensor(f"in_{name}", a.shape, mybir.dt.from_np(a.dtype), kind="ExternalInput").ap())
    out = nc.dram_tensor("out_0", (T, D), F32, kind="ExternalOutput").ap()
    build(nc, *args, out)
    r = run_bass_kernel_spmd(nc, [given], core_ids=[0])
    return r.results[0]["out_0"].reshape(B, S, D)
```

```python
import concourse.bass as bass
from concourse import mybir
from contextlib import ExitStack

F32, F16, U32 = mybir.dt.float32, mybir.dt.float16, mybir.dt.uint32
ALU, ACT, AX = mybir.AluOpType, mybir.ActivationFunctionType, mybir.AxisListType

B, S, D = 32, 64, 512
T = B * S
P = 128
NT = T // P
TQ = 4
NQ = NT // TQ
QT = TQ * P
KD = D // P
H1, HD1 = 32, 16
HG = P // HD1
H2, HKV, HD2 = 32, 8, 128
GQ = H2 // HKV
NE, TOPK, FI = 16, 4, 256
IB = FI // P
EPS = 1e-5
WS = 64.0
OS = 64.0
BIG = 3.0e38


class Timeline:

    def __init__(self, sem, body, rounds, post=()):
        self.sem, self.body, self.rounds, self.post = sem, list(body), rounds, list(post)
        self.index = {k: n for n, k in enumerate(self.body)}
        self.post_index = {k: n for n, k in enumerate(self.post)}
        assert len(self.index) == len(self.body)
        self.cursor = 0

    def start(self, eng):
        eng.sem_inc(self.sem, len(self.body))

    def mark(self, instruction, name, step):
        order = self.post if step.i is None else self.body
        key = name if step.i is None else (step.q, name)
        assert order[self.cursor] == key, (order[self.cursor], key)
        self.cursor = (self.cursor + 1) % len(order)
        instruction.then_inc(self.sem, 1)

    def value(self, name, step, back=0):
        n = len(self.body)
        if step.i is None:
            if back == 0:
                return (self.rounds + 1) * n + self.post_index[name] + 1
            return self.rounds * n + self.index[(NQ - back, name)] + 1
        q = step.q - back
        if q >= 0:
            return step.i * n + n + self.index[(q, name)] + 1
        return step.i * n + self.index[(q + NQ, name)] + 1


class Step:

    def __init__(self, i, q):
        self.i, self.q = i, q


def events(per_step, extra=()):
    out = []
    for q in range(NQ):
        for name in per_step:
            out.append((q, name))
            for qq, after, names in extra:
                if qq == q and after == name:
                    out += [(q, x) for x in names]
    return out


def build(nc, x, xT, cT, maskf, wqT, bq, wkT, bk, wvT, bv, woT, bo, xwq, xwk, xwv, xwo,
          gwT, gbias, egu, ed, causal, cosT, sinT, parity, eye, iota, out):
    top = ExitStack()
    with top:
        def sb(name, shape, dt=F32, where=top):
            return where.enter_context(nc.sbuf_tensor(name, shape, dt))

        def sem(name):
            return top.enter_context(nc.semaphore(name))

        bank = [top.enter_context(nc.psum_tensor(f"bank{n}", [P, 512], F32)) for n in range(8)]

        acc = sb("acc", [P, NT, D])
        xh = sb("xh", [P, KD, T], F16)
        xl = sb("xl", [P, KD, T], F16)
        ident = sb("ident", [P, P])
        mv = sb("mv", [P, NT, 2])
        rstd = sb("rstd", [P, NT, 1])
        eps = sb("eps", [P, 1])
        FRONT, OUTW = KD * (GQ + 2) * HD2, GQ * D
        raw_front, front_h, front_l = sb("raw_front", [P, FRONT]), sb("front_h", [P, FRONT], F16), sb("front_l", [P, FRONT], F16)
        raw_out, out_h, out_l = sb("raw_out", [P, OUTW]), sb("out_h", [P, OUTW], F16), sb("out_l", [P, OUTW], F16)

        def blocks(buffer, k):
            def view(n):
                return buffer[:, 0:k * n].rearrange("p (k n) -> p k n", k=k)
            return view

        s_met = sem("waits_met")

        def met(eng):
            eng.sem_inc(s_met, 1)

        def split_on_pool(pool, chain, raw, hi, lo, scale=None):
            if scale:
                chain(pool.tensor_scalar(raw, raw, scale, None, ALU.mult))
            chain(pool.tensor_copy(hi, raw))
            chain(pool.tensor_tensor(lo, raw, hi, ALU.subtract))

        def chained(eng, s):
            n = [0]

            def chain(m):
                n[0] += 1
                m.then_inc(s, 1)
                eng.wait_ge(s, n[0])
            return chain

        def layernorm(tag, last, prefetch=None, prepare=None):
            with ExitStack() as ctx:
                st = sb(f"{tag}_st", [P, NT, 6], where=ctx)
                xn = [sb(f"{tag}_xn{j}", [P, D], where=ctx) for j in range(TQ)]
                s_st, s_ag, s_sq, s_rs = sem(f"{tag}_st"), sem(f"{tag}_ag"), sem(f"{tag}_sq"), sem(f"{tag}_rs")
                s_out = [sem(f"{tag}_s_out{j}") for j in range(TQ)] if last else None
                order = [f"norm{j}" for j in range(TQ)] + ([] if last else [f"lo{j}" for j in range(TQ)])
                DV = Timeline(sem(f"{tag}_dve"), [(0, n) for n in order], NQ)
                AC = Timeline(sem(f"{tag}_act"), [(0, f"{w}{j}") for j in range(TQ) for w in ("hi", "back")], NQ)
                PE = Timeline(sem(f"{tag}_pe"), [(0, f"turn{j}") for j in range(TQ)], NQ)

                def before(tl, name, r):
                    return r.i * len(tl.body) + tl.index[(0, name)] + 1

                block = ctx.enter_context(nc.Block())

                @block.vector
                def _(dve):
                    for t in range(NT):
                        dve.bn_stats(st[:, t, :], acc[:, t, :]).then_inc(s_st, 1)
                    for t in range(NT):
                        dve.wait_ge(s_st, t + 1)
                        dve.bn_aggr(mv[:, t, :], st[:, t, :]).then_inc(s_ag, 1)
                    dve.wait_ge(s_sq, 1)
                    dve.reciprocal(rstd[:, :, :], rstd[:, :, :]).then_inc(s_rs, 1)
                    dve.wait_ge(s_rs, 1)
                    DV.start(dve)
                    with dve.Fori(0, NQ) as i:
                        r = Step(i, 0)
                        for j in range(TQ):
                            if last:
                                dve.wait_ge(s_out[j], i * 16 + 16)
                            else:
                                dve.wait_ge(AC.sem, before(AC, f"back{j}", r))
                            DV.mark(dve.tensor_scalar(xn[j][:, :], acc[:, i * TQ + j, :], mv[:, i * TQ + j, 0:1],
                                                      rstd[:, i * TQ + j, 0:1], ALU.subtract, ALU.mult), f"norm{j}", r)
                        for j in range(TQ if not last else 0):
                            dve.wait_ge(AC.sem, AC.value(f"hi{j}", r))
                            tok = bass.ds(i * QT + j * P, P)
                            DV.mark(dve.tensor_tensor(xl[:, :, tok], bank[j][:, :].rearrange("p (k t) -> p k t", k=KD),
                                                      xh[:, :, tok], ALU.subtract), f"lo{j}", r)

                @block.scalar
                def _(act):
                    act.wait_ge(s_ag, NT)
                    act.activation(rstd[:, :, :], mv[:, :, 1:2], ACT.Sqrt, bias=eps[:, :]).then_inc(s_sq, 1)
                    if last:
                        return
                    AC.start(act)
                    with act.Fori(0, NQ) as i:
                        r = Step(i, 0)
                        for j in range(TQ):
                            act.wait_ge(PE.sem, PE.value(f"turn{j}", r))
                            AC.mark(act.activation(xh[:, :, bass.ds(i * QT + j * P, P)],
                                                   bank[j][:, :].rearrange("p (k t) -> p k t", k=KD), ACT.Copy), f"hi{j}", r)
                            AC.mark(act.activation(acc[:, i * TQ + j, :], xn[j][:, :], ACT.Copy), f"back{j}", r)

                @block.gpsimd
                def _(pool):
                    if prepare:
                        prepare(pool)

                @block.sync
                def _(sp):
                    if prefetch:
                        prefetch(sp)
                    if last:
                        for j in range(TQ):
                            sp.sem_inc(s_out[j], 16)
                        with sp.Fori(0, NQ) as i:
                            r = Step(i, 0)
                            for j in range(TQ):
                                sp.wait_ge(DV.sem, DV.value(f"norm{j}", r))
                                met(sp)
                                sp.dma_start(out[bass.ds(i * QT + j * P, P), :], xn[j][:, :]).then_inc(s_out[j], 16)
                        for j in range(TQ):
                            sp.wait_ge(s_out[j], 16 * (NQ + 1))

                @block.tensor
                def _(pe):
                    if last:
                        return
                    PE.start(pe)
                    with pe.Fori(0, NQ) as i:
                        r = Step(i, 0)
                        for j in range(TQ):
                            pe.wait_ge(DV.sem, DV.value(f"norm{j}", r))
                            pe.wait_ge(DV.sem, before(DV, f"lo{j}", r))
                            for k in range(KD):
                                mm = pe.transpose(bank[j][:, k * P:(k + 1) * P], xn[j][:, k * P:(k + 1) * P], ident[:, :])
                            PE.mark(mm, f"turn{j}", r)

        def three_pass(pe, out_ap, pairs, start=True, stop=True):
            n = len(pairs)
            for m, (ah, al, bh, bl) in enumerate(pairs):
                pe.matmul(out_ap, ah, bh, start=start and m == 0, stop=False)
                pe.matmul(out_ap, ah, bl, start=False, stop=False)
                mm = pe.matmul(out_ap, al, bh, start=False, stop=stop and m == n - 1)
            return mm

        def self_attention(prefetch_ctx):
            NG, FW = H1 // HG, 3 * P
            with ExitStack() as ctx:
                def b(name, shape, dt=F32):
                    return sb("sa_" + name, shape, dt, ctx)
                raw_f, wf_h, wf_l = (blocks(z, KD)(FW) for z in (raw_front, front_h, front_l))
                flat_f = [z[:, 0:KD * FW] for z in (raw_front, front_h, front_l)]
                raw_o, wo_h, wo_l = raw_out[:, 0:D], out_h[:, 0:D], out_l[:, 0:D]
                stage = [b(f"stage{n}", [P, KD, QT]) for n in range(2)]
                rawb, bias_c, bv_row = b("rawb", [P, 2 + P]), b("bias_c", [P, 2]), b("bv_row", [P, P])
                par, caus = b("par", [P, 2]), b("caus", [P, S])
                qh, ql = b("qh", [P, QT], F16), b("ql", [P, QT], F16)
                kf, kxh, kxl = b("kf", [P, QT]), b("kxh", [P, 2, QT], F16), b("kxl", [P, 2, QT], F16)
                sc = b("sc", [P, 4, TQ, 2, S])
                mx, sm, rs = b("mx", [P, 4, 8]), b("sm", [P, 4, 8]), b("rs", [P, TQ, HG, 1])
                vf, vh, vl = b("vf", [P, TQ, P]), b("vh", [P, TQ, P], F16), b("vl", [P, TQ, P], F16)
                vbh, vbl = (b(n, [P, 2, TQ, 4, 2, HD1], F16) for n in ("vbh", "vbl"))
                pth, ptl = b("pth", [P, 4, TQ, P], F16), b("ptl", [P, 4, TQ, P], F16)
                at = b("at", [P, TQ, P])
                oh, ol = b("oh", [P, QT], F16), b("ol", [P, QT], F16)
                s_rf, s_ro, s_cn = sem("sa_s_rf"), sem("sa_s_ro"), sem("sa_s_cn")
                s_st, s_q0h, s_q0l, s_xq, s_acc = (sem("sa_" + n) for n in ("s_st0", "s_q0h", "s_q0l", "s_xq", "s_acc"))

                SB, PTB, PVB = [bank[2], bank[3]], [bank[4], bank[5]], bank[6]
                uses = ["k", "q", "v", "oT", "w0", "w1", "w2", "w3"]
                J4 = range(4)
                PE = Timeline(sem("sa_pe"), events(["k", "q", "pt0", "pt1", "v", "pt2", "pt3", "s0", "s1", "pv", "s2", "oT",
                                                    "s3", "w0", "w1", "w2", "w3"]), NG,
                              ["pt0", "pt1", "pt2", "pt3", "pv", "oT", "w0", "w1", "w2", "w3"])
                AC = Timeline(sem("sa_act"), events(["kf", "qh", "ke", "ko", "pe0", "pe1", "pe2", "pe3", "vh", "oh", "vb",
                                                     "ex0", "ex1", "ex2", "ex3"], [(3, "vb", ["wfh"]), (0, "ex3", ["woh"])]), NG,
                              ["pe0", "pe1", "pe2", "pe3", "oh"])
                DV = Timeline(sem("sa_dve"), events(["ql", "kle", "klo", "pl0", "pl1", "vf", "pl2", "pl3",
                                                     "mn0", "mx0", "sb0", "mn1", "mx1", "sb1", "no", "mn2", "mx2", "ol", "mn3",
                                                     "sb2", "mx3", "sb3", "w0", "w1", "vl", "vb", "w2", "w3", "sum", "rc"],
                                                    [(3, "vb", ["wfl", "bc0", "bc1"]), (0, "w3", ["wol"])]), NG,
                              ["pl0", "pl1", "pl2", "pl3", "no", "ol", "w0", "w1", "w2", "w3"])
                freed = {"k": (AC, "kf"), "q": (DV, "ql"), "oT": (DV, "ol"), "v": (DV, "vf"),
                         "w0": (DV, "w0"), "w1": (DV, "w1"), "w2": (DV, "w2"), "w3": (DV, "w3")}
                s_pre_a, s_pre_v, s_zero = sem("sa_pre_a"), sem("sa_pre_v"), sem("sa_zero")
                block = ctx.enter_context(nc.Block())

                def gbank(pe, name, st):
                    n = uses.index(name)
                    prev = uses[n - 2]
                    tl, ev = freed[prev]
                    back = 1 if n < 2 or (st.i is None and prev in ("k", "q", "v")) else 0
                    pe.wait_ge(tl.sem, tl.value(ev, st, back))
                    return bank[n % 2]

                def pair_values(copy, out, v, done):
                    for e in range(2):
                        for b2 in range(2):
                            rows, src = slice(64 * e, 64 * e + 64), slice(64 * b2, 64 * b2 + 64)
                            m = copy(out[rows, b2, :, :, e, :],
                                     v[src, :, :].rearrange("p t (j e d) -> p t j e d", j=4, e=2)[:, :, :, e, :])
                    done(m)

                @block.sync
                def _(sp):
                    def front_weights(g):
                        for n, w in enumerate((wkT, wqT, wvT)):
                            sp.dma_start(raw_f[:, :, n * P:(n + 1) * P],
                                         w.rearrange("(k p) n -> p k n", p=P)[:, :, bass.ds(g * P, P)]).then_inc(s_rf, 16)
                        for n, w in enumerate((bk, bq)):
                            sp.dma_start(rawb[:, n:n + 1], w.rearrange("(p a) -> p a", a=1)[bass.ds(g * P, P), :]).then_inc(s_rf, 16)
                        sp.dma_start(rawb[:, 2:2 + P],
                                     bv.rearrange("(a n) -> a n", a=1)[:, bass.ds(g * P, P)].to_broadcast([P, P])).then_inc(s_rf, 16)
                    sp.dma_start(stage[0][:, :, :], xT.rearrange("(k p) t -> p k t", p=P)[:, :, 0:QT]).then_inc(s_st, 16)
                    front_weights(0)
                    sp.dma_start(par[:, :], parity).then_inc(s_cn, 16)
                    sp.dma_start(caus[:, :], causal).then_inc(s_cn, 16)
                    sp.dma_start(ident[:, :], eye).then_inc(s_cn, 16)
                    sp.dma_start(raw_o, woT[0:P, :]).then_inc(s_ro, 16)
                    sp.wait_ge(s_pre_v, 3)
                    with sp.Fori(0, NG) as i:
                        nxt = (i + 1) % NG
                        front_weights(nxt)
                        sp.wait_ge(DV.sem, DV.value("wol", Step(i, 0)))
                        met(sp)
                        sp.dma_start(raw_o, woT[bass.ds(nxt * P, P), :]).then_inc(s_ro, 16)
                        sp.wait_ge(DV.sem, DV.value("bc1", Step(i, 3)))
                        met(sp)
                    sp.wait_ge(s_ro, 16 * (NG + 1))

                def split_front_hi(act):
                    return act.activation(flat_f[1], flat_f[0], ACT.Copy, scale=WS)

                def split_front_lo(dve):
                    return dve.scalar_tensor_tensor(flat_f[2], flat_f[0], WS, flat_f[1], ALU.mult, ALU.subtract)

                @block.gpsimd
                def _(pool):
                    chain = chained(pool, sem("sa_pool"))
                    pool.memset(eps[:, :], EPS)
                    for z in (sc, vbh, vbl, wo_h, wo_l):
                        pool.memset(z[:], 0.0)
                    chain(pool.memset(rs[:], 0.0))
                    pool.sem_inc(s_zero, 1)
                    s_a, s_bo = sem("sa_acc"), sem("sa_bo")
                    s_stage = [sem(f"sa_stage{n}") for n in range(2)]
                    views = [(xT, xh, xl), (cT, ch, cl)]

                    def load(n):
                        src = views[n // NQ][0].rearrange("(k p) t -> p k t", p=P)
                        q = n % NQ
                        pool.dma_start(stage[n % 2][:, :, :], src[:, :, q * QT:(q + 1) * QT]).then_inc(s_stage[n % 2], 16)

                    def split(n):
                        _, hi, lo = views[n // NQ]
                        tok = slice((n % NQ) * QT, (n % NQ + 1) * QT)
                        pool.wait_ge(s_stage[n % 2], 16 * ((n + 1) // 2))
                        split_on_pool(pool, chain, stage[n % 2][:, :, :], hi[:, :, tok], lo[:, :, tok])
                        pool.sem_inc(s_xq, 1)
                    pool.wait_ge(s_rf, 96)
                    load(1)
                    with nc.sbuf_tensor("bo_rows", [P, D], F32) as bo_rows:
                        pool.dma_start(bo_rows[:, :], bo.rearrange("(a n) -> a n", a=1).to_broadcast([P, D])).then_inc(s_bo, 16)
                        pool.dma_start(acc[:, :, :], x.rearrange("(t p) d -> p t d", p=P)).then_inc(s_a, 16)
                        split(1)
                        pool.wait_ge(s_bo, 16)
                        pool.wait_ge(s_a, 16)
                        chain(pool.tensor_tensor(acc[:, :, :], acc[:, :, :],
                                                 bo_rows[:, :].rearrange("p (a n) -> p a n", a=1).to_broadcast([P, NT, D]),
                                                 ALU.add))
                        pool.sem_inc(s_acc, 1)
                    pool.wait_ge(s_q0l, 1)
                    load(2)
                    for n in range(2, 2 * NQ):
                        if n + 1 < 2 * NQ:
                            load(n + 1)
                        split(n)
                    prefetch_ctx(pool)

                @block.scalar
                def _(act):
                    act.wait_ge(s_st, 16)
                    act.activation(xh[:, :, 0:QT], stage[0][:, :, :], ACT.Copy).then_inc(s_q0h, 1)
                    act.wait_ge(s_rf, 96)
                    split_front_hi(act).then_inc(s_pre_a, 1)
                    AC.start(act)
                    act.wait_ge(s_pre_v, 3)
                    act.wait_ge(s_zero, 1)

                    def back_p(st):
                        for j in J4:
                            act.wait_ge(PE.sem, PE.value(f"pt{j}", st))
                            act.wait_ge(PE.sem, PE.value("pv", st, 1))
                            AC.mark(act.activation(pth[:, j, :, :].rearrange("p a b -> p (a b)"), PTB[j % 2][:, :], ACT.Copy),
                                    f"pe{j}", st)

                    def back_o(st):
                        act.wait_ge(PE.sem, PE.value("oT", st))
                        act.wait_ge(PE.sem, PE.value("w3", st, 1))
                        AC.mark(act.activation(oh[:, :], bank[1][:, :], ACT.Copy), "oh", st)

                    with act.Fori(0, NG) as i:
                        for q in range(NQ):
                            st = Step(i, q)
                            act.wait_ge(PE.sem, PE.value("k", st))
                            act.wait_ge(DV.sem, DV.value("klo", st, 1))
                            if q == 0:
                                act.wait_ge(DV.sem, DV.value("bc1", st, 1))
                            AC.mark(act.activation(kf[:, :], bank[0][:, :], ACT.Identity, bias=bias_c[:, 0:1]), "kf", st)
                            act.wait_ge(PE.sem, PE.value("q", st))
                            act.wait_ge(PE.sem, PE.value("s3", st, 1))
                            AC.mark(act.activation(qh[:, :], bank[1][:, :], ACT.Identity, bias=bias_c[:, 1:2]), "qh", st)
                            act.wait_ge(AC.sem, AC.value("kf", st))
                            for e in range(2):
                                AC.mark(act.activation(kxh[:, e, :], kf[:, :], ACT.Copy, scale=par[:, e:e + 1]),
                                        ("ke", "ko")[e], st)
                            back_p(st)
                            act.wait_ge(DV.sem, DV.value("vf", st))
                            act.wait_ge(DV.sem, DV.value("vb", st, 1))
                            AC.mark(act.activation(vh[:, :, :], vf[:, :, :], ACT.Copy), "vh", st)
                            back_o(st)
                            act.wait_ge(AC.sem, AC.value("vh", st))
                            pair_values(lambda o, v: act.activation(o, v, ACT.Copy), vbh, vh,
                                        lambda m: AC.mark(m, "vb", st))
                            if q == 3:
                                act.wait_ge(s_rf, i * 96 + 192)
                                AC.mark(split_front_hi(act), "wfh", st)
                            for j in J4:
                                act.wait_ge(DV.sem, DV.value(f"sb{j}", st))
                                s2 = sc[:, j, :, :, :].rearrange("p a b c -> p (a b c)")
                                AC.mark(act.activation(s2, s2, ACT.Exp, scale=float(HD1) ** -0.5 / (WS * WS)), f"ex{j}", st)
                            if q == 0:
                                act.wait_ge(s_ro, i * 16 + 16)
                                act.wait_ge(PE.sem, PE.value("w3", st))
                                AC.mark(act.activation(wo_h, raw_o, ACT.Copy, scale=WS), "woh", st)
                    back_p(Step(None, 0))
                    back_o(Step(None, 0))

                @block.vector
                def _(dve):
                    dve.wait_ge(s_q0h, 1)
                    dve.tensor_tensor(xl[:, :, 0:QT], stage[0][:, :, :], xh[:, :, 0:QT], ALU.subtract).then_inc(s_q0l, 1)
                    dve.wait_ge(s_pre_a, 1)
                    split_front_lo(dve).then_inc(s_pre_v, 1)

                    def biases(done0, done1):
                        done0(dve.tensor_scalar(bias_c[:, :], rawb[:, 0:2], WS, None, ALU.mult))
                        done1(dve.tensor_scalar(bv_row[:, :], rawb[:, 2:2 + P], WS, None, ALU.mult))
                    dve.wait_ge(s_rf, 96)
                    biases(lambda m: m.then_inc(s_pre_v, 1), lambda m: m.then_inc(s_pre_v, 1))
                    dve.wait_ge(s_pre_v, 3)
                    dve.wait_ge(s_cn, 48)
                    dve.wait_ge(s_zero, 1)
                    DV.start(dve)

                    def back_lo(st, j):
                        dve.wait_ge(AC.sem, AC.value(f"pe{j}", st))
                        h2 = pth[:, j, :, :].rearrange("p a b -> p (a b)")
                        DV.mark(dve.tensor_tensor(ptl[:, j, :, :].rearrange("p a b -> p (a b)"), PTB[j % 2][:, :], h2,
                                                  ALU.subtract), f"pl{j}", st)

                    def back_norm(st):
                        dve.wait_ge(PE.sem, PE.value("pv", st))
                        dve.wait_ge(DV.sem, DV.value("rc", st, 1))
                        dve.wait_ge(PE.sem, PE.value("oT", st, 1))
                        DV.mark(dve.tensor_tensor(at[:, :, :].rearrange("p t (g d) -> p t g d", d=HD1),
                                                  PVB[:, :].rearrange("p (t g d) -> p t g d", t=TQ, d=HD1),
                                                  rs[:, :, :, :].to_broadcast([P, TQ, HG, HD1]),
                                                  ALU.mult), "no", st)

                    def back_out_lo(st):
                        dve.wait_ge(AC.sem, AC.value("oh", st))
                        DV.mark(dve.tensor_tensor(ol[:, :], bank[1][:, :], oh[:, :], ALU.subtract), "ol", st)

                    def back_add(st, tiles):
                        dve.wait_ge(s_acc, 1)
                        for t in tiles:
                            dve.wait_ge(PE.sem, PE.value(f"w{t}", st))
                            row = acc[:, t + TQ * ((st.q - 1) % NQ if st.i is not None else NQ - 1), :]
                            DV.mark(dve.scalar_tensor_tensor(row, bank[t % 2][:, :], 1 / (WS * WS), row, ALU.mult, ALU.add),
                                    f"w{t}", st)

                    def smax(st, j, part):
                        s3 = sc[:, j, :, :, :].rearrange("p a b c -> p (a b) c")
                        if part == "mn":
                            dve.wait_ge(PE.sem, PE.value(f"s{j}", st))
                            DV.mark(dve.tensor_tensor(s3, SB[j % 2][:, :].rearrange("p (a c) -> p a c", a=8),
                                                      caus[:, :].rearrange("p (a c) -> p a c", a=1).to_broadcast([P, 8, S]),
                                                      ALU.min), f"mn{j}", st)
                        elif part == "mx":
                            dve.wait_ge(DV.sem, DV.value(f"mn{j}", st))
                            DV.mark(dve.tensor_reduce(mx[:, j, :], s3, AX.X, ALU.max), f"mx{j}", st)
                        else:
                            dve.wait_ge(DV.sem, DV.value(f"mx{j}", st))
                            DV.mark(dve.tensor_tensor(s3, s3, mx[:, j, :].rearrange("p (a c) -> p a c", c=1)
                                                      .to_broadcast([P, 8, S]), ALU.subtract), f"sb{j}", st)

                    with dve.Fori(0, NG) as i:
                        for q in range(NQ):
                            st = Step(i, q)
                            dve.wait_ge(AC.sem, AC.value("qh", st))
                            DV.mark(dve.scalar_tensor_tensor(ql[:, :], bank[1][:, :], bias_c[:, 1:2], qh[:, :], ALU.add,
                                                             ALU.subtract), "ql", st)
                            for e in range(2):
                                dve.wait_ge(AC.sem, AC.value(("ke", "ko")[e], st))
                                DV.mark(dve.scalar_tensor_tensor(kxl[:, e, :], kf[:, :], par[:, e:e + 1], kxh[:, e, :], ALU.mult,
                                                                 ALU.subtract), ("kle", "klo")[e], st)
                            back_lo(st, 0)
                            back_lo(st, 1)
                            dve.wait_ge(PE.sem, PE.value("v", st))
                            DV.mark(dve.tensor_tensor(vf[:, :, :], bank[0][:, :].rearrange("p (t n) -> p t n", t=TQ),
                                                      bv_row[:, :].rearrange("p (a n) -> p a n", a=1).to_broadcast([P, TQ, P]),
                                                      ALU.add), "vf", st)
                            back_lo(st, 2)
                            back_lo(st, 3)
                            for j in range(2):
                                for part in ("mn", "mx", "sb"):
                                    smax(st, j, part)
                            back_norm(st)
                            smax(st, 2, "mn")
                            smax(st, 2, "mx")
                            back_out_lo(st)
                            smax(st, 3, "mn")
                            smax(st, 2, "sb")
                            smax(st, 3, "mx")
                            smax(st, 3, "sb")
                            back_add(st, (0, 1))
                            dve.wait_ge(AC.sem, AC.value("vh", st))
                            DV.mark(dve.tensor_tensor(vl[:, :, :], vf[:, :, :], vh[:, :, :], ALU.subtract), "vl", st)
                            dve.wait_ge(DV.sem, DV.value("vl", st))
                            pair_values(lambda o, v: dve.tensor_copy(o, v), vbl, vl, lambda m: DV.mark(m, "vb", st))
                            if q == 3:
                                dve.wait_ge(AC.sem, AC.value("wfh", st))
                                DV.mark(split_front_lo(dve), "wfl", st)
                                dve.wait_ge(DV.sem, DV.value("vf", st))
                                biases(lambda m: DV.mark(m, "bc0", st), lambda m: DV.mark(m, "bc1", st))
                            back_add(st, (2, 3))
                            if q == 0:
                                dve.wait_ge(AC.sem, AC.value("woh", st))
                                DV.mark(dve.scalar_tensor_tensor(wo_l, raw_o, WS, wo_h, ALU.mult, ALU.subtract), "wol", st)
                            dve.wait_ge(AC.sem, AC.value("ex3", st))
                            DV.mark(dve.tensor_reduce(sm[:, :, :], sc[:, :, :, :, :].rearrange("p j a b c -> p j (a b) c"), AX.X,
                                                      ALU.add), "sum", st)
                            dve.wait_ge(DV.sem, DV.value("sum", st))
                            DV.mark(dve.reciprocal(rs[:, :, :, 0].rearrange("p t (j e) -> p t j e", e=2),
                                                   sm[:, :, :].rearrange("p j (t e) -> p t j e", e=2)), "rc", st)
                    st = Step(None, 0)
                    for j in J4:
                        back_lo(st, j)
                    back_norm(st)
                    back_out_lo(st)
                    back_add(st, range(TQ))

                @block.tensor
                def _(pe):
                    PE.start(pe)
                    pe.wait_ge(s_q0l, 1)
                    pe.wait_ge(s_zero, 1)
                    pe.wait_ge(s_cn, 48)
                    pe.wait_ge(s_pre_v, 3)

                    def feature_major(name, st, col):
                        o = gbank(pe, name, st)
                        tok = slice(st.q * QT, (st.q + 1) * QT)
                        PE.mark(three_pass(pe, o[:, :], [(wf_h[:, k, col:col + P], wf_l[:, k, col:col + P], xh[:, k, tok],
                                                          xl[:, k, tok]) for k in range(KD)]), name, st)

                    def back_p(st, js):
                        for j in js:
                            if j == 0:
                                pe.wait_ge(AC.sem, AC.value("ex3", st, 1))
                            if j < 2:
                                pe.wait_ge(DV.sem, DV.value(f"pl{j + 2}", st, 1))
                            else:
                                pe.wait_ge(DV.sem, DV.value(f"pl{j - 2}", st))
                            for t in range(TQ):
                                mm = pe.transpose(PTB[j % 2][:, t * P:(t + 1) * P],
                                                  sc[:, j, t, :, :].rearrange("p e k -> p (e k)"), ident[:, :])
                            PE.mark(mm, f"pt{j}", st)

                    def back_pv(st):
                        pe.wait_ge(AC.sem, AC.value("vb", st, 1))
                        pe.wait_ge(DV.sem, DV.value("no", st, 1))
                        pe.wait_ge(DV.sem, DV.value("pl3", st))
                        for t in range(TQ):
                            for b2 in range(2):
                                qs = slice(64 * b2, 64 * b2 + 64)
                                for j in J4:
                                    pair = "p e d -> p (e d)"
                                    mm = three_pass(pe, PVB[qs, (4 * t + j) * 2 * HD1:(4 * t + j + 1) * 2 * HD1],
                                                    [(pth[:, j, t, qs], ptl[:, j, t, qs], vbh[:, b2, t, j, :, :].rearrange(pair),
                                                      vbl[:, b2, t, j, :, :].rearrange(pair))])
                        PE.mark(mm, "pv", st)

                    def back_turn(st):
                        o = gbank(pe, "oT", st)
                        pe.wait_ge(DV.sem, DV.value("no", st))
                        for t in range(TQ):
                            mm = pe.transpose(o[:, t * P:(t + 1) * P], at[:, t, :], ident[:, :])
                        PE.mark(mm, "oT", st)

                    def back_out(st):
                        pe.wait_ge(DV.sem, DV.value("ol", st))
                        if st.q == 1:
                            pe.wait_ge(DV.sem, DV.value("wol", st, 1))
                        for t in range(TQ):
                            o = gbank(pe, f"w{t}", st)
                            tok = slice(t * P, (t + 1) * P)
                            PE.mark(three_pass(pe, o[:, :], [(oh[:, tok], ol[:, tok], wo_h, wo_l)]), f"w{t}", st)

                    def scores(st, js):
                        for j in js:
                            if j < 2:
                                pe.wait_ge(DV.sem, DV.value(f"mn{j + 2}", st, 1))
                            else:
                                pe.wait_ge(DV.sem, DV.value(f"mn{j - 2}", st))
                            r = slice(32 * j, 32 * j + 32)
                            for t in range(TQ):
                                for b2 in range(2):
                                    tok = slice(t * P + b2 * 64, t * P + b2 * 64 + 64)
                                    mm = three_pass(pe, SB[j % 2][64 * b2:64 * b2 + 64, t * P:(t + 1) * P],
                                                    [(qh[r, tok], ql[r, tok], kxh[r, :, tok], kxl[r, :, tok])])
                            PE.mark(mm, f"s{j}", st)

                    with pe.Fori(0, NG) as i:
                        for q in range(NQ):
                            st = Step(i, q)
                            if q == 0:
                                pe.wait_ge(DV.sem, DV.value("wfl", st, 1))
                            else:
                                pe.wait_ge(s_xq, q)
                            feature_major("k", st, 0)
                            feature_major("q", st, P)
                            back_p(st, (0, 1))
                            o = gbank(pe, "v", st)
                            for t in range(TQ):
                                tok = slice(q * QT + t * P, q * QT + (t + 1) * P)
                                mm = three_pass(pe, o[:, t * P:(t + 1) * P],
                                                [(xh[:, k, tok], xl[:, k, tok], wf_h[:, k, 2 * P:3 * P], wf_l[:, k, 2 * P:3 * P])
                                                 for k in range(KD)])
                            PE.mark(mm, "v", st)
                            back_p(st, (2, 3))
                            pe.wait_ge(DV.sem, DV.value("klo", st))
                            scores(st, (0, 1))
                            back_pv(st)
                            scores(st, (2,))
                            back_turn(st)
                            scores(st, (3,))
                            back_out(st)
                    st = Step(None, 0)
                    back_p(st, J4)
                    back_pv(st)
                    back_turn(st)
                    back_out(st)

        def cross_attention():
            NG = HKV
            FW = GQ * HD2 + 2 * HD2
            with ExitStack() as ctx:
                def b(name, shape, dt=F32):
                    return sb("xa_" + name, shape, dt, ctx)
                raw_f, wf_h, wf_l = (blocks(z, KD)(FW) for z in (raw_front, front_h, front_l))
                flat_f = [z[:, 0:KD * FW] for z in (raw_front, front_h, front_l)]
                raw_o, wo_h, wo_l = (blocks(z, GQ)(D) for z in (raw_out, out_h, out_l))
                cs, sn = b("cs", [P, S]), b("sn", [P, S])
                NR = 1 + GQ
                x0 = [b(f"x0_{r}", [P, QT]) for r in range(NR)]
                xs = [b(f"xs_{r}", [P, QT]) for r in range(NR)]
                rr = [b(f"rr_{r}", [P, QT]) for r in range(2)]
                rkh, rkl = b("rkh", [P, 2 * TQ, S], F16), b("rkl", [P, 2 * TQ, S], F16)
                rqh, rql = (b(n, [P, GQ // 2, 2 * TQ, 2, S], F16) for n in ("rqh", "rql"))
                sc = b("sc", [P, 2, TQ, 2, S])
                mx, sm, rs = b("mx", [P, 2, 8]), b("sm", [P, 2, 8]), b("rs", [P, 2, 8])
                vh, vl = b("vh", [P, TQ, P], F16), b("vl", [P, TQ, P], F16)
                pth, ptl = b("pth", [P, 2, TQ, P], F16), b("ptl", [P, 2, TQ, P], F16)
                oh, ol = b("oh", [P, GQ, QT], F16), b("ol", [P, GQ, QT], F16)
                s_rf, s_ro, s_cn = sem("xa_s_rf"), sem("xa_s_ro"), sem("xa_s_cn")
                SB, PTB, PVB = [bank[2], bank[3]], [bank[4], bank[5]], [bank[6], bank[7]]
                names = [f"r{r}" for r in range(NR)]
                uses = names + ["v", "w0", "w1", "w2", "w3"]
                PE = Timeline(sem("xa_pe"), events(names + ["pt0", "pt1", "v", "pv0", "pv1", "s0", "pv2", "pv3", "s1",
                                                            "w0", "w1", "w2", "w3"]), NG,
                              ["pt0", "pt1", "pv0", "pv1", "pv2", "pv3", "w0", "w1", "w2", "w3"])
                act_order, rope_order = [], []
                for r in range(NR):
                    act_order += [f"r{r}"] + ([f"h{r - 2}"] if r >= 2 else [])
                    rope_order += [f"cm{r}"] + ([f"ra{r - 1}"] if r >= 1 else []) + ([f"l{r - 2}"] if r >= 2 else [])
                AC = Timeline(sem("xa_act"), events(act_order + ["pe0", "pe1", f"h{NR - 2}", f"h{NR - 1}", "hi0", "hi1", "hi2", "hi3",
                                                                 "vh", "ex0", "ex1"],
                                                    [(3, "vh", ["wfh"]), (0, "ex1", ["woh"])]), NG,
                              ["pe0", "pe1", "hi0", "hi1", "hi2", "hi3"])
                DV = Timeline(sem("xa_dve"), events(rope_order + ["pl0", "pl1", f"l{NR - 2}", f"ra{NR - 1}", f"l{NR - 1}",
                                                                  "lo0", "lo1", "mn0", "lo2", "lo3", "vl", "mn1", "mx0",
                                                                  "sb0", "mx1", "sb1", "w0", "w1", "w2", "w3", "sum", "rc"],
                                                    [(3, "sb1", ["wfl"]), (0, "w3", ["wol"])]), NG,
                              ["pl0", "pl1", "lo0", "lo1", "lo2", "lo3", "w0", "w1", "w2", "w3"])
                PO = Timeline(sem("xa_pool"), events([f"sm{r}" for r in range(NR)] + ["nm"]), NG)
                freed = {n: (AC, n) for n in names}
                freed["v"] = (DV, "vl")
                freed.update({f"w{t}": (DV, f"w{t}") for t in range(TQ)})
                block = ctx.enter_context(nc.Block())

                def heads(o, tp, b2):
                    return o[:, :, :].rearrange("p h (t b s) -> p t b h s", t=TQ, b=2)[:, 2 * tp:2 * tp + 2, b2, :, :]

                def rotated(keys, queries, r):
                    return keys[:, :, :] if r == 0 else queries[:, (r - 1) // 2, :, (r - 1) % 2, :]

                def gbank(pe, name, st):
                    n = uses.index(name)
                    prev = uses[n - 2]
                    tl, ev = freed[prev]
                    back = 1 if n < 2 or (st.i is None and not prev.startswith("w")) else 0
                    pe.wait_ge(tl.sem, tl.value(ev, st, back))
                    return bank[n % 2]

                @block.sync
                def _(sp):
                    def front_weights(g):
                        c = 0
                        for w, n in ((xwq, GQ * HD2), (xwk, HD2), (xwv, HD2)):
                            sp.dma_start(raw_f[:, :, c:c + n],
                                         w.rearrange("(k p) n -> p k n", p=P)[:, :, bass.ds(g * n, n)]).then_inc(s_rf, 16)
                            c += n

                    def out_weights(g):
                        sp.dma_start(raw_o[:, :, :], xwo[bass.ds(g * GQ * HD2, GQ * HD2), :]
                                     .rearrange("(h p) n -> p h n", p=P)).then_inc(s_ro, 16)
                    sp.dma_start(cs[:, :], cosT).then_inc(s_cn, 16)
                    sp.dma_start(sn[:, :], sinT).then_inc(s_cn, 16)
                    out_weights(0)
                    with sp.Fori(0, NG) as i:
                        nxt = (i + 1) % NG
                        front_weights(nxt)
                        sp.wait_ge(DV.sem, DV.value("wol", Step(i, 0)))
                        met(sp)
                        out_weights(nxt)
                        sp.wait_ge(DV.sem, DV.value("wfl", Step(i, 3)))
                        met(sp)
                    sp.wait_ge(s_ro, 16 * (NG + 1))

                def split_front_hi(act):
                    return act.activation(flat_f[1], flat_f[0], ACT.Copy, scale=WS)

                def split_front_lo(dve):
                    return dve.scalar_tensor_tensor(flat_f[2], flat_f[0], WS, flat_f[1], ALU.mult, ALU.subtract)

                @block.gpsimd
                def _(pool):
                    s_zero = sem("xa_zero")
                    for z in (sc, vh):
                        pool.memset(z[:], 0.0)
                    pool.memset(vl[:], 0.0).then_inc(s_zero, 1)
                    pool.wait_ge(s_zero, 1)
                    pool.wait_ge(s_cn, 32)
                    PO.start(pool)
                    with pool.Fori(0, NG) as i:
                        for q in range(NQ):
                            st = Step(i, q)
                            for r in range(NR):
                                pool.wait_ge(AC.sem, AC.value(f"r{r}", st))
                                xr = xs[r][:, :].rearrange("p (a s) -> p a s", s=S)
                                PO.mark(pool.tensor_tensor(xr, xr, sn[:, :].rearrange("p (a s) -> p a s", a=1)
                                                           .to_broadcast([P, QT // S, S]), ALU.mult), f"sm{r}", st)
                            pool.wait_ge(DV.sem, DV.value("rc", st))
                            s4 = sc[:, :, :, :, :].rearrange("p h t b k -> p (h t b) k")
                            PO.mark(pool.tensor_tensor(s4, s4, rs[:, :, :].rearrange("p h (t a) -> p (h t) a", a=1)
                                                       .to_broadcast([P, 16, S]), ALU.mult), "nm", st)

                @block.scalar
                def _(act):
                    AC.start(act)

                    def back_p(st):
                        for h in range(2):
                            act.wait_ge(PE.sem, PE.value(f"pt{h}", st))
                            act.wait_ge(PE.sem, PE.value("pv3", st, 1))
                            AC.mark(act.activation(pth[:, h, :, :].rearrange("p a b -> p (a b)"), PTB[h][:, :], ACT.Copy, scale=OS),
                                    f"pe{h}", st)

                    def back_o(st):
                        for c in range(4):
                            tp, b2 = c // 2, c % 2
                            act.wait_ge(PE.sem, PE.value(f"pv{c}", st))
                            act.wait_ge(PE.sem, PE.value("w3", st, 1))
                            AC.mark(act.activation(heads(oh, tp, b2), PVB[b2][:, :].rearrange("p (t h s) -> p t h s", t=2, h=GQ),
                                                   ACT.Copy), f"hi{c}", st)

                    def copies(st, r):
                        act.wait_ge(PE.sem, PE.value(f"r{r}", st))
                        if r == 0:
                            act.wait_ge(DV.sem, DV.value(f"ra{NR - 1}", st, 1))
                        src = bank[r % 2]
                        act.activation(x0[r][:, :], src[:, :], ACT.Copy)
                        act.activation(xs[r][0:64, :], src[64:128, :], ACT.Copy)
                        AC.mark(act.activation(xs[r][64:128, :], src[0:64, :], ACT.Copy), f"r{r}", st)

                    def rotated_hi(st, r):
                        act.wait_ge(DV.sem, DV.value(f"ra{r}", st))
                        if r == 0:
                            act.wait_ge(PE.sem, PE.value("s1", st, 1))
                        AC.mark(act.activation(rotated(rkh, rqh, r), rr[r % 2][:, :].rearrange("p (a s) -> p a s", s=S),
                                               ACT.Copy), f"h{r}", st)

                    with act.Fori(0, NG) as i:
                        for q in range(NQ):
                            st = Step(i, q)
                            for r in range(NR):
                                copies(st, r)
                                if r >= 2:
                                    rotated_hi(st, r - 2)
                            back_p(st)
                            rotated_hi(st, NR - 2)
                            rotated_hi(st, NR - 1)
                            back_o(st)
                            act.wait_ge(PE.sem, PE.value("pv3", st))
                            AC.mark(act.activation(vh[:, :, :].rearrange("p t n -> p (t n)"), bank[uses.index("v") % 2][:, :],
                                                   ACT.Copy, scale=1 / WS), "vh", st)
                            if q == 3:
                                act.wait_ge(s_rf, i * 48 + 48)
                                AC.mark(split_front_hi(act), "wfh", st)
                            for h in range(2):
                                act.wait_ge(DV.sem, DV.value(f"sb{h}", st))
                                s2 = sc[:, h, :, :, :].rearrange("p a b c -> p (a b c)")
                                AC.mark(act.activation(s2, s2, ACT.Exp, scale=float(HD2) ** -0.5), f"ex{h}", st)
                            if q == 0:
                                act.wait_ge(s_ro, i * 16 + 16)
                                act.wait_ge(PE.sem, PE.value("w3", st))
                                AC.mark(act.activation(wo_h[:, :, :], raw_o[:, :, :], ACT.Copy, scale=WS), "woh", st)
                    back_p(Step(None, 0))
                    back_o(Step(None, 0))

                @block.vector
                def _(dve):
                    dve.wait_ge(s_cn, 32)
                    DV.start(dve)

                    def back_p_lo(st):
                        for h in range(2):
                            dve.wait_ge(AC.sem, AC.value(f"pe{h}", st))
                            DV.mark(dve.scalar_tensor_tensor(ptl[:, h, :, :].rearrange("p a b -> p (a b)"), PTB[h][:, :], OS,
                                                             pth[:, h, :, :].rearrange("p a b -> p (a b)"), ALU.mult,
                                                             ALU.subtract), f"pl{h}", st)

                    def back_lo(st, cs):
                        for c in cs:
                            tp, b2 = c // 2, c % 2
                            dve.wait_ge(AC.sem, AC.value(f"hi{c}", st))
                            DV.mark(dve.tensor_tensor(heads(ol, tp, b2), PVB[b2][:, :].rearrange("p (t h s) -> p t h s", t=2, h=GQ),
                                                      heads(oh, tp, b2), ALU.subtract), f"lo{c}", st)

                    def back_add(st):
                        for t in range(TQ):
                            dve.wait_ge(PE.sem, PE.value(f"w{t}", st))
                            row = acc[:, t + TQ * ((st.q - 1) % NQ if st.i is not None else NQ - 1), :]
                            DV.mark(dve.scalar_tensor_tensor(row, bank[uses.index(f"w{t}") % 2][:, :], 1 / (WS * OS), row,
                                                             ALU.mult, ALU.add), f"w{t}", st)

                    def cosine(st, r):
                        dve.wait_ge(AC.sem, AC.value(f"r{r}", st))
                        xr = x0[r][:, :].rearrange("p (a s) -> p a s", s=S)
                        DV.mark(dve.tensor_tensor(xr, xr, cs[:, :].rearrange("p (a s) -> p a s", a=1)
                                                  .to_broadcast([P, QT // S, S]), ALU.mult), f"cm{r}", st)

                    def rotate(st, r):
                        dve.wait_ge(PO.sem, PO.value(f"sm{r}", st))
                        dve.wait_ge(DV.sem, DV.value(f"cm{r}", st))
                        dve.wait_ge(DV.sem, DV.value(f"l{r - 2}", st) if r >= 2 else DV.value(f"l{NR - 1}", st, 1))
                        DV.mark(dve.tensor_tensor(rr[r % 2][:, :], x0[r][:, :], xs[r][:, :], ALU.add), f"ra{r}", st)

                    def rotated_lo(st, r):
                        dve.wait_ge(AC.sem, AC.value(f"h{r}", st))
                        DV.mark(dve.tensor_tensor(rotated(rkl, rql, r), rr[r % 2][:, :].rearrange("p (a s) -> p a s", s=S),
                                                  rotated(rkh, rqh, r), ALU.subtract), f"l{r}", st)

                    def smax(st, h, part):
                        s3 = sc[:, h, :, :, :].rearrange("p a b c -> p (a b) c")
                        if part == "mn":
                            bnd = bound[:, 2 * TQ * st.q:2 * TQ * (st.q + 1), :]
                            dve.wait_ge(PE.sem, PE.value(f"s{h}", st))
                            DV.mark(dve.tensor_tensor(s3, SB[h][:, :].rearrange("p (a c) -> p a c", a=8), bnd, ALU.min),
                                    f"mn{h}", st)
                        elif part == "mx":
                            dve.wait_ge(DV.sem, DV.value(f"mn{h}", st))
                            DV.mark(dve.tensor_reduce(mx[:, h, :], s3, AX.X, ALU.max), f"mx{h}", st)
                        else:
                            dve.wait_ge(DV.sem, DV.value(f"mx{h}", st))
                            DV.mark(dve.tensor_tensor(s3, s3, mx[:, h, :].rearrange("p (a c) -> p a c", c=1)
                                                      .to_broadcast([P, 8, S]), ALU.subtract), f"sb{h}", st)

                    with dve.Fori(0, NG) as i:
                        for q in range(NQ):
                            st = Step(i, q)
                            for r in range(NR):
                                cosine(st, r)
                                if r >= 1:
                                    rotate(st, r - 1)
                                if r >= 2:
                                    rotated_lo(st, r - 2)
                            back_p_lo(st)
                            rotated_lo(st, NR - 2)
                            rotate(st, NR - 1)
                            rotated_lo(st, NR - 1)
                            back_lo(st, (0, 1))
                            smax(st, 0, "mn")
                            back_lo(st, (2, 3))
                            dve.wait_ge(AC.sem, AC.value("vh", st))
                            DV.mark(dve.scalar_tensor_tensor(vl[:, :, :].rearrange("p t n -> p (t n)"),
                                                             bank[uses.index("v") % 2][:, :], 1 / WS,
                                                             vh[:, :, :].rearrange("p t n -> p (t n)"), ALU.mult, ALU.subtract),
                                    "vl", st)
                            smax(st, 1, "mn")
                            for h in range(2):
                                smax(st, h, "mx")
                                smax(st, h, "sb")
                            if q == 3:
                                dve.wait_ge(AC.sem, AC.value("wfh", st))
                                DV.mark(split_front_lo(dve), "wfl", st)
                            back_add(st)
                            if q == 0:
                                dve.wait_ge(AC.sem, AC.value("woh", st))
                                DV.mark(dve.scalar_tensor_tensor(wo_l[:, :, :].rearrange("p a b -> p (a b)"),
                                                                 raw_o[:, :, :].rearrange("p a b -> p (a b)"), WS,
                                                                 wo_h[:, :, :].rearrange("p a b -> p (a b)"),
                                                                 ALU.mult, ALU.subtract), "wol", st)
                            dve.wait_ge(AC.sem, AC.value("ex1", st))
                            DV.mark(dve.tensor_reduce(sm[:, :, :], sc[:, :, :, :, :].rearrange("p h t b k -> p h (t b) k"), AX.X,
                                                      ALU.add), "sum", st)
                            dve.wait_ge(DV.sem, DV.value("sum", st))
                            DV.mark(dve.reciprocal(rs[:, :, :], sm[:, :, :]), "rc", st)
                    st = Step(None, 0)
                    back_p_lo(st)
                    back_lo(st, range(4))
                    back_add(st)

                @block.tensor
                def _(pe):
                    PE.start(pe)

                    def back_p(st):
                        pe.wait_ge(PO.sem, PO.value("nm", st, 1))
                        for h in range(2):
                            pe.wait_ge(DV.sem, DV.value(f"pl{h}", st, 1))
                            for t in range(TQ):
                                mm = pe.transpose(PTB[h][:, t * P:(t + 1) * P],
                                                  sc[:, h, t, :, :].rearrange("p b k -> p (b k)"), ident[:, :])
                            PE.mark(mm, f"pt{h}", st)

                    def back_pv(st, cs):
                        pe.wait_ge(DV.sem, DV.value("pl1", st))
                        pe.wait_ge(DV.sem, DV.value("vl", st, 1))
                        for c in cs:
                            tp, b2 = c // 2, c % 2
                            if c < 2:
                                pe.wait_ge(DV.sem, DV.value(f"lo{c + 2}", st, 1))
                            else:
                                pe.wait_ge(DV.sem, DV.value(f"lo{c - 2}", st))
                            rows = slice(64 * b2, 64 * b2 + 64)
                            for t2 in range(2):
                                t = 2 * tp + t2
                                mm = three_pass(pe, PVB[b2][:, t2 * 256:(t2 + 1) * 256],
                                                [(vh[rows, t, :], vl[rows, t, :], pth[rows, :, t, :], ptl[rows, :, t, :])])
                            PE.mark(mm, f"pv{c}", st)

                    def back_out(st):
                        pe.wait_ge(DV.sem, DV.value("lo3", st))
                        if st.q == 1:
                            pe.wait_ge(DV.sem, DV.value("wol", st, 1))
                        for t in range(TQ):
                            o = gbank(pe, f"w{t}", st)
                            tok = slice(t * P, (t + 1) * P)
                            PE.mark(three_pass(pe, o[:, :], [(oh[:, h, tok], ol[:, h, tok], wo_h[:, h, :], wo_l[:, h, :])
                                                             for h in range(GQ)]), f"w{t}", st)

                    def scores(st, h):
                        pe.wait_ge(DV.sem, DV.value(f"mn{h}", st, 1))
                        pe.wait_ge(DV.sem, DV.value(f"l{NR - 1}", st))
                        for bb in range(2 * TQ):
                            pair = "p a s -> p (a s)"
                            mm = three_pass(pe, SB[h][:, 64 * bb:64 * bb + 64],
                                            [(rqh[:, h, bb, :, :].rearrange(pair), rql[:, h, bb, :, :].rearrange(pair),
                                              rkh[:, bb, :], rkl[:, bb, :])])
                        PE.mark(mm, f"s{h}", st)

                    with pe.Fori(0, NG) as i:
                        for q in range(NQ):
                            st = Step(i, q)
                            if q == 0:
                                pe.wait_ge(DV.sem, DV.value("wfl", st, 1))
                            tok = slice(q * QT, (q + 1) * QT)
                            for r in range(NR):
                                o = gbank(pe, f"r{r}", st)
                                c = GQ * HD2 if r == 0 else (r - 1) * HD2
                                ah, al = (ch, cl) if r == 0 else (xh, xl)
                                PE.mark(three_pass(pe, o[:, :], [(wf_h[:, k, c:c + P], wf_l[:, k, c:c + P], ah[:, k, tok],
                                                                  al[:, k, tok]) for k in range(KD)]), f"r{r}", st)
                            back_p(st)
                            o = gbank(pe, "v", st)
                            c = (GQ + 1) * HD2
                            for t in range(TQ):
                                tk = slice(q * QT + t * P, q * QT + (t + 1) * P)
                                mm = three_pass(pe, o[:, t * P:(t + 1) * P],
                                                [(ch[:, k, tk], cl[:, k, tk], wf_h[:, k, c:c + P], wf_l[:, k, c:c + P])
                                                 for k in range(KD)])
                            PE.mark(mm, "v", st)
                            back_pv(st, (0, 1))
                            scores(st, 0)
                            back_pv(st, (2, 3))
                            scores(st, 1)
                            back_out(st)
                    st = Step(None, 0)
                    back_p(st)
                    back_pv(st, range(4))
                    back_out(st)

        cw = sb("cw", [P, NT, NE + 1])

        def router():
            with ExitStack() as ctx:
                def b(name, shape, dt=F32):
                    return sb("ro_" + name, shape, dt, ctx)
                raw, gh, gl = b("raw", [P, KD, NE]), b("gh", [P, KD, NE], F16), b("gl", [P, KD, NE], F16)
                bi, io = b("bi", [P, NE]), b("io", [P, NE])
                sg = b("sg", [P, NT, NE])
                top8, idx, idf = b("top8", [P, NT, 8]), b("idx", [P, NT, 8], U32), b("idf", [P, NT, 8])
                tot, rt, w4 = b("tot", [P, NT]), b("rt", [P, NT]), b("w4", [P, NT, TOPK])
                one, hit = b("one", [P, NT, NE]), b("hit", [P, NT, NE])
                s_in, s_g, s_mm, s_a, s_v = sem("ro_in"), sem("ro_g"), sem("ro_mm"), sem("ro_a"), sem("ro_v")
                block = ctx.enter_context(nc.Block())

                @block.sync
                def _(sp):
                    sp.dma_start(raw[:, :, :], gwT.rearrange("(k p) n -> p k n", p=P)).then_inc(s_in, 16)
                    sp.dma_start(bi[:, :], gbias.rearrange("(a n) -> a n", a=1).to_broadcast([P, NE])).then_inc(s_in, 16)
                    sp.dma_start(io[:, :], iota).then_inc(s_in, 16)

                @block.tensor
                def _(pe):
                    pe.wait_ge(s_g, 2)
                    for t in range(NT):
                        tok = slice(t * P, (t + 1) * P)
                        mm = three_pass(pe, bank[0][:, t * NE:(t + 1) * NE],
                                        [(xh[:, k, tok], xl[:, k, tok], gh[:, k, :], gl[:, k, :]) for k in range(KD)])
                    mm.then_inc(s_mm, 1)

                @block.scalar
                def _(act):
                    act.wait_ge(s_mm, 1)
                    act.activation(sg[:, :, :].rearrange("p t e -> p (t e)"), bank[0][:, 0:NT * NE], ACT.Exp,
                                   scale=-1 / WS).then_inc(s_a, 1)

                @block.vector
                def _(dve):
                    n = [0]

                    def then(m):
                        n[0] += 1
                        m.then_inc(s_v, 1)
                        dve.wait_ge(s_v, n[0])
                    dve.wait_ge(s_in, 48)
                    dve.tensor_scalar(gh[:, :, :], raw[:, :, :], WS, None, ALU.mult).then_inc(s_g, 1)
                    dve.wait_ge(s_g, 1)
                    dve.scalar_tensor_tensor(gl[:, :, :].rearrange("p k n -> p (k n)"), raw[:, :, :].rearrange("p k n -> p (k n)"), WS,
                                             gh[:, :, :].rearrange("p k n -> p (k n)"), ALU.mult, ALU.subtract).then_inc(s_g, 1)
                    dve.wait_ge(s_a, 1)
                    then(dve.tensor_scalar(sg[:, :, :], sg[:, :, :], 1.0, None, ALU.add))
                    then(dve.reciprocal(sg[:, :, :], sg[:, :, :]))
                    then(dve.tensor_tensor(sg[:, :, :], sg[:, :, :], bi[:, :].rearrange("p (a e) -> p a e", a=1)
                                           .to_broadcast([P, NT, NE]), ALU.add))
                    for t in range(NT):
                        m = dve.max(top8[:, t, :], sg[:, t, :])
                    then(m)
                    for t in range(NT):
                        m = dve.max_index(idx[:, t, :], top8[:, t, :], sg[:, t, :])
                    dve.tensor_reduce(tot[:, :], top8[:, :, 0:TOPK], AX.X, ALU.add)
                    then(m2 := dve.memset(cw[:, :, :], 0.0))
                    dve.tensor_copy(idf[:, :, :], idx[:, :, :])
                    then(dve.tensor_scalar(tot[:, :], tot[:, :], 1e-20, None, ALU.add))
                    then(dve.reciprocal(rt[:, :], tot[:, :]))
                    dve.memset(cw[:, :, NE:NE + 1], 1.0)
                    then(dve.tensor_tensor(w4[:, :, :], top8[:, :, 0:TOPK], rt[:, :].rearrange("p (t a) -> p t a", a=1)
                                           .to_broadcast([P, NT, TOPK]), ALU.mult))
                    for j in range(TOPK):
                        then(dve.tensor_tensor(one[:, :, :], io[:, :].rearrange("p (a e) -> p a e", a=1).to_broadcast([P, NT, NE]),
                                               idf[:, :, j:j + 1].to_broadcast([P, NT, NE]), ALU.is_equal))
                        then(dve.tensor_tensor(hit[:, :, :], one[:, :, :], w4[:, :, j:j + 1].to_broadcast([P, NT, NE]), ALU.mult))
                        then(dve.tensor_tensor(cw[:, :, 0:NE], cw[:, :, 0:NE], hit[:, :, :], ALU.add))
                    then(dve.tensor_scalar(cw[:, :, :], cw[:, :, :], 1 / (WS * OS), None, ALU.mult))

        def experts():
            NG = NE + 1
            with ExitStack() as ctx:
                def b(name, shape, dt=F32):
                    return sb("mo_" + name, shape, dt, ctx)
                raw_f, wf_h, wf_l = (blocks(z, KD)(2 * FI) for z in (raw_front, front_h, front_l))
                flat_f = [z[:, 0:KD * 2 * FI] for z in (raw_front, front_h, front_l)]
                raw_o, wo_h, wo_l = (blocks(z, IB)(D) for z in (raw_out, out_h, out_l))
                cwe = b("cwe", [P, NT])
                sg = b("sg", [P, IB, QT])
                z = b("z", [P, IB, QT])
                zh = [b(f"zh{j}", [P, IB, QT], F16) for j in range(2)]
                zl = [b(f"zl{j}", [P, IB, QT], F16) for j in range(2)]
                s_rf, s_ro = sem("mo_s_rf"), sem("mo_s_ro")
                PE = Timeline(sem("mo_pe"), events(["g0", "u0", "g1", "u1", "y0", "y1", "y2", "y3"]), NG, ["y0", "y1", "y2", "y3"])
                AC = Timeline(sem("mo_act"), events(["si0", "si1"], [(3, "si1", ["wfh"]), (0, "si1", ["woh"])]), NG)
                DV = Timeline(sem("mo_dve"), events(["z0", "z1", "y0", "y1", "y2", "y3"], [(3, "z1", ["wfl"]), (0, "y3", ["wol", "cw"])]),
                              NG, ["y0", "y1", "y2", "y3"])
                PO = Timeline(sem("mo_pool"), events(["zh0", "zl0", "zh1", "zl1"]), NG)
                block = ctx.enter_context(nc.Block())

                @block.sync
                def _(sp):
                    def front_weights(g):
                        sp.dma_start(raw_f[:, :, :], egu[bass.ds(g * D, D), :].rearrange("(k p) n -> p k n", p=P)).then_inc(s_rf, 16)

                    def out_weights(g):
                        sp.dma_start(raw_o[:, :, :], ed[bass.ds(g * FI, FI), :].rearrange("(k p) n -> p k n", p=P)).then_inc(s_ro, 16)
                    out_weights(0)
                    with sp.Fori(0, NG) as i:
                        nxt = (i + 1) % NG
                        front_weights(nxt)
                        sp.wait_ge(DV.sem, DV.value("wol", Step(i, 0)))
                        met(sp)
                        out_weights(nxt)
                        sp.wait_ge(DV.sem, DV.value("wfl", Step(i, 3)))
                        met(sp)
                    sp.wait_ge(s_ro, 16 * (NG + 1))

                def split_front_hi(act):
                    return act.activation(flat_f[1], flat_f[0], ACT.Copy, scale=WS)

                def split_front_lo(dve):
                    return dve.scalar_tensor_tensor(flat_f[2], flat_f[0], WS, flat_f[1], ALU.mult, ALU.subtract)

                @block.gpsimd
                def _(pool):
                    s_zero = sem("mo_zero")
                    pool.memset(zh[1][:], 0.0)
                    pool.memset(zl[1][:], 0.0).then_inc(s_zero, 1)
                    pool.wait_ge(s_zero, 1)
                    PO.start(pool)
                    with pool.Fori(0, NG) as i:
                        for q in range(NQ):
                            st = Step(i, q)
                            for n in range(IB):
                                pool.wait_ge(DV.sem, DV.value(f"z{n}", st))
                                pool.wait_ge(PE.sem, PE.value("y3", st, 1))
                                met(pool)
                                PO.mark(pool.tensor_copy(zh[q % 2][:, n, :], z[:, n, :]), f"zh{n}", st)
                                pool.wait_ge(PO.sem, PO.value(f"zh{n}", st))
                                PO.mark(pool.tensor_tensor(zl[q % 2][:, n, :], z[:, n, :], zh[q % 2][:, n, :], ALU.subtract),
                                        f"zl{n}", st)

                @block.scalar
                def _(act):
                    AC.start(act)
                    with act.Fori(0, NG) as i:
                        for q in range(NQ):
                            st = Step(i, q)
                            for n in range(IB):
                                act.wait_ge(PE.sem, PE.value(f"g{n}", st))
                                act.wait_ge(DV.sem, DV.value(f"z{n}", st, 1))
                                AC.mark(act.activation(sg[:, n, :], bank[2 * n][:, :], ACT.Silu, scale=1 / WS), f"si{n}", st)
                            if q == 3:
                                act.wait_ge(s_rf, i * 16 + 16)
                                act.wait_ge(PE.sem, PE.value("u1", st))
                                AC.mark(split_front_hi(act), "wfh", st)
                            if q == 0:
                                act.wait_ge(s_ro, i * 16 + 16)
                                act.wait_ge(PE.sem, PE.value("y3", st))
                                AC.mark(act.activation(wo_h[:, :, :], raw_o[:, :, :], ACT.Copy, scale=WS), "woh", st)

                @block.vector
                def _(dve):
                    s_cwe = sem("mo_cwe0")
                    dve.memset(cwe[:, :], 0.0).then_inc(s_cwe, 1)
                    dve.wait_ge(s_cwe, 1)
                    DV.start(dve)

                    def back_add(st):
                        for t in range(TQ):
                            tile = t + TQ * ((st.q - 1) % NQ if st.i is not None else NQ - 1)
                            dve.wait_ge(PE.sem, PE.value(f"y{t}", st))
                            DV.mark(dve.scalar_tensor_tensor(acc[:, tile, :], bank[4 + t][:, :], cwe[:, tile:tile + 1],
                                                             acc[:, tile, :], ALU.mult, ALU.add), f"y{t}", st)

                    with dve.Fori(0, NG) as i:
                        for q in range(NQ):
                            st = Step(i, q)
                            for n in range(IB):
                                dve.wait_ge(PE.sem, PE.value(f"u{n}", st))
                                dve.wait_ge(AC.sem, AC.value(f"si{n}", st))
                                dve.wait_ge(PO.sem, PO.value(f"zl{n}", st, 1))
                                DV.mark(dve.scalar_tensor_tensor(z[:, n, :], bank[2 * n + 1][:, :], OS / WS, sg[:, n, :],
                                                                 ALU.mult, ALU.mult), f"z{n}", st)
                            if q == 3:
                                dve.wait_ge(AC.sem, AC.value("wfh", st))
                                DV.mark(split_front_lo(dve), "wfl", st)
                            if q == 1:
                                dve.wait_ge(DV.sem, DV.value("cw", st, 1))
                            back_add(st)
                            if q == 0:
                                dve.wait_ge(AC.sem, AC.value("woh", st))
                                DV.mark(dve.scalar_tensor_tensor(wo_l[:, :, :].rearrange("p a b -> p (a b)"),
                                                                 raw_o[:, :, :].rearrange("p a b -> p (a b)"), WS,
                                                                 wo_h[:, :, :].rearrange("p a b -> p (a b)"),
                                                                 ALU.mult, ALU.subtract), "wol", st)
                                dve.wait_ge(DV.sem, DV.value("y3", st))
                                DV.mark(dve.tensor_copy(cwe[:, :].rearrange("p (t a) -> p t a", a=1), cw[:, :, bass.ds(i, 1)]),
                                        "cw", st)
                    back_add(Step(None, 0))

                @block.tensor
                def _(pe):
                    PE.start(pe)

                    def back_out(st):
                        par = (st.q - 1) % 2 if st.i is not None else (NQ - 1) % 2
                        if st.q == 1:
                            pe.wait_ge(DV.sem, DV.value("wol", st, 1))
                        pe.wait_ge(PO.sem, PO.value("zl1", st, 1))
                        for t in range(TQ):
                            pe.wait_ge(DV.sem, DV.value(f"y{t}", st, 1))
                            tok = slice(t * P, (t + 1) * P)
                            PE.mark(three_pass(pe, bank[4 + t][:, :], [(zh[par][:, n, tok], zl[par][:, n, tok], wo_h[:, n, :],
                                                                        wo_l[:, n, :]) for n in range(IB)]), f"y{t}", st)

                    with pe.Fori(0, NG) as i:
                        for q in range(NQ):
                            st = Step(i, q)
                            if q == 0:
                                pe.wait_ge(DV.sem, DV.value("wfl", st, 1))
                            tok = slice(q * QT, (q + 1) * QT)
                            for n in range(IB):
                                for u, name in enumerate(("g", "u")):
                                    if u == 0:
                                        pe.wait_ge(AC.sem, AC.value(f"si{n}", st, 1))
                                    else:
                                        pe.wait_ge(DV.sem, DV.value(f"z{n}", st, 1))
                                    c = u * FI + n * P
                                    PE.mark(three_pass(pe, bank[2 * n + u][:, :],
                                                       [(wf_h[:, k, c:c + P], wf_l[:, k, c:c + P], xh[:, k, tok], xl[:, k, tok])
                                                        for k in range(KD)]), f"{name}{n}", st)
                            back_out(st)
                    back_out(Step(None, 0))

        def first_group(tag, loads, front):
            s_w, s_c = sem(f"{tag}_w0"), sem(f"{tag}_w0_chain")

            def prefetch(sp):
                for dst, src in loads:
                    sp.dma_start(dst, src).then_inc(s_w, 16)

            def prepare(pool):
                chain = chained(pool, s_c)
                pool.memset(out_h[:, :], 0.0)
                chain(pool.memset(out_l[:, :], 0.0))
                pool.wait_ge(s_w, 16 * len(loads))
                split_on_pool(pool, chain, raw_front[:, 0:front], front_h[:, 0:front], front_l[:, 0:front], WS)
            return prefetch, prepare

        with ExitStack() as held:
            ch, cl = sb("ch", [P, KD, T], F16, held), sb("cl", [P, KD, T], F16, held)
            bound = sb("bound", [P, B, S], F32, held)

            def mask_bound(pool):
                s_m, chain = sem("mask_in"), chained(pool, sem("mask_chain"))
                for h in range(2):
                    pool.dma_start(bound[64 * h:64 * h + 64, :, :], maskf.rearrange("b q k -> q b k")).then_inc(s_m, 16)
                pool.wait_ge(s_m, 32)
                bd = bound[:, :, :].rearrange("p b k -> p (b k)")
                chain(pool.tensor_scalar(bd, bd, 0.0, 0.0, ALU.is_equal, ALU.is_equal))
                chain(pool.tensor_scalar(bd, bd, BIG, -1e9 * float(HD2) ** 0.5, ALU.mult, ALU.add))

            self_attention(mask_bound)
            fw = (GQ + 2) * HD2
            wf = blocks(raw_front, KD)(fw)
            loads, c = [], 0
            for w, n in ((xwq, GQ * HD2), (xwk, HD2), (xwv, HD2)):
                loads.append((wf[:, :, c:c + n], w.rearrange("(k p) n -> p k n", p=P)[:, :, 0:n]))
                c += n
            layernorm("ln1", False, *first_group("xa", loads, KD * fw))
            cross_attention()
        layernorm("ln2", False, *first_group("mo", [(blocks(raw_front, KD)(2 * FI), egu[0:D, :].rearrange("(k p) n -> p k n", p=P))],
                                             KD * 2 * FI))
        router()
        experts()
        layernorm("ln3", True)


def kernel(**inputs):
    import numpy as np
    import concourse.bacc as bacc
    from concourse.bass_utils import run_bass_kernel_spmd

    f = {k: np.asarray(v) for k, v in inputs.items()}
    x = f["x"].reshape(T, D)
    half = HD2 // 2
    inv = (np.float32(1.0) / np.power(np.float32(10000.0), np.arange(0, HD2, 2, dtype=np.float32) / np.float32(HD2))).astype(np.float32)
    ang = (np.arange(S, dtype=np.float32)[None, :] * inv[:, None]).astype(np.float32)
    cos, sin = np.cos(ang) / np.float32(WS), np.sin(ang) / np.float32(WS)
    pos = np.arange(P) % S
    arrays = {
        "x": x,
        "xT": x.T,
        "cT": f["ctx_4096"].reshape(T, D).T,
        "maskf": f["mask_BxSxS2_ff1"],
        "wqT": f["L0_attn_Wq"].T, "bq": f["L0_attn_bq"],
        "wkT": f["L0_attn_Wk"].T, "bk": f["L0_attn_bk"],
        "wvT": f["L0_attn_Wv"].T, "bv": f["L0_attn_bv"],
        "woT": f["L0_attn_Wo"].T, "bo": f["L0_attn_bo"],
        "xwq": f["L0_xattn_wq"], "xwk": f["L0_xattn_wk"], "xwv": f["L0_xattn_wv"], "xwo": f["L0_xattn_wo"],
        "gwT": f["L0_ffn_gate_w"].T, "gbias": f["L0_ffn_bias"],
        "egu": np.concatenate([np.concatenate([f["L0_ffn_Wg"], f["L0_ffn_Sg"][None]]).transpose(0, 2, 1),
                               np.concatenate([f["L0_ffn_Wu"], f["L0_ffn_Su"][None]]).transpose(0, 2, 1)], axis=2)
        .reshape((NE + 1) * D, 2 * FI),
        "ed": np.concatenate([f["L0_ffn_Wd"], f["L0_ffn_Sd"][None]]).transpose(0, 2, 1).reshape((NE + 1) * FI, D),
        "causal": np.where(np.arange(S)[None, :] <= pos[:, None], np.float32(BIG), np.float32(-1e30)).astype(np.float32),
        "cosT": np.concatenate([cos, cos]).astype(np.float32),
        "sinT": np.concatenate([-sin, sin]).astype(np.float32),
        "parity": np.stack([(np.arange(P) // HD1) % 2 == e for e in range(2)], axis=1).astype(np.float32),
        "eye": np.eye(P, dtype=np.float32),
        "iota": np.broadcast_to(np.arange(NE, dtype=np.float32), (P, NE)),
    }
    nc = bacc.Bacc("TRN2", target_bir_lowering=False, num_devices=1)
    given, args = {}, []
    for name, a in arrays.items():
        a = np.ascontiguousarray(a)
        given[f"in_{name}"] = a
        args.append(nc.dram_tensor(f"in_{name}", a.shape, mybir.dt.from_np(a.dtype), kind="ExternalInput").ap())
    out = nc.dram_tensor("out_0", (T, D), F32, kind="ExternalOutput").ap()
    build(nc, *args, out)
    r = run_bass_kernel_spmd(nc, [given], core_ids=[0])
    return r.results[0]["out_0"].reshape(B, S, D)
```

```python
import concourse.bass as bass
from concourse import mybir
from contextlib import ExitStack

F32, F16, U32 = mybir.dt.float32, mybir.dt.float16, mybir.dt.uint32
ALU, ACT, AX = mybir.AluOpType, mybir.ActivationFunctionType, mybir.AxisListType

B, S, D = 32, 64, 512
T = B * S
P = 128
NT = T // P
TQ = 4
NQ = NT // TQ
QT = TQ * P
KD = D // P
H1, HD1 = 32, 16
HG = P // HD1
H2, HKV, HD2 = 32, 8, 128
GQ = H2 // HKV
NE, TOPK, FI = 16, 4, 256
IB = FI // P
ST = 256
SH = ST // P
PICKS = T * TOPK
NTILES = -(-((PICKS + NE * (ST - 1)) // ST) // 2) * 2
COLS = (NTILES + 2) * SH
DUMMY = 4 * SH
EPS = 1e-5
WS = 64.0
OS = 64.0
BIG = 3.0e38
ROUND = 1.5 * 2.0 ** 23


class Timeline:

    def __init__(self, sem, body, rounds, post=(), steps=NQ):
        self.sem, self.body, self.rounds, self.post, self.steps = sem, list(body), rounds, list(post), steps
        self.index = {k: n for n, k in enumerate(self.body)}
        self.post_index = {k: n for n, k in enumerate(self.post)}
        assert len(self.index) == len(self.body)
        self.cursor = 0

    def start(self, eng):
        eng.sem_inc(self.sem, len(self.body))

    def mark(self, instruction, name, step):
        order = self.post if step.i is None else self.body
        key = name if step.i is None else (step.q, name)
        assert order[self.cursor] == key, (order[self.cursor], key)
        self.cursor = (self.cursor + 1) % len(order)
        instruction.then_inc(self.sem, 1)

    def value(self, name, step, back=0):
        n = len(self.body)
        if step.i is None:
            if back == 0:
                return (self.rounds + 1) * n + self.post_index[name] + 1
            return self.rounds * n + self.index[(self.steps - back, name)] + 1
        q = step.q - back
        if q >= 0:
            return step.i * n + n + self.index[(q, name)] + 1
        return step.i * n + self.index[(q + self.steps, name)] + 1


class Step:

    def __init__(self, i, q):
        self.i, self.q = i, q


def events(per_step, extra=(), steps=NQ):
    out = []
    for q in range(steps):
        for name in per_step:
            out.append((q, name))
            for qq, after, names in extra:
                if qq == q and after == name:
                    out += [(q, x) for x in names]
    return out


def build(nc, x, xT, cT, maskf, wqT, bq, wkT, bk, wvT, bv, woT, bo, xwq, xwk, xwv, xwo,
          gwT, gbias, egu, ed, causal, cosT, sinT, parity, eye,
          iota, tileno, partno, spare, limits, below, ones, lower, xs, ys, out):
    top = ExitStack()
    with top:
        def sb(name, shape, dt=F32, where=top):
            return where.enter_context(nc.sbuf_tensor(name, shape, dt))

        def sem(name):
            return top.enter_context(nc.semaphore(name))

        bank = [top.enter_context(nc.psum_tensor(f"bank{n}", [P, 512], F32)) for n in range(8)]

        acc = sb("acc", [P, NT, D])
        xh = sb("xh", [P, KD, T], F16)
        xl = sb("xl", [P, KD, T], F16)
        ident = sb("ident", [P, P])
        mv = sb("mv", [P, NT, 2])
        rstd = sb("rstd", [P, NT, 1])
        eps = sb("eps", [P, 1])
        FRONT, OUTW = KD * (GQ + 2) * HD2, GQ * D
        raw_front, front_h, front_l = sb("raw_front", [P, FRONT]), sb("front_h", [P, FRONT], F16), sb("front_l", [P, FRONT], F16)
        raw_out, out_h, out_l = sb("raw_out", [P, OUTW]), sb("out_h", [P, OUTW], F16), sb("out_l", [P, OUTW], F16)

        def blocks(buffer, k):
            def view(n):
                return buffer[:, 0:k * n].rearrange("p (k n) -> p k n", k=k)
            return view

        s_met = sem("waits_met")

        def met(eng):
            eng.sem_inc(s_met, 1)

        def split_on_pool(pool, chain, raw, hi, lo, scale=None):
            if scale:
                chain(pool.tensor_scalar(raw, raw, scale, None, ALU.mult))
            chain(pool.tensor_copy(hi, raw))
            chain(pool.tensor_tensor(lo, raw, hi, ALU.subtract))

        def chained(eng, s):
            n = [0]

            def chain(m):
                n[0] += 1
                m.then_inc(s, 1)
                eng.wait_ge(s, n[0])
            return chain

        def layernorm(tag, prefetch, prepare):
            with ExitStack() as ctx:
                st = sb(f"{tag}_st", [P, NT, 6], where=ctx)
                xn = [sb(f"{tag}_xn{j}", [P, D], where=ctx) for j in range(TQ)]
                s_st, s_ag, s_sq, s_rs = sem(f"{tag}_st"), sem(f"{tag}_ag"), sem(f"{tag}_sq"), sem(f"{tag}_rs")
                order = [f"norm{j}" for j in range(TQ)] + [f"lo{j}" for j in range(TQ)]
                DV = Timeline(sem(f"{tag}_dve"), [(0, n) for n in order], NQ)
                AC = Timeline(sem(f"{tag}_act"), [(0, f"{w}{j}") for j in range(TQ) for w in ("hi", "back")], NQ)
                PE = Timeline(sem(f"{tag}_pe"), [(0, f"turn{j}") for j in range(TQ)], NQ)

                def before(tl, name, r):
                    return r.i * len(tl.body) + tl.index[(0, name)] + 1

                block = ctx.enter_context(nc.Block())

                @block.vector
                def _(dve):
                    for t in range(NT):
                        dve.bn_stats(st[:, t, :], acc[:, t, :]).then_inc(s_st, 1)
                    for t in range(NT):
                        dve.wait_ge(s_st, t + 1)
                        dve.bn_aggr(mv[:, t, :], st[:, t, :]).then_inc(s_ag, 1)
                    dve.wait_ge(s_sq, 1)
                    dve.reciprocal(rstd[:, :, :], rstd[:, :, :]).then_inc(s_rs, 1)
                    dve.wait_ge(s_rs, 1)
                    DV.start(dve)
                    with dve.Fori(0, NQ) as i:
                        r = Step(i, 0)
                        for j in range(TQ):
                            dve.wait_ge(AC.sem, before(AC, f"back{j}", r))
                            DV.mark(dve.tensor_scalar(xn[j][:, :], acc[:, i * TQ + j, :], mv[:, i * TQ + j, 0:1],
                                                      rstd[:, i * TQ + j, 0:1], ALU.subtract, ALU.mult), f"norm{j}", r)
                        for j in range(TQ):
                            dve.wait_ge(AC.sem, AC.value(f"hi{j}", r))
                            tok = bass.ds(i * QT + j * P, P)
                            DV.mark(dve.tensor_tensor(xl[:, :, tok], bank[j][:, :].rearrange("p (k t) -> p k t", k=KD),
                                                      xh[:, :, tok], ALU.subtract), f"lo{j}", r)

                @block.scalar
                def _(act):
                    act.wait_ge(s_ag, NT)
                    act.activation(rstd[:, :, :], mv[:, :, 1:2], ACT.Sqrt, bias=eps[:, :]).then_inc(s_sq, 1)
                    AC.start(act)
                    with act.Fori(0, NQ) as i:
                        r = Step(i, 0)
                        for j in range(TQ):
                            act.wait_ge(PE.sem, PE.value(f"turn{j}", r))
                            AC.mark(act.activation(xh[:, :, bass.ds(i * QT + j * P, P)],
                                                   bank[j][:, :].rearrange("p (k t) -> p k t", k=KD), ACT.Copy), f"hi{j}", r)
                            AC.mark(act.activation(acc[:, i * TQ + j, :], xn[j][:, :], ACT.Copy), f"back{j}", r)

                @block.gpsimd
                def _(pool):
                    prepare(pool)

                @block.sync
                def _(sp):
                    prefetch(sp)

                @block.tensor
                def _(pe):
                    PE.start(pe)
                    with pe.Fori(0, NQ) as i:
                        r = Step(i, 0)
                        for j in range(TQ):
                            pe.wait_ge(DV.sem, DV.value(f"norm{j}", r))
                            pe.wait_ge(DV.sem, before(DV, f"lo{j}", r))
                            for k in range(KD):
                                mm = pe.transpose(bank[j][:, k * P:(k + 1) * P], xn[j][:, k * P:(k + 1) * P], ident[:, :])
                            PE.mark(mm, f"turn{j}", r)

        def three_pass(pe, out_ap, pairs, start=True, stop=True):
            n = len(pairs)
            for m, (ah, al, bh, bl) in enumerate(pairs):
                pe.matmul(out_ap, ah, bh, start=start and m == 0, stop=False)
                pe.matmul(out_ap, ah, bl, start=False, stop=False)
                mm = pe.matmul(out_ap, al, bh, start=False, stop=stop and m == n - 1)
            return mm

        def self_attention(prefetch_ctx):
            NG, FW = H1 // HG, 3 * P
            with ExitStack() as ctx:
                def b(name, shape, dt=F32):
                    return sb("sa_" + name, shape, dt, ctx)
                raw_f, wf_h, wf_l = (blocks(z, KD)(FW) for z in (raw_front, front_h, front_l))
                flat_f = [z[:, 0:KD * FW] for z in (raw_front, front_h, front_l)]
                raw_o, wo_h, wo_l = raw_out[:, 0:D], out_h[:, 0:D], out_l[:, 0:D]
                stage = [b(f"stage{n}", [P, KD, QT]) for n in range(2)]
                rawb, bias_c, bv_row = b("rawb", [P, 2 + P]), b("bias_c", [P, 2]), b("bv_row", [P, P])
                par, caus = b("par", [P, 2]), b("caus", [P, S])
                qh, ql = b("qh", [P, QT], F16), b("ql", [P, QT], F16)
                kf, kxh, kxl = b("kf", [P, QT]), b("kxh", [P, 2, QT], F16), b("kxl", [P, 2, QT], F16)
                sc = b("sc", [P, 4, TQ, 2, S])
                mx, sm, rs = b("mx", [P, 4, 8]), b("sm", [P, 4, 8]), b("rs", [P, TQ, HG, 1])
                vf, vh, vl = b("vf", [P, TQ, P]), b("vh", [P, TQ, P], F16), b("vl", [P, TQ, P], F16)
                vbh, vbl = (b(n, [P, 2, TQ, 4, 2, HD1], F16) for n in ("vbh", "vbl"))
                pth, ptl = b("pth", [P, 4, TQ, P], F16), b("ptl", [P, 4, TQ, P], F16)
                at = b("at", [P, TQ, P])
                oh, ol = b("oh", [P, QT], F16), b("ol", [P, QT], F16)
                s_rf, s_ro, s_cn = sem("sa_s_rf"), sem("sa_s_ro"), sem("sa_s_cn")
                s_st, s_q0h, s_q0l, s_xq, s_acc = (sem("sa_" + n) for n in ("s_st0", "s_q0h", "s_q0l", "s_xq", "s_acc"))

                SB, PTB, PVB = [bank[2], bank[3]], [bank[4], bank[5]], bank[6]
                uses = ["k", "q", "v", "oT", "w0", "w1", "w2", "w3"]
                J4 = range(4)
                PE = Timeline(sem("sa_pe"), events(["k", "pt0", "pt1", "q", "pt2", "pt3", "s0", "s1", "v", "pv", "s2", "oT",
                                                    "s3", "w0", "w1", "w2", "w3"]), NG,
                              ["pt0", "pt1", "pt2", "pt3", "pv", "oT", "w0", "w1", "w2", "w3"])
                AC = Timeline(sem("sa_act"), events(["kf", "pe0", "pe1", "qh", "ke", "ko", "pe2", "pe3", "ex0", "ex1", "vh", "oh",
                                                     "vb", "ex2", "ex3"], [(3, "vb", ["wfh"]), (0, "ex3", ["woh"])]), NG,
                              ["pe0", "pe1", "pe2", "pe3", "oh"])
                DV = Timeline(sem("sa_dve"), events(["pl0", "pl1", "ql", "kle", "klo", "pl2", "pl3",
                                                     "mn0", "mx0", "sb0", "mn1", "mx1", "sb1", "no", "vf", "mn2", "mx2", "ol", "mn3",
                                                     "sb2", "mx3", "sb3", "w0", "w1", "vl", "vb", "w2", "w3", "sum", "rc"],
                                                    [(3, "vb", ["wfl", "bc0", "bc1"]), (0, "w3", ["wol"])]), NG,
                              ["pl0", "pl1", "pl2", "pl3", "no", "ol", "w0", "w1", "w2", "w3"])
                freed = {"k": (AC, "kf"), "q": (DV, "ql"), "oT": (DV, "ol"), "v": (DV, "vf"),
                         "w0": (DV, "w0"), "w1": (DV, "w1"), "w2": (DV, "w2"), "w3": (DV, "w3")}
                s_pre_a, s_pre_v, s_zero = sem("sa_pre_a"), sem("sa_pre_v"), sem("sa_zero")
                block = ctx.enter_context(nc.Block())

                def gbank(pe, name, st):
                    n = uses.index(name)
                    prev = uses[n - 2]
                    tl, ev = freed[prev]
                    back = 1 if n < 2 or (st.i is None and prev in ("k", "q", "v")) else 0
                    pe.wait_ge(tl.sem, tl.value(ev, st, back))
                    return bank[n % 2]

                def pair_values(copy, out, v, done):
                    for e in range(2):
                        for b2 in range(2):
                            rows, src = slice(64 * e, 64 * e + 64), slice(64 * b2, 64 * b2 + 64)
                            m = copy(out[rows, b2, :, :, e, :],
                                     v[src, :, :].rearrange("p t (j e d) -> p t j e d", j=4, e=2)[:, :, :, e, :])
                    done(m)

                @block.sync
                def _(sp):
                    def front_weights(g):
                        for n, w in enumerate((wkT, wqT, wvT)):
                            sp.dma_start(raw_f[:, :, n * P:(n + 1) * P],
                                         w.rearrange("(k p) n -> p k n", p=P)[:, :, bass.ds(g * P, P)]).then_inc(s_rf, 16)
                        for n, w in enumerate((bk, bq)):
                            sp.dma_start(rawb[:, n:n + 1], w.rearrange("(p a) -> p a", a=1)[bass.ds(g * P, P), :]).then_inc(s_rf, 16)
                        sp.dma_start(rawb[:, 2:2 + P],
                                     bv.rearrange("(a n) -> a n", a=1)[:, bass.ds(g * P, P)].to_broadcast([P, P])).then_inc(s_rf, 16)
                    sp.dma_start(stage[0][:, :, :], xT.rearrange("(k p) t -> p k t", p=P)[:, :, 0:QT]).then_inc(s_st, 16)
                    front_weights(0)
                    sp.dma_start(par[:, :], parity).then_inc(s_cn, 16)
                    sp.dma_start(caus[:, :], causal).then_inc(s_cn, 16)
                    sp.dma_start(ident[:, :], eye).then_inc(s_cn, 16)
                    sp.dma_start(raw_o, woT[0:P, :]).then_inc(s_ro, 16)
                    sp.wait_ge(s_pre_v, 3)
                    with sp.Fori(0, NG) as i:
                        nxt = (i + 1) % NG
                        front_weights(nxt)
                        sp.wait_ge(DV.sem, DV.value("wol", Step(i, 0)))
                        met(sp)
                        sp.dma_start(raw_o, woT[bass.ds(nxt * P, P), :]).then_inc(s_ro, 16)
                        sp.wait_ge(DV.sem, DV.value("bc1", Step(i, 3)))
                        met(sp)
                    sp.wait_ge(s_ro, 16 * (NG + 1))

                def split_front_hi(act):
                    return act.activation(flat_f[1], flat_f[0], ACT.Copy, scale=WS)

                def split_front_lo(dve):
                    return dve.scalar_tensor_tensor(flat_f[2], flat_f[0], WS, flat_f[1], ALU.mult, ALU.subtract)

                @block.gpsimd
                def _(pool):
                    chain = chained(pool, sem("sa_pool"))
                    pool.memset(eps[:, :], EPS)
                    for z in (sc, vbh, vbl, wo_h, wo_l):
                        pool.memset(z[:], 0.0)
                    chain(pool.memset(rs[:], 0.0))
                    pool.sem_inc(s_zero, 1)
                    s_a, s_bo = sem("sa_acc"), sem("sa_bo")
                    s_stage = [sem(f"sa_stage{n}") for n in range(2)]
                    views = [(xT, xh, xl), (cT, ch, cl)]

                    def load(n):
                        src = views[n // NQ][0].rearrange("(k p) t -> p k t", p=P)
                        q = n % NQ
                        pool.dma_start(stage[n % 2][:, :, :], src[:, :, q * QT:(q + 1) * QT]).then_inc(s_stage[n % 2], 16)

                    def split(n):
                        _, hi, lo = views[n // NQ]
                        tok = slice((n % NQ) * QT, (n % NQ + 1) * QT)
                        pool.wait_ge(s_stage[n % 2], 16 * ((n + 1) // 2))
                        split_on_pool(pool, chain, stage[n % 2][:, :, :], hi[:, :, tok], lo[:, :, tok])
                        pool.sem_inc(s_xq, 1)
                    pool.wait_ge(s_rf, 96)
                    load(1)
                    with nc.sbuf_tensor("bo_rows", [P, D], F32) as bo_rows:
                        pool.dma_start(bo_rows[:, :], bo.rearrange("(a n) -> a n", a=1).to_broadcast([P, D])).then_inc(s_bo, 16)
                        pool.dma_start(acc[:, :, :], x.rearrange("(t p) d -> p t d", p=P)).then_inc(s_a, 16)
                        split(1)
                        pool.wait_ge(s_bo, 16)
                        pool.wait_ge(s_a, 16)
                        chain(pool.tensor_tensor(acc[:, :, :], acc[:, :, :],
                                                 bo_rows[:, :].rearrange("p (a n) -> p a n", a=1).to_broadcast([P, NT, D]),
                                                 ALU.add))
                        pool.sem_inc(s_acc, 1)
                    pool.wait_ge(s_q0l, 1)
                    load(2)
                    for n in range(2, 2 * NQ):
                        if n + 1 < 2 * NQ:
                            load(n + 1)
                        split(n)
                    prefetch_ctx(pool)

                @block.scalar
                def _(act):
                    act.wait_ge(s_st, 16)
                    act.activation(xh[:, :, 0:QT], stage[0][:, :, :], ACT.Copy).then_inc(s_q0h, 1)
                    act.wait_ge(s_rf, 96)
                    split_front_hi(act).then_inc(s_pre_a, 1)
                    AC.start(act)
                    act.wait_ge(s_pre_v, 3)
                    act.wait_ge(s_zero, 1)

                    def back_p(st, js=J4):
                        for j in js:
                            act.wait_ge(PE.sem, PE.value(f"pt{j}", st))
                            act.wait_ge(PE.sem, PE.value("pv", st, 1))
                            AC.mark(act.activation(pth[:, j, :, :].rearrange("p a b -> p (a b)"), PTB[j % 2][:, :], ACT.Copy),
                                    f"pe{j}", st)

                    def back_o(st):
                        act.wait_ge(PE.sem, PE.value("oT", st))
                        act.wait_ge(PE.sem, PE.value("w3", st, 1))
                        AC.mark(act.activation(oh[:, :], bank[1][:, :], ACT.Copy), "oh", st)

                    def exponentials(st, js):
                        for j in js:
                            act.wait_ge(DV.sem, DV.value(f"sb{j}", st))
                            s2 = sc[:, j, :, :, :].rearrange("p a b c -> p (a b c)")
                            AC.mark(act.activation(s2, s2, ACT.Exp, scale=float(HD1) ** -0.5 / (WS * WS)), f"ex{j}", st)

                    with act.Fori(0, NG) as i:
                        for q in range(NQ):
                            st = Step(i, q)
                            act.wait_ge(PE.sem, PE.value("k", st))
                            act.wait_ge(DV.sem, DV.value("klo", st, 1))
                            if q == 0:
                                act.wait_ge(DV.sem, DV.value("bc1", st, 1))
                            AC.mark(act.activation(kf[:, :], bank[0][:, :], ACT.Identity, bias=bias_c[:, 0:1]), "kf", st)
                            back_p(st, (0, 1))
                            act.wait_ge(PE.sem, PE.value("q", st))
                            act.wait_ge(PE.sem, PE.value("s3", st, 1))
                            AC.mark(act.activation(qh[:, :], bank[1][:, :], ACT.Identity, bias=bias_c[:, 1:2]), "qh", st)
                            act.wait_ge(AC.sem, AC.value("kf", st))
                            for e in range(2):
                                AC.mark(act.activation(kxh[:, e, :], kf[:, :], ACT.Copy, scale=par[:, e:e + 1]),
                                        ("ke", "ko")[e], st)
                            back_p(st, (2, 3))
                            exponentials(st, (0, 1))
                            act.wait_ge(DV.sem, DV.value("vf", st))
                            act.wait_ge(DV.sem, DV.value("vb", st, 1))
                            AC.mark(act.activation(vh[:, :, :], vf[:, :, :], ACT.Copy), "vh", st)
                            back_o(st)
                            act.wait_ge(AC.sem, AC.value("vh", st))
                            pair_values(lambda o, v: act.activation(o, v, ACT.Copy), vbh, vh,
                                        lambda m: AC.mark(m, "vb", st))
                            if q == 3:
                                act.wait_ge(s_rf, i * 96 + 192)
                                AC.mark(split_front_hi(act), "wfh", st)
                            exponentials(st, (2, 3))
                            if q == 0:
                                act.wait_ge(s_ro, i * 16 + 16)
                                act.wait_ge(PE.sem, PE.value("w3", st))
                                AC.mark(act.activation(wo_h, raw_o, ACT.Copy, scale=WS), "woh", st)
                    back_p(Step(None, 0))
                    back_o(Step(None, 0))

                @block.vector
                def _(dve):
                    dve.wait_ge(s_q0h, 1)
                    dve.tensor_tensor(xl[:, :, 0:QT], stage[0][:, :, :], xh[:, :, 0:QT], ALU.subtract).then_inc(s_q0l, 1)
                    dve.wait_ge(s_pre_a, 1)
                    split_front_lo(dve).then_inc(s_pre_v, 1)

                    def biases(done0, done1):
                        done0(dve.tensor_scalar(bias_c[:, :], rawb[:, 0:2], WS, None, ALU.mult))
                        done1(dve.tensor_scalar(bv_row[:, :], rawb[:, 2:2 + P], WS, None, ALU.mult))
                    dve.wait_ge(s_rf, 96)
                    biases(lambda m: m.then_inc(s_pre_v, 1), lambda m: m.then_inc(s_pre_v, 1))
                    dve.wait_ge(s_pre_v, 3)
                    dve.wait_ge(s_cn, 48)
                    dve.wait_ge(s_zero, 1)
                    DV.start(dve)

                    def back_lo(st, j):
                        dve.wait_ge(AC.sem, AC.value(f"pe{j}", st))
                        h2 = pth[:, j, :, :].rearrange("p a b -> p (a b)")
                        DV.mark(dve.tensor_tensor(ptl[:, j, :, :].rearrange("p a b -> p (a b)"), PTB[j % 2][:, :], h2,
                                                  ALU.subtract), f"pl{j}", st)

                    def back_norm(st):
                        dve.wait_ge(PE.sem, PE.value("pv", st))
                        dve.wait_ge(DV.sem, DV.value("rc", st, 1))
                        dve.wait_ge(PE.sem, PE.value("oT", st, 1))
                        DV.mark(dve.tensor_tensor(at[:, :, :].rearrange("p t (g d) -> p t g d", d=HD1),
                                                  PVB[:, :].rearrange("p (t g d) -> p t g d", t=TQ, d=HD1),
                                                  rs[:, :, :, :].to_broadcast([P, TQ, HG, HD1]),
                                                  ALU.mult), "no", st)

                    def back_out_lo(st):
                        dve.wait_ge(AC.sem, AC.value("oh", st))
                        DV.mark(dve.tensor_tensor(ol[:, :], bank[1][:, :], oh[:, :], ALU.subtract), "ol", st)

                    def back_add(st, tiles):
                        dve.wait_ge(s_acc, 1)
                        for t in tiles:
                            dve.wait_ge(PE.sem, PE.value(f"w{t}", st))
                            row = acc[:, t + TQ * ((st.q - 1) % NQ if st.i is not None else NQ - 1), :]
                            DV.mark(dve.scalar_tensor_tensor(row, bank[t % 2][:, :], 1 / (WS * WS), row, ALU.mult, ALU.add),
                                    f"w{t}", st)

                    def smax(st, j, part):
                        s3 = sc[:, j, :, :, :].rearrange("p a b c -> p (a b) c")
                        if part == "mn":
                            dve.wait_ge(PE.sem, PE.value(f"s{j}", st))
                            DV.mark(dve.tensor_tensor(s3, SB[j % 2][:, :].rearrange("p (a c) -> p a c", a=8),
                                                      caus[:, :].rearrange("p (a c) -> p a c", a=1).to_broadcast([P, 8, S]),
                                                      ALU.min), f"mn{j}", st)
                        elif part == "mx":
                            dve.wait_ge(DV.sem, DV.value(f"mn{j}", st))
                            DV.mark(dve.tensor_reduce(mx[:, j, :], s3, AX.X, ALU.max), f"mx{j}", st)
                        else:
                            dve.wait_ge(DV.sem, DV.value(f"mx{j}", st))
                            DV.mark(dve.tensor_tensor(s3, s3, mx[:, j, :].rearrange("p (a c) -> p a c", c=1)
                                                      .to_broadcast([P, 8, S]), ALU.subtract), f"sb{j}", st)

                    with dve.Fori(0, NG) as i:
                        for q in range(NQ):
                            st = Step(i, q)
                            back_lo(st, 0)
                            back_lo(st, 1)
                            dve.wait_ge(AC.sem, AC.value("qh", st))
                            DV.mark(dve.scalar_tensor_tensor(ql[:, :], bank[1][:, :], bias_c[:, 1:2], qh[:, :], ALU.add,
                                                             ALU.subtract), "ql", st)
                            for e in range(2):
                                dve.wait_ge(AC.sem, AC.value(("ke", "ko")[e], st))
                                DV.mark(dve.scalar_tensor_tensor(kxl[:, e, :], kf[:, :], par[:, e:e + 1], kxh[:, e, :], ALU.mult,
                                                                 ALU.subtract), ("kle", "klo")[e], st)
                            back_lo(st, 2)
                            back_lo(st, 3)
                            for j in range(2):
                                for part in ("mn", "mx", "sb"):
                                    smax(st, j, part)
                            back_norm(st)
                            dve.wait_ge(PE.sem, PE.value("v", st))
                            DV.mark(dve.tensor_tensor(vf[:, :, :], bank[0][:, :].rearrange("p (t n) -> p t n", t=TQ),
                                                      bv_row[:, :].rearrange("p (a n) -> p a n", a=1).to_broadcast([P, TQ, P]),
                                                      ALU.add), "vf", st)
                            smax(st, 2, "mn")
                            smax(st, 2, "mx")
                            back_out_lo(st)
                            smax(st, 3, "mn")
                            smax(st, 2, "sb")
                            smax(st, 3, "mx")
                            smax(st, 3, "sb")
                            back_add(st, (0, 1))
                            dve.wait_ge(AC.sem, AC.value("vh", st))
                            DV.mark(dve.tensor_tensor(vl[:, :, :], vf[:, :, :], vh[:, :, :], ALU.subtract), "vl", st)
                            dve.wait_ge(DV.sem, DV.value("vl", st))
                            pair_values(lambda o, v: dve.tensor_copy(o, v), vbl, vl, lambda m: DV.mark(m, "vb", st))
                            if q == 3:
                                dve.wait_ge(AC.sem, AC.value("wfh", st))
                                DV.mark(split_front_lo(dve), "wfl", st)
                                dve.wait_ge(DV.sem, DV.value("vf", st))
                                biases(lambda m: DV.mark(m, "bc0", st), lambda m: DV.mark(m, "bc1", st))
                            back_add(st, (2, 3))
                            if q == 0:
                                dve.wait_ge(AC.sem, AC.value("woh", st))
                                DV.mark(dve.scalar_tensor_tensor(wo_l, raw_o, WS, wo_h, ALU.mult, ALU.subtract), "wol", st)
                            dve.wait_ge(AC.sem, AC.value("ex3", st))
                            DV.mark(dve.tensor_reduce(sm[:, :, :], sc[:, :, :, :, :].rearrange("p j a b c -> p j (a b) c"), AX.X,
                                                      ALU.add), "sum", st)
                            dve.wait_ge(DV.sem, DV.value("sum", st))
                            DV.mark(dve.reciprocal(rs[:, :, :, 0].rearrange("p t (j e) -> p t j e", e=2),
                                                   sm[:, :, :].rearrange("p j (t e) -> p t j e", e=2)), "rc", st)
                    st = Step(None, 0)
                    for j in J4:
                        back_lo(st, j)
                    back_norm(st)
                    back_out_lo(st)
                    back_add(st, range(TQ))

                @block.tensor
                def _(pe):
                    PE.start(pe)
                    pe.wait_ge(s_q0l, 1)
                    pe.wait_ge(s_zero, 1)
                    pe.wait_ge(s_cn, 48)
                    pe.wait_ge(s_pre_v, 3)

                    def feature_major(name, st, col):
                        o = gbank(pe, name, st)
                        tok = slice(st.q * QT, (st.q + 1) * QT)
                        PE.mark(three_pass(pe, o[:, :], [(wf_h[:, k, col:col + P], wf_l[:, k, col:col + P], xh[:, k, tok],
                                                          xl[:, k, tok]) for k in range(KD)]), name, st)

                    def back_p(st, js):
                        for j in js:
                            if j == 0:
                                pe.wait_ge(AC.sem, AC.value("ex3", st, 1))
                            if j < 2:
                                pe.wait_ge(DV.sem, DV.value(f"pl{j + 2}", st, 1))
                            else:
                                pe.wait_ge(DV.sem, DV.value(f"pl{j - 2}", st))
                            for t in range(TQ):
                                mm = pe.transpose(PTB[j % 2][:, t * P:(t + 1) * P],
                                                  sc[:, j, t, :, :].rearrange("p e k -> p (e k)"), ident[:, :])
                            PE.mark(mm, f"pt{j}", st)

                    def back_pv(st, ts=range(TQ)):
                        if 0 in ts:
                            pe.wait_ge(AC.sem, AC.value("vb", st, 1))
                            pe.wait_ge(DV.sem, DV.value("no", st, 1))
                            pe.wait_ge(DV.sem, DV.value("pl3", st))
                        for t in ts:
                            for b2 in range(2):
                                qs = slice(64 * b2, 64 * b2 + 64)
                                for j in J4:
                                    pair = "p e d -> p (e d)"
                                    mm = three_pass(pe, PVB[qs, (4 * t + j) * 2 * HD1:(4 * t + j + 1) * 2 * HD1],
                                                    [(pth[:, j, t, qs], ptl[:, j, t, qs], vbh[:, b2, t, j, :, :].rearrange(pair),
                                                      vbl[:, b2, t, j, :, :].rearrange(pair))])
                        if TQ - 1 in ts:
                            PE.mark(mm, "pv", st)

                    def back_turn(st):
                        o = gbank(pe, "oT", st)
                        pe.wait_ge(DV.sem, DV.value("no", st))
                        for t in range(TQ):
                            mm = pe.transpose(o[:, t * P:(t + 1) * P], at[:, t, :], ident[:, :])
                        PE.mark(mm, "oT", st)

                    def back_out(st):
                        pe.wait_ge(DV.sem, DV.value("ol", st))
                        if st.q == 1:
                            pe.wait_ge(DV.sem, DV.value("wol", st, 1))
                        for t in range(TQ):
                            o = gbank(pe, f"w{t}", st)
                            tok = slice(t * P, (t + 1) * P)
                            PE.mark(three_pass(pe, o[:, :], [(oh[:, tok], ol[:, tok], wo_h, wo_l)]), f"w{t}", st)

                    def scores(st, js):
                        for j in js:
                            if j < 2:
                                pe.wait_ge(DV.sem, DV.value(f"mn{j + 2}", st, 1))
                            else:
                                pe.wait_ge(DV.sem, DV.value(f"mn{j - 2}", st))
                            r = slice(32 * j, 32 * j + 32)
                            for t in range(TQ):
                                for b2 in range(2):
                                    tok = slice(t * P + b2 * 64, t * P + b2 * 64 + 64)
                                    mm = three_pass(pe, SB[j % 2][64 * b2:64 * b2 + 64, t * P:(t + 1) * P],
                                                    [(qh[r, tok], ql[r, tok], kxh[r, :, tok], kxl[r, :, tok])])
                            PE.mark(mm, f"s{j}", st)

                    with pe.Fori(0, NG) as i:
                        for q in range(NQ):
                            st = Step(i, q)
                            if q == 0:
                                pe.wait_ge(DV.sem, DV.value("wfl", st, 1))
                            else:
                                pe.wait_ge(s_xq, q)
                            def values(ts):
                                for t in ts:
                                    tok = slice(q * QT + t * P, q * QT + (t + 1) * P)
                                    mm = three_pass(pe, bank[0][:, t * P:(t + 1) * P],
                                                    [(xh[:, k, tok], xl[:, k, tok], wf_h[:, k, 2 * P:3 * P], wf_l[:, k, 2 * P:3 * P])
                                                     for k in range(KD)])
                                return mm
                            feature_major("k", st, 0)
                            back_p(st, (0, 1))
                            feature_major("q", st, P)
                            back_p(st, (2, 3))
                            gbank(pe, "v", st)
                            values((0, 1, 2))
                            pe.wait_ge(DV.sem, DV.value("klo", st))
                            scores(st, (0, 1))
                            back_pv(st, (0, 1))
                            PE.mark(values((3,)), "v", st)
                            back_pv(st, (2, 3))
                            scores(st, (2,))
                            back_turn(st)
                            scores(st, (3,))
                            back_out(st)
                    st = Step(None, 0)
                    back_p(st, J4)
                    back_pv(st)
                    back_turn(st)
                    back_out(st)

        def cross_attention():
            NG = HKV
            FW = GQ * HD2 + 2 * HD2
            with ExitStack() as ctx:
                def b(name, shape, dt=F32):
                    return sb("xa_" + name, shape, dt, ctx)
                raw_f, wf_h, wf_l = (blocks(z, KD)(FW) for z in (raw_front, front_h, front_l))
                flat_f = [z[:, 0:KD * FW] for z in (raw_front, front_h, front_l)]
                raw_o, wo_h, wo_l = (blocks(z, GQ)(D) for z in (raw_out, out_h, out_l))
                cs, sn = b("cs", [P, S]), b("sn", [P, S])
                NR = 1 + GQ
                x0 = [b(f"x0_{r}", [P, QT]) for r in range(NR)]
                xs = [b(f"xs_{r}", [P, QT]) for r in range(NR)]
                rr = [b(f"rr_{r}", [P, QT]) for r in range(2)]
                rkh, rkl = b("rkh", [P, 2 * TQ, S], F16), b("rkl", [P, 2 * TQ, S], F16)
                rqh, rql = (b(n, [P, GQ // 2, 2 * TQ, 2, S], F16) for n in ("rqh", "rql"))
                sc = b("sc", [P, 2, TQ, 2, S])
                mx, sm, rs = b("mx", [P, 2, 8]), b("sm", [P, 2, 8]), b("rs", [P, 2, 8])
                vh, vl = b("vh", [P, TQ, P], F16), b("vl", [P, TQ, P], F16)
                pth, ptl = b("pth", [P, 2, TQ, P], F16), b("ptl", [P, 2, TQ, P], F16)
                oh, ol = b("oh", [P, GQ, QT], F16), b("ol", [P, GQ, QT], F16)
                s_rf, s_ro, s_cn = sem("xa_s_rf"), sem("xa_s_ro"), sem("xa_s_cn")
                SB, PTB, PVB = [bank[2], bank[3]], [bank[4], bank[5]], [bank[6], bank[7], bank[4], bank[5]]
                names = [f"r{r}" for r in range(NR)]
                uses = names + ["v", "w0", "w1", "w2", "w3"]
                PE = Timeline(sem("xa_pe"), events(names[:-1] + ["pt0", "pt1", names[-1], "v", "pv0", "pv1", "pv2", "pv3",
                                                                 "s0", "s1", "w0", "w1", "w2", "w3"]), NG,
                              ["pt0", "pt1", "pv0", "pv1", "pv2", "pv3", "w0", "w1", "w2", "w3"])
                act_order, rope_order = [], []
                for r in range(NR):
                    if r == NR - 1:
                        act_order += ["pe0", "pe1"]
                        rope_order += ["pl0", "pl1"]
                    act_order += [f"r{r}"] + ([f"h{r - 2}"] if r >= 2 else [])
                    rope_order += [f"cm{r}"] + ([f"ra{r - 1}"] if r >= 1 else []) + ([f"l{r - 2}"] if r >= 2 else [])
                AC = Timeline(sem("xa_act"), events(act_order + [f"h{NR - 2}", f"h{NR - 1}", "hi0", "hi1", "hi2", "hi3",
                                                                 "vh", "ex0", "ex1"],
                                                    [(3, "vh", ["wfh"]), (0, "ex1", ["woh"])]), NG,
                              ["pe0", "pe1", "hi0", "hi1", "hi2", "hi3"])
                DV = Timeline(sem("xa_dve"), events(rope_order + [f"l{NR - 2}", f"ra{NR - 1}", f"l{NR - 1}",
                                                                  "lo0", "lo1", "lo2", "lo3", "mn0", "vl", "mn1", "mx0",
                                                                  "sb0", "w0", "mx1", "sb1", "w1", "w2", "w3", "sum", "rc"],
                                                    [(3, "w1", ["wfl"]), (0, "w3", ["wol"])]), NG,
                              ["pl0", "pl1", "lo0", "lo1", "lo2", "lo3", "w0", "w1", "w2", "w3"])
                PO = Timeline(sem("xa_pool"), events([f"sm{r}" for r in range(NR)] + ["nm"]), NG)
                freed = {n: (AC, n) for n in names}
                freed["v"] = (DV, "vl")
                freed.update({f"w{t}": (DV, f"w{t}") for t in range(TQ)})
                block = ctx.enter_context(nc.Block())

                def heads(o, tp, b2):
                    return o[:, :, :].rearrange("p h (t b s) -> p t b h s", t=TQ, b=2)[:, 2 * tp:2 * tp + 2, b2, :, :]

                def rotated(keys, queries, r):
                    return keys[:, :, :] if r == 0 else queries[:, (r - 1) // 2, :, (r - 1) % 2, :]

                def gbank(pe, name, st):
                    n = uses.index(name)
                    prev = uses[n - 2]
                    tl, ev = freed[prev]
                    back = 1 if n < 2 or (st.i is None and not prev.startswith("w")) else 0
                    pe.wait_ge(tl.sem, tl.value(ev, st, back))
                    return bank[n % 2]

                @block.sync
                def _(sp):
                    def front_weights(g):
                        c = 0
                        for w, n in ((xwq, GQ * HD2), (xwk, HD2), (xwv, HD2)):
                            sp.dma_start(raw_f[:, :, c:c + n],
                                         w.rearrange("(k p) n -> p k n", p=P)[:, :, bass.ds(g * n, n)]).then_inc(s_rf, 16)
                            c += n

                    def out_weights(g):
                        sp.dma_start(raw_o[:, :, :], xwo[bass.ds(g * GQ * HD2, GQ * HD2), :]
                                     .rearrange("(h p) n -> p h n", p=P)).then_inc(s_ro, 16)
                    sp.dma_start(cs[:, :], cosT).then_inc(s_cn, 16)
                    sp.dma_start(sn[:, :], sinT).then_inc(s_cn, 16)
                    out_weights(0)
                    with sp.Fori(0, NG) as i:
                        nxt = (i + 1) % NG
                        front_weights(nxt)
                        sp.wait_ge(DV.sem, DV.value("wol", Step(i, 0)))
                        met(sp)
                        out_weights(nxt)
                        sp.wait_ge(DV.sem, DV.value("wfl", Step(i, 3)))
                        met(sp)
                    sp.wait_ge(s_ro, 16 * (NG + 1))

                def split_front_hi(act):
                    return act.activation(flat_f[1], flat_f[0], ACT.Copy, scale=WS)

                def split_front_lo(dve):
                    return dve.scalar_tensor_tensor(flat_f[2], flat_f[0], WS, flat_f[1], ALU.mult, ALU.subtract)

                @block.gpsimd
                def _(pool):
                    s_zero = sem("xa_zero")
                    for z in (sc, vh):
                        pool.memset(z[:], 0.0)
                    pool.memset(vl[:], 0.0).then_inc(s_zero, 1)
                    pool.wait_ge(s_zero, 1)
                    pool.wait_ge(s_cn, 32)
                    PO.start(pool)
                    with pool.Fori(0, NG) as i:
                        for q in range(NQ):
                            st = Step(i, q)
                            for r in range(NR):
                                pool.wait_ge(AC.sem, AC.value(f"r{r}", st))
                                xr = xs[r][:, :].rearrange("p (a s) -> p a s", s=S)
                                PO.mark(pool.tensor_tensor(xr, xr, sn[:, :].rearrange("p (a s) -> p a s", a=1)
                                                           .to_broadcast([P, QT // S, S]), ALU.mult), f"sm{r}", st)
                            pool.wait_ge(DV.sem, DV.value("rc", st))
                            s4 = sc[:, :, :, :, :].rearrange("p h t b k -> p (h t b) k")
                            PO.mark(pool.tensor_tensor(s4, s4, rs[:, :, :].rearrange("p h (t a) -> p (h t) a", a=1)
                                                       .to_broadcast([P, 16, S]), ALU.mult), "nm", st)

                @block.scalar
                def _(act):
                    AC.start(act)

                    def back_p(st):
                        for h in range(2):
                            act.wait_ge(PE.sem, PE.value(f"pt{h}", st))
                            act.wait_ge(PE.sem, PE.value("pv3", st, 1))
                            AC.mark(act.activation(pth[:, h, :, :].rearrange("p a b -> p (a b)"), PTB[h][:, :], ACT.Copy, scale=OS),
                                    f"pe{h}", st)

                    def back_o(st):
                        for c in range(4):
                            tp, b2 = c // 2, c % 2
                            act.wait_ge(PE.sem, PE.value(f"pv{c}", st))
                            act.wait_ge(PE.sem, PE.value("w3", st, 1))
                            AC.mark(act.activation(heads(oh, tp, b2), PVB[c][:, :].rearrange("p (t h s) -> p t h s", t=2, h=GQ),
                                                   ACT.Copy), f"hi{c}", st)

                    def copies(st, r):
                        act.wait_ge(PE.sem, PE.value(f"r{r}", st))
                        if r == 0:
                            act.wait_ge(DV.sem, DV.value(f"ra{NR - 1}", st, 1))
                        src = bank[r % 2]
                        act.activation(x0[r][:, :], src[:, :], ACT.Copy)
                        act.activation(xs[r][0:64, :], src[64:128, :], ACT.Copy)
                        AC.mark(act.activation(xs[r][64:128, :], src[0:64, :], ACT.Copy), f"r{r}", st)

                    def rotated_hi(st, r):
                        act.wait_ge(DV.sem, DV.value(f"ra{r}", st))
                        if r == 0:
                            act.wait_ge(PE.sem, PE.value("s1", st, 1))
                        AC.mark(act.activation(rotated(rkh, rqh, r), rr[r % 2][:, :].rearrange("p (a s) -> p a s", s=S),
                                               ACT.Copy), f"h{r}", st)

                    with act.Fori(0, NG) as i:
                        for q in range(NQ):
                            st = Step(i, q)
                            for r in range(NR):
                                if r == NR - 1:
                                    back_p(st)
                                copies(st, r)
                                if r >= 2:
                                    rotated_hi(st, r - 2)
                            rotated_hi(st, NR - 2)
                            rotated_hi(st, NR - 1)
                            back_o(st)
                            act.wait_ge(PE.sem, PE.value("pv3", st))
                            AC.mark(act.activation(vh[:, :, :].rearrange("p t n -> p (t n)"), bank[uses.index("v") % 2][:, :],
                                                   ACT.Copy, scale=1 / WS), "vh", st)
                            if q == 3:
                                act.wait_ge(s_rf, i * 48 + 48)
                                AC.mark(split_front_hi(act), "wfh", st)
                            for h in range(2):
                                act.wait_ge(DV.sem, DV.value(f"sb{h}", st))
                                s2 = sc[:, h, :, :, :].rearrange("p a b c -> p (a b c)")
                                AC.mark(act.activation(s2, s2, ACT.Exp, scale=float(HD2) ** -0.5), f"ex{h}", st)
                            if q == 0:
                                act.wait_ge(s_ro, i * 16 + 16)
                                act.wait_ge(PE.sem, PE.value("w3", st))
                                AC.mark(act.activation(wo_h[:, :, :], raw_o[:, :, :], ACT.Copy, scale=WS), "woh", st)
                    back_p(Step(None, 0))
                    back_o(Step(None, 0))

                @block.vector
                def _(dve):
                    dve.wait_ge(s_cn, 32)
                    DV.start(dve)

                    def back_p_lo(st):
                        for h in range(2):
                            dve.wait_ge(AC.sem, AC.value(f"pe{h}", st))
                            DV.mark(dve.scalar_tensor_tensor(ptl[:, h, :, :].rearrange("p a b -> p (a b)"), PTB[h][:, :], OS,
                                                             pth[:, h, :, :].rearrange("p a b -> p (a b)"), ALU.mult,
                                                             ALU.subtract), f"pl{h}", st)

                    def back_lo(st):
                        for c in range(4):
                            tp, b2 = c // 2, c % 2
                            dve.wait_ge(AC.sem, AC.value(f"hi{c}", st))
                            DV.mark(dve.tensor_tensor(heads(ol, tp, b2), PVB[c][:, :].rearrange("p (t h s) -> p t h s", t=2, h=GQ),
                                                      heads(oh, tp, b2), ALU.subtract), f"lo{c}", st)

                    def back_add(st, ts=range(TQ)):
                        for t in ts:
                            dve.wait_ge(PE.sem, PE.value(f"w{t}", st))
                            row = acc[:, t + TQ * ((st.q - 1) % NQ if st.i is not None else NQ - 1), :]
                            DV.mark(dve.scalar_tensor_tensor(row, bank[uses.index(f"w{t}") % 2][:, :], 1 / (WS * OS), row,
                                                             ALU.mult, ALU.add), f"w{t}", st)

                    def cosine(st, r):
                        dve.wait_ge(AC.sem, AC.value(f"r{r}", st))
                        xr = x0[r][:, :].rearrange("p (a s) -> p a s", s=S)
                        DV.mark(dve.tensor_tensor(xr, xr, cs[:, :].rearrange("p (a s) -> p a s", a=1)
                                                  .to_broadcast([P, QT // S, S]), ALU.mult), f"cm{r}", st)

                    def rotate(st, r):
                        dve.wait_ge(PO.sem, PO.value(f"sm{r}", st))
                        dve.wait_ge(DV.sem, DV.value(f"cm{r}", st))
                        dve.wait_ge(DV.sem, DV.value(f"l{r - 2}", st) if r >= 2 else DV.value(f"l{NR - 1}", st, 1))
                        DV.mark(dve.tensor_tensor(rr[r % 2][:, :], x0[r][:, :], xs[r][:, :], ALU.add), f"ra{r}", st)

                    def rotated_lo(st, r):
                        dve.wait_ge(AC.sem, AC.value(f"h{r}", st))
                        DV.mark(dve.tensor_tensor(rotated(rkl, rql, r), rr[r % 2][:, :].rearrange("p (a s) -> p a s", s=S),
                                                  rotated(rkh, rqh, r), ALU.subtract), f"l{r}", st)

                    def smax(st, h, part):
                        s3 = sc[:, h, :, :, :].rearrange("p a b c -> p (a b) c")
                        if part == "mn":
                            bnd = bound[:, 2 * TQ * st.q:2 * TQ * (st.q + 1), :]
                            dve.wait_ge(PE.sem, PE.value(f"s{h}", st))
                            DV.mark(dve.tensor_tensor(s3, SB[h][:, :].rearrange("p (a c) -> p a c", a=8), bnd, ALU.min),
                                    f"mn{h}", st)
                        elif part == "mx":
                            dve.wait_ge(DV.sem, DV.value(f"mn{h}", st))
                            DV.mark(dve.tensor_reduce(mx[:, h, :], s3, AX.X, ALU.max), f"mx{h}", st)
                        else:
                            dve.wait_ge(DV.sem, DV.value(f"mx{h}", st))
                            DV.mark(dve.tensor_tensor(s3, s3, mx[:, h, :].rearrange("p (a c) -> p a c", c=1)
                                                      .to_broadcast([P, 8, S]), ALU.subtract), f"sb{h}", st)

                    with dve.Fori(0, NG) as i:
                        for q in range(NQ):
                            st = Step(i, q)
                            for r in range(NR):
                                if r == NR - 1:
                                    back_p_lo(st)
                                cosine(st, r)
                                if r >= 1:
                                    rotate(st, r - 1)
                                if r >= 2:
                                    rotated_lo(st, r - 2)
                            rotated_lo(st, NR - 2)
                            rotate(st, NR - 1)
                            rotated_lo(st, NR - 1)
                            back_lo(st)
                            smax(st, 0, "mn")
                            dve.wait_ge(AC.sem, AC.value("vh", st))
                            DV.mark(dve.scalar_tensor_tensor(vl[:, :, :].rearrange("p t n -> p (t n)"),
                                                             bank[uses.index("v") % 2][:, :], 1 / WS,
                                                             vh[:, :, :].rearrange("p t n -> p (t n)"), ALU.mult, ALU.subtract),
                                    "vl", st)
                            smax(st, 1, "mn")
                            for h in range(2):
                                smax(st, h, "mx")
                                smax(st, h, "sb")
                                back_add(st, [h])
                            if q == 3:
                                dve.wait_ge(AC.sem, AC.value("wfh", st))
                                DV.mark(split_front_lo(dve), "wfl", st)
                            back_add(st, [2, 3])
                            if q == 0:
                                dve.wait_ge(AC.sem, AC.value("woh", st))
                                DV.mark(dve.scalar_tensor_tensor(wo_l[:, :, :].rearrange("p a b -> p (a b)"),
                                                                 raw_o[:, :, :].rearrange("p a b -> p (a b)"), WS,
                                                                 wo_h[:, :, :].rearrange("p a b -> p (a b)"),
                                                                 ALU.mult, ALU.subtract), "wol", st)
                            dve.wait_ge(AC.sem, AC.value("ex1", st))
                            DV.mark(dve.tensor_reduce(sm[:, :, :], sc[:, :, :, :, :].rearrange("p h t b k -> p h (t b) k"), AX.X,
                                                      ALU.add), "sum", st)
                            dve.wait_ge(DV.sem, DV.value("sum", st))
                            DV.mark(dve.reciprocal(rs[:, :, :], sm[:, :, :]), "rc", st)
                    st = Step(None, 0)
                    back_p_lo(st)
                    back_lo(st)
                    back_add(st)

                @block.tensor
                def _(pe):
                    PE.start(pe)

                    def back_p(st):
                        pe.wait_ge(PO.sem, PO.value("nm", st, 1))
                        for h in range(2):
                            pe.wait_ge(DV.sem, DV.value(f"lo{2 + h}", st, 1))
                            for t in range(TQ):
                                mm = pe.transpose(PTB[h][:, t * P:(t + 1) * P],
                                                  sc[:, h, t, :, :].rearrange("p b k -> p (b k)"), ident[:, :])
                            PE.mark(mm, f"pt{h}", st)

                    def back_pv(st):
                        pe.wait_ge(DV.sem, DV.value("pl1", st))
                        pe.wait_ge(DV.sem, DV.value("vl", st, 1))
                        for c in range(4):
                            tp, b2 = c // 2, c % 2
                            if c < 2:
                                pe.wait_ge(DV.sem, DV.value(f"lo{c}", st, 1))
                            rows = slice(64 * b2, 64 * b2 + 64)
                            for t2 in range(2):
                                t = 2 * tp + t2
                                mm = three_pass(pe, PVB[c][:, t2 * 256:(t2 + 1) * 256],
                                                [(vh[rows, t, :], vl[rows, t, :], pth[rows, :, t, :], ptl[rows, :, t, :])])
                            PE.mark(mm, f"pv{c}", st)

                    def back_out(st):
                        if st.q == 1:
                            pe.wait_ge(DV.sem, DV.value("wol", st, 1))
                        for t in range(TQ):
                            if t % 2 == 0:
                                pe.wait_ge(DV.sem, DV.value(f"lo{t + 1}", st))
                            o = gbank(pe, f"w{t}", st)
                            tok = slice(t * P, (t + 1) * P)
                            PE.mark(three_pass(pe, o[:, :], [(oh[:, h, tok], ol[:, h, tok], wo_h[:, h, :], wo_l[:, h, :])
                                                             for h in range(GQ)]), f"w{t}", st)

                    def scores(st, h):
                        pe.wait_ge(DV.sem, DV.value(f"mn{h}", st, 1))
                        pe.wait_ge(DV.sem, DV.value(f"l{2 * h + 2}", st))
                        for bb in range(2 * TQ):
                            pair = "p a s -> p (a s)"
                            mm = three_pass(pe, SB[h][:, 64 * bb:64 * bb + 64],
                                            [(rqh[:, h, bb, :, :].rearrange(pair), rql[:, h, bb, :, :].rearrange(pair),
                                              rkh[:, bb, :], rkl[:, bb, :])])
                        PE.mark(mm, f"s{h}", st)

                    with pe.Fori(0, NG) as i:
                        for q in range(NQ):
                            st = Step(i, q)
                            if q == 0:
                                pe.wait_ge(DV.sem, DV.value("wfl", st, 1))
                            tok = slice(q * QT, (q + 1) * QT)
                            for r in range(NR):
                                if r == NR - 1:
                                    back_p(st)
                                o = gbank(pe, f"r{r}", st)
                                c = GQ * HD2 if r == 0 else (r - 1) * HD2
                                ah, al = (ch, cl) if r == 0 else (xh, xl)
                                PE.mark(three_pass(pe, o[:, :], [(wf_h[:, k, c:c + P], wf_l[:, k, c:c + P], ah[:, k, tok],
                                                                  al[:, k, tok]) for k in range(KD)]), f"r{r}", st)
                            o = gbank(pe, "v", st)
                            c = (GQ + 1) * HD2
                            for t in range(TQ):
                                tk = slice(q * QT + t * P, q * QT + (t + 1) * P)
                                mm = three_pass(pe, o[:, t * P:(t + 1) * P],
                                                [(ch[:, k, tk], cl[:, k, tk], wf_h[:, k, c:c + P], wf_l[:, k, c:c + P])
                                                 for k in range(KD)])
                            PE.mark(mm, "v", st)
                            back_pv(st)
                            scores(st, 0)
                            scores(st, 1)
                            back_out(st)
                    st = Step(None, 0)
                    back_p(st)
                    back_pv(st)
                    back_out(st)

        def shared_weights(m):
            s_w, s_c, s_ch = sem("se_w"), sem("se_c"), sem("se_chain")

            def prefetch(sp):
                sp.dma_start(blocks(raw_front, KD)(2 * FI), egu[NE * D:, :].rearrange("(k p) n -> p k n", p=P)).then_inc(s_w, 16)
                sp.dma_start(blocks(raw_out, IB)(D), ed[NE * FI:, :].rearrange("(k p) n -> p k n", p=P)).then_inc(s_w, 16)
                sp.dma_start(m.gate[:, :, :], gwT.rearrange("(k p) n -> p k n", p=P)).then_inc(s_c, 16)
                sp.dma_start(m.bias[:, :], gbias.rearrange("(a n) -> a n", a=1).to_broadcast([P, NE])).then_inc(s_c, 16)
                sp.dma_start(m.below[:, :, :], below).then_inc(s_c, 16)
                for dst, src in ((m.count, iota), (m.tile_no, tileno), (m.part_no, partno), (m.limits, limits), (m.spare, spare), (m.ones, ones),
                                 (m.lower, lower)):
                    sp.dma_start(dst[:, :], src).then_inc(s_c, 16)
                sp.wait_ge(s_c, 16 * 10)

            def prepare(pool):
                chain = chained(pool, s_ch)
                pool.wait_ge(s_w, 32)
                for raw, hi, lo, n in ((raw_front, front_h, front_l, KD * 2 * FI), (raw_out, out_h, out_l, IB * D)):
                    split_on_pool(pool, chain, raw[:, 0:n], hi[:, 0:n], lo[:, 0:n], WS)
            return prefetch, prepare

        class MoeBuffers:
            pass

        def moe_buffers(where):
            def b(name, shape, dt=F32):
                return sb("moe_" + name, shape, dt, where)
            m, fw, ow = MoeBuffers(), KD * 2 * FI, IB * D
            m.raw_f = [b("raw_f", [P, fw])[:, :], raw_front[:, 0:fw]]
            m.wf_h = [b("wf_h", [P, fw], F16)[:, :], front_h[:, 0:fw]]
            m.wf_l = [b("wf_l", [P, fw], F16)[:, :], front_l[:, 0:fw]]
            m.raw_o = [raw_out[:, ow:2 * ow], raw_out[:, 0:ow]]
            m.wo_h = [out_h[:, ow:2 * ow], out_h[:, 0:ow]]
            m.wo_l = [out_l[:, ow:2 * ow], out_l[:, 0:ow]]
            m.rows = [b(f"rows{p}", [P, SH, 2 * D], F16) for p in range(2)]
            m.xth = [b(f"xth{p}", [P, KD, ST], F16) for p in range(2)]
            m.xtl = [b(f"xtl{p}", [P, KD, ST], F16) for p in range(2)]
            m.identh = b("identh", [P, P], F16)
            m.list = b("list", [P, COLS], U32)
            m.gate, m.bias, m.count = b("gate", [P, KD, NE]), b("bias", [P, NE]), b("count", [P, P])
            m.limits, m.spare = b("limits", [P, T // ST]), b("spare", [P, COLS + DUMMY])
            m.tile_no, m.part_no = b("tile_no", [P, TOPK * NT]), b("part_no", [P, 1])
            m.below, m.ones, m.lower = b("below", [P, NE, NE]), b("ones", [P, P], F16), b("lower", [P, P], F16)
            m.owner = b("owner", [1, NTILES + 2], U32)
            m.to = b("to", [P, COLS + DUMMY], U32)
            m.w4 = b("w4", [P, NT, TOPK])
            return m

        def expert_weights(sp, m, tile, par, s_rf, s_ro, front=True, outer=True):
            e = sp.value_load(m.owner[0:1, bass.ds(tile, 1)], min_val=0, max_val=NE - 1)
            if front:
                sp.dma_start(m.raw_f[par].rearrange("p (k n) -> p k n", k=KD),
                             egu[bass.ds(e * D, D), :].rearrange("(k p) n -> p k n", p=P)).then_inc(s_rf, 16)
            if outer:
                sp.dma_start(m.raw_o[par].rearrange("p (k n) -> p k n", k=IB),
                             ed[bass.ds(e * FI, FI), :].rearrange("(k p) n -> p k n", p=P)).then_inc(s_ro, 16)

        def gather_rows(pool, m, columns, par, s_rows):
            for h in range(SH):
                pool.indirect_dma_start(m.rows[par][:, h, :], None, xs[:, :],
                                        bass.IndirectOffsetOnAxis(columns[h], 0)).then_inc(s_rows, 16)

        def turn_rows(pe, m, par):
            for part in range(2):
                for h in range(SH):
                    for k in range(KD):
                        c = (k % 2) * ST + h * P
                        mm = pe.matmul(bank[4 + 2 * part + k // 2][:, c:c + P],
                                       m.rows[par][:, h, part * D + k * P:part * D + (k + 1) * P], m.identh[:, :],
                                       start=True, stop=True)
            return mm

        def turned(m, par, part, half):
            dst = (m.xth, m.xtl)[part][par][:, 2 * half:2 * half + 2, :]
            return dst, bank[4 + 2 * part + half][:, :].rearrange("p (k t) -> p k t", k=2)

        def route_and_shared(m):
            with ExitStack() as ctx:
                def b(name, shape, dt=F32):
                    return sb("ro_" + name, shape, dt, ctx)
                gh, gl = b("gh", [P, KD, NE], F16), b("gl", [P, KD, NE], F16)
                raw, bi, io, lim, bel = m.gate, m.bias, m.count, m.limits, m.below
                sg = b("sg", [P, NT, NE])
                top8, idx, idf = b("top8", [P, NT, 8]), b("idx", [P, NT, 8], U32), b("idf", [P, NT, 8])
                tot, rt = b("tot", [P, NT]), b("rt", [P, NT])
                pick = b("pick", [P, TOPK, NT, NE])
                where = b("where", [P, TOPK, NT, NE])
                chosen = b("chosen", [P, NT, NE], F16)
                before = b("before", [P, NT + 1, NE])
                more, till, start, end = b("more", [P, NE, T // ST]), b("till", [P, NE]), b("start", [P, NE]), b("end", [P, NE])
                prior, past, own = b("prior", [P, NE, NE]), b("past", [1, NTILES + 2, NE]), b("own", [1, NTILES + 2])
                slotf, col, row = b("slotf", [P, TOPK, NT]), b("col", [P, TOPK, NT]), b("row", [P, TOPK, NT])
                filled, empty, turn_no = b("filled", [P, COLS]), b("empty", [P, COLS]), b("turn_no", [P, COLS])
                NR = 8
                PLACES = TOPK * NT // NR
                at_row, at_col, part_at, tile_at = ([b(f"{w}{n}", [P, NR, c], F16) for n in range(2)] for w, c in
                                                    (("at_row", P), ("at_col", COLS), ("part_at", COLS), ("tile_at", COLS)))
                th = m.rows[1][:, :, :].rearrange("p h n -> p (h n)").rearrange("p (t n) -> p t n", t=TQ)
                tl = b("tl", [P, TQ, D], F16)
                sgl, z = raw_front[:, 2048:3072].rearrange("p (n t) -> p n t", n=IB), b("z", [P, IB, QT])
                zh, zl = b("zh", [P, IB, QT], F16), b("zl", [P, IB, QT], F16)
                wf_h, wf_l = (blocks(w, KD)(2 * FI) for w in (front_h, front_l))
                wo_h, wo_l = (blocks(w, IB)(D) for w in (out_h, out_l))
                s_g, s_v, s_x, s_rows, s_w = (sem("ro_" + n) for n in ("g", "v", "x", "rows", "w"))
                N0 = Step(None, 0)
                def quad(name, q, n):
                    return [f"{name}{q}.{k}" for k in range(n)]

                def place(*n):
                    return [f"place{k}" for k in n]
                assert PLACES == 8
                PE = Timeline(sem("ro_pe"), [], 0,
                              ["logits"] + quad("gu", 0, IB) + ["counts"] + quad("gu", 1, IB) + quad("y", 0, TQ) + place(0, 1)
                              + quad("y", 1, TQ) + place(2, 3) + ["gu2.0"] + place(4, 5) + ["gu2.1"] + place(6, 7)
                              + quad("y", 2, TQ) + quad("gu", 3, IB) + ["turn"] + quad("y", 3, TQ))
                shared_act = [[f"{w}{q}.{n}" for n in range(IB) for w in ("si", "zh")] for q in range(NQ)]
                AC = Timeline(sem("ro_act"), [], 0, ["th0", "sig"] + shared_act[0] + ["th1", "th2"] + shared_act[1]
                              + ["part0", "part1", "part2", "part3", "th3", "part4", "part5"] + shared_act[2][:2]
                              + ["part6", "part7"] + shared_act[2][2:] + ["wfh"] + shared_act[3] + ["xh0", "xh1"])
                DV = Timeline(sem("ro_dve"), [], 0,
                              ["split"] + quad("z", 0, IB) + ["chosen", "slots"] + quad("y", 0, TQ) + quad("z", 1, IB)
                              + ["col0", "row0", "col1", "row1"] + quad("y", 1, TQ)
                              + ["col2", "row2", "col3", "row3", "col4", "row4", "col5", "row5", "z2.0",
                                 "col6", "row6", "col7", "row7", "z2.1", "list"]
                              + quad("y", 2, TQ) + ["wfl"] + quad("z", 3, IB) + ["xl0", "xl1"] + quad("y", 3, TQ))
                PO = Timeline(sem("ro_pool"), [], 0, ["tl0"] + quad("zl", 0, IB) + ["tl1", "tl2"] + quad("zl", 1, IB)
                              + ["tile0", "tile1", "tile2", "tile3", "tile4", "tile5", "tl3", "zl2.0", "tile6", "tile7", "zl2.1"] + quad("zl", 3, IB))
                block = ctx.enter_context(nc.Block())

                def wait(eng, tl_, name):
                    eng.wait_ge(tl_.sem, tl_.value(name, N0))

                @block.sync
                def _(sp):
                    for q in range(NQ):
                        rows = xs[q * QT:(q + 1) * QT, :].rearrange("(t p) n -> p t n", p=P)
                        wait(sp, AC, f"th{q}")
                        sp.dma_start(rows[:, :, 0:D], th[:, :, :]).then_inc(s_x, 16)
                        wait(sp, PO, f"tl{q}")
                        sp.dma_start(rows[:, :, D:2 * D], tl[:, :, :]).then_inc(s_x, 16)
                    wait(sp, DV, "slots")
                    expert_weights(sp, m, 0, 0, s_w, s_w)
                    sp.wait_ge(s_w, 32)

                @block.gpsimd
                def _(pool):
                    chain = chained(pool, sem("ro_pool_chain"))
                    chain(pool.tensor_copy(m.identh[:, :], ident[:, :]))

                    def low_tokens(q):
                        wait(pool, AC, f"th{q}")
                        if q:
                            pool.wait_ge(s_x, 32 * q)
                        PO.mark(pool.tensor_tensor(tl[:, :, :], acc[:, q * TQ:(q + 1) * TQ, :], th, ALU.subtract), f"tl{q}", N0)

                    def low_part(q, n):
                        wait(pool, AC, f"zh{q}.{n}")
                        if q:
                            wait(pool, PE, f"y{q - 1}.3")
                        PO.mark(pool.tensor_tensor(zl[:, n, :], z[:, n, :], zh[:, n, :], ALU.subtract), f"zl{q}.{n}", N0)

                    def low_parts(q):
                        for n in range(IB):
                            low_part(q, n)

                    def tile_numbers(*groups):
                        for g in groups:
                            wait(pool, DV, f"col{g}")
                            no = m.tile_no[:, g * NR:(g + 1) * NR].rearrange("p (n a) -> p n a", a=1).to_broadcast([P, NR, COLS])
                            PO.mark(pool.tensor_tensor(tile_at[g % 2][:, :, :], at_col[g % 2][:, :, :], no, ALU.mult), f"tile{g}", N0)
                    low_tokens(0)
                    low_parts(0)
                    low_tokens(1)
                    low_tokens(2)
                    low_parts(1)
                    tile_numbers(0, 1, 2, 3, 4, 5)
                    low_tokens(3)
                    low_part(2, 0)
                    tile_numbers(6, 7)
                    low_part(2, 1)
                    pool.wait_ge(s_x, 32 * NQ)
                    wait(pool, DV, "list")
                    gather_rows(pool, m, [m.list[:, h:h + 1] for h in range(SH)], 0, s_rows)
                    low_parts(3)
                    pool.wait_ge(s_rows, 16 * SH)

                @block.scalar
                def _(act):
                    def high_tokens(q):
                        if q:
                            act.wait_ge(s_x, 32 * q)
                            wait(act, PO, f"tl{q - 1}")
                        AC.mark(act.activation(th, acc[:, q * TQ:(q + 1) * TQ, :], ACT.Copy), f"th{q}", N0)

                    def part_numbers(*groups):
                        for g in groups:
                            wait(act, DV, f"col{g}")
                            AC.mark(act.activation(part_at[g % 2][:, :, :], at_col[g % 2][:, :, :], ACT.Copy,
                                                   scale=m.part_no[:, 0:1]), f"part{g}", N0)

                    def shared(q, blocks_of=range(IB)):
                        for n in blocks_of:
                            wait(act, PE, f"gu{q}.{n}")
                            if q:
                                wait(act, DV, f"z{q - 1}.{n}")
                            AC.mark(act.activation(sgl[:, n, :], bank[2 + 2 * n][:, :], ACT.Silu, scale=1 / WS), f"si{q}.{n}", N0)
                            wait(act, DV, f"z{q}.{n}")
                            if q:
                                wait(act, PE, f"y{q - 1}.3")
                            AC.mark(act.activation(zh[:, n, :], z[:, n, :], ACT.Copy), f"zh{q}.{n}", N0)
                    high_tokens(0)
                    wait(act, PE, "logits")
                    AC.mark(act.activation(sg[:, :, :].rearrange("p t e -> p (t e)"), bank[0][:, 0:NT * NE], ACT.Exp,
                                           scale=-1 / WS), "sig", N0)
                    shared(0)
                    high_tokens(1)
                    high_tokens(2)
                    shared(1)
                    part_numbers(0, 1, 2, 3)
                    high_tokens(3)
                    part_numbers(4, 5)
                    shared(2, [0])
                    part_numbers(6, 7)
                    shared(2, [1])
                    act.wait_ge(s_w, 32)
                    AC.mark(act.activation(m.wf_h[0], m.raw_f[0], ACT.Copy, scale=WS), "wfh", N0)
                    shared(3)
                    wait(act, PE, "turn")
                    for half in range(2):
                        dst, src = turned(m, 0, 0, half)
                        AC.mark(act.activation(dst, src, ACT.Copy), f"xh{half}", N0)

                @block.vector
                def _(dve):
                    n_ = [0]

                    def then(i):
                        n_[0] += 1
                        i.then_inc(s_v, 1)
                        dve.wait_ge(s_v, n_[0])

                    def product(q, n):
                        wait(dve, AC, f"si{q}.{n}")
                        if q:
                            wait(dve, PO, f"zl{q - 1}.{n}")
                        DV.mark(dve.scalar_tensor_tensor(z[:, n, :], bank[3 + 2 * n][:, :], OS / WS, sgl[:, n, :],
                                                         ALU.mult, ALU.mult), f"z{q}.{n}", N0)

                    def products(q):
                        for n in range(IB):
                            product(q, n)

                    def one_hot(out, values, g):
                        shape = [P, NR, out.shape[2]]
                        v = values[:, :, :].rearrange("p j t -> p (j t)")[:, g * NR:(g + 1) * NR]
                        return dve.tensor_tensor(out[:, :, :], io[:, 0:shape[2]].rearrange("p (a c) -> p a c", a=1).to_broadcast(shape),
                                                 v.rearrange("p (n a) -> p n a", a=1).to_broadcast(shape), ALU.is_equal)

                    def locate(*groups):
                        for g in groups:
                            if g >= 2:
                                wait(dve, PE, f"place{g - 2}")
                            DV.mark(one_hot(at_col[g % 2], col, g), f"col{g}", N0)
                            DV.mark(one_hot(at_row[g % 2], row, g), f"row{g}", N0)

                    def add(q):
                        for t in range(TQ):
                            wait(dve, PE, f"y{q}.{t}")
                            DV.mark(dve.scalar_tensor_tensor(acc[:, q * TQ + t, :], bank[6 + t % 2][:, :], 1 / (WS * OS),
                                                             acc[:, q * TQ + t, :], ALU.mult, ALU.add), f"y{q}.{t}", N0)
                    tall = [P, NT, NE]
                    dve.tensor_scalar(gh[:, :, :], raw[:, :, :], WS, None, ALU.mult).then_inc(s_g, 1)
                    dve.wait_ge(s_g, 1)
                    DV.mark(dve.scalar_tensor_tensor(gl[:, :, :].rearrange("p k n -> p (k n)"), raw[:, :, :].rearrange("p k n -> p (k n)"),
                                                     WS, gh[:, :, :].rearrange("p k n -> p (k n)"), ALU.mult, ALU.subtract), "split", N0)
                    wait(dve, AC, "sig")
                    then(dve.tensor_scalar(sg[:, :, :], sg[:, :, :], 1.0, None, ALU.add))
                    then(dve.reciprocal(sg[:, :, :], sg[:, :, :]))
                    then(dve.tensor_tensor(sg[:, :, :], sg[:, :, :], bi[:, :].rearrange("p (a e) -> p a e", a=1)
                                           .to_broadcast(tall), ALU.add))
                    for t in range(NT):
                        i = dve.max(top8[:, t, :], sg[:, t, :])
                    then(i)
                    for t in range(NT):
                        i = dve.max_index(idx[:, t, :], top8[:, t, :], sg[:, t, :])
                    then(i)
                    dve.tensor_reduce(tot[:, :], top8[:, :, 0:TOPK], AX.X, ALU.add)
                    then(dve.tensor_copy(idf[:, :, :], idx[:, :, :]))
                    for j in range(TOPK):
                        i = dve.tensor_tensor(pick[:, j, :, :], io[:, 0:NE].rearrange("p (a e) -> p a e", a=1).to_broadcast(tall),
                                              idf[:, :, j:j + 1].to_broadcast(tall), ALU.is_equal)
                    then(dve.tensor_scalar(tot[:, :], tot[:, :], 1e-20, None, ALU.add))
                    for j in range(2):
                        i = dve.tensor_tensor(where[:, j, :, :], pick[:, 2 * j, :, :], pick[:, 2 * j + 1, :, :], ALU.add)
                    then(dve.reciprocal(rt[:, :], tot[:, :]))
                    products(0)
                    DV.mark(dve.tensor_tensor(chosen[:, :, :], where[:, 0, :, :], where[:, 1, :, :], ALU.add), "chosen", N0)
                    dve.scalar_tensor_tensor(m.w4[:, :, :], top8[:, :, 0:TOPK], 1 / (WS * OS),
                                             rt[:, :].rearrange("p (t a) -> p t a", a=1).to_broadcast([P, NT, TOPK]),
                                             ALU.mult, ALU.mult)
                    then(dve.memset(before[:, 0, :], 0.0))
                    wait(dve, PE, "counts")
                    for t in range(NT):
                        then(dve.tensor_tensor(before[:, t + 1, :], bank[1][:, 256 + t * NE:256 + (t + 1) * NE], before[:, t, :], ALU.add))
                    ex = before[:, NT, :].rearrange("p (e a) -> p e a", a=1).to_broadcast([P, NE, T // ST])
                    then(dve.tensor_tensor(more[:, :, :], ex, lim[:, :].rearrange("p (a k) -> p a k", a=1)
                                           .to_broadcast([P, NE, T // ST]), ALU.is_gt))
                    then(dve.tensor_reduce(till[:, :], more[:, :, :], AX.X, ALU.add))
                    then(dve.tensor_tensor(prior[:, :, :], bel[:, :, :], till[:, :].rearrange("p (a e) -> p a e", a=1)
                                           .to_broadcast([P, NE, NE]), ALU.mult))
                    then(dve.tensor_reduce(start[:, :], prior[:, :, :], AX.X, ALU.add))
                    dve.tensor_tensor(end[:, :], start[:, :], till[:, :], ALU.add)
                    then(dve.tensor_scalar(start[:, :], start[:, :], float(ST), None, ALU.mult))
                    wide = [1, NTILES + 2, NE]
                    dve.tensor_tensor(past[:, :, :], io[0:1, 0:NTILES + 2].rearrange("p (n a) -> p n a", a=1).to_broadcast(wide),
                                      end[0:1, :].rearrange("p (a e) -> p a e", a=1).to_broadcast(wide), ALU.is_ge)
                    then(dve.tensor_tensor(sg[:, :, :], before[:, 0:NT, :], start[:, :].rearrange("p (a e) -> p a e", a=1)
                                           .to_broadcast(tall), ALU.add))
                    dve.tensor_reduce(own[:, :], past[:, :, :], AX.X, ALU.add)
                    then(dve.tensor_tensor(sg[:, :, :], sg[:, :, :], bank[1][:, 0:256].rearrange("p (t e) -> p t e", e=NE), ALU.add))
                    dve.tensor_scalar(m.owner[:, :], own[:, :], float(NE - 1), None, ALU.min)
                    for j in range(TOPK):
                        i = dve.tensor_tensor(where[:, j, :, :], pick[:, j, :, :], sg[:, :, :], ALU.mult)
                    then(i)
                    then(dve.tensor_reduce(slotf[:, :, :].rearrange("p j t -> p (j t)"),
                                           where[:, :, :, :].rearrange("p j t e -> p (j t) e"), AX.X, ALU.add))
                    def floor_of_quotient(out, x, d):
                        then(dve.tensor_scalar(out, x, 1 / d, -(d - 1) / (2 * d), ALU.mult, ALU.add))
                        then(dve.tensor_scalar(out, out, ROUND, None, ALU.add))
                        then(dve.tensor_scalar(out, out, ROUND, None, ALU.subtract))
                    floor_of_quotient(col[:, :, :], slotf[:, :, :], P)
                    DV.mark(dve.scalar_tensor_tensor(row[:, :, :].rearrange("p j t -> p (j t)"), col[:, :, :].rearrange("p j t -> p (j t)"),
                                                     -float(P), slotf[:, :, :].rearrange("p j t -> p (j t)"),
                                                     ALU.mult, ALU.add), "slots", N0)
                    wait(dve, DV, "slots")
                    add(0)
                    products(1)
                    locate(0, 1)
                    add(1)
                    locate(2, 3, 4, 5)
                    product(2, 0)
                    locate(6, 7)
                    product(2, 1)
                    wait(dve, PE, f"place{PLACES - 1}")
                    then(dve.tensor_scalar(filled[:, :], bank[0][:, 0:COLS], -1.0, 0.0, ALU.add, ALU.max))
                    then(dve.tensor_scalar(empty[:, :], bank[0][:, 0:COLS], 0.0, None, ALU.is_equal))
                    floor_of_quotient(turn_no[:, :], filled[:, :], T)
                    dve.tensor_tensor(empty[:, :], empty[:, :], m.spare[:, DUMMY:], ALU.mult)
                    dve.tensor_copy(m.to[:, 0:DUMMY], m.spare[:, 0:DUMMY])
                    then(dve.scalar_tensor_tensor(turn_no[:, :], turn_no[:, :], -float(T), filled[:, :], ALU.mult, ALU.add))
                    dve.tensor_tensor(m.to[:, DUMMY:], empty[:, :], filled[:, :], ALU.add)
                    DV.mark(dve.tensor_copy(m.list[:, :], turn_no[:, :]), "list", N0)
                    add(2)
                    wait(dve, AC, "wfh")
                    DV.mark(dve.scalar_tensor_tensor(m.wf_l[0], m.raw_f[0], WS, m.wf_h[0], ALU.mult, ALU.subtract),
                            "wfl", N0)
                    products(3)
                    wait(dve, PE, "turn")
                    for half in range(2):
                        dst, src = turned(m, 0, 1, half)
                        DV.mark(dve.tensor_copy(dst, src), f"xl{half}", N0)
                    add(3)

                @block.tensor
                def _(pe):
                    def place_picks(*groups):
                        for g in groups:
                            wait(pe, PO, f"tile{g}")
                            wait(pe, AC, f"part{g}")
                            wait(pe, DV, f"row{g}")
                            for n in range(NR):
                                pe.matmul(bank[0][:, 0:COLS], at_row[g % 2][:, n, :], tile_at[g % 2][:, n, :],
                                          start=g == 0 and n == 0, stop=False)
                                mm = pe.matmul(bank[0][:, 0:COLS], at_row[g % 2][:, n, :], part_at[g % 2][:, n, :],
                                               start=False, stop=g == PLACES - 1 and n == NR - 1)
                            PE.mark(mm, f"place{g}", N0)

                    def front(q, blocks_of=range(IB)):
                        tok = slice(q * QT, (q + 1) * QT)
                        for n in blocks_of:
                            if q:
                                wait(pe, DV, f"z{q - 1}.{n}")
                            for u in range(2):
                                c = u * FI + n * P
                                mm = three_pass(pe, bank[2 + 2 * n + u][:, :],
                                                [(wf_h[:, k, c:c + P], wf_l[:, k, c:c + P], xh[:, k, tok], xl[:, k, tok])
                                                 for k in range(KD)])
                            PE.mark(mm, f"gu{q}.{n}", N0)

                    def back(q):
                        wait(pe, PO, f"zl{q}.1")
                        for t in range(TQ):
                            if t >= 2:
                                wait(pe, DV, f"y{q}.{t - 2}")
                            elif q:
                                wait(pe, DV, f"y{q - 1}.{t + 2}")
                            if q == NQ - 1 and t < 2:
                                wait(pe, DV, "xl1")
                            tok = slice(t * P, (t + 1) * P)
                            PE.mark(three_pass(pe, bank[6 + t % 2][:, :], [(zh[:, n, tok], zl[:, n, tok], wo_h[:, n, :], wo_l[:, n, :])
                                                                           for n in range(IB)]), f"y{q}.{t}", N0)
                    wait(pe, DV, "split")
                    for t in range(NT):
                        tok = slice(t * P, (t + 1) * P)
                        mm = three_pass(pe, bank[0][:, t * NE:(t + 1) * NE],
                                        [(xh[:, k, tok], xl[:, k, tok], gh[:, k, :], gl[:, k, :]) for k in range(KD)])
                    PE.mark(mm, "logits", N0)
                    front(0)
                    wait(pe, DV, "chosen")
                    taken = chosen[:, :, :].rearrange("p t e -> p (t e)")
                    pe.matmul(bank[1][:, 0:256], m.lower[:, :], taken, start=True, stop=True)
                    PE.mark(pe.matmul(bank[1][:, 256:512], m.ones[:, :], taken, start=True, stop=True), "counts", N0)
                    front(1)
                    back(0)
                    place_picks(0, 1)
                    back(1)
                    place_picks(2, 3)
                    front(2, [0])
                    place_picks(4, 5)
                    front(2, [1])
                    place_picks(6, 7)
                    back(2)
                    front(3)
                    pe.wait_ge(s_rows, 16 * SH)
                    wait(pe, DV, "z3.1")
                    wait(pe, DV, "y2.3")
                    PE.mark(turn_rows(pe, m, 0), "turn", N0)
                    back(3)

        def experts(m):
            NR, U = NTILES // 2, 2
            with ExitStack() as ctx:
                def b(name, shape, dt=F32):
                    return sb("mo_" + name, shape, dt, ctx)
                sg, z = b("sg", [P, IB, ST]), b("z", [P, IB, ST])
                zh = [b(f"zh{j}", [P, IB, ST], F16) for j in range(2)]
                zl = [b(f"zl{j}", [P, IB, ST], F16) for j in range(2)]
                yo = [b(f"yo{j}", [P, SH, D]) for j in range(2)]
                cols = [b(f"cols{j}", [P, SH], U32) for j in range(2)]
                rows_to = [b(f"rows_to{j}", [P, SH], U32) for j in range(2)]
                s_rf, s_ro, s_rows, s_yo = ([sem(f"mo_{n}{j}") for j in range(2)] for n in ("rf", "ro", "rows", "yo"))
                PE = Timeline(sem("mo_pe"), events(["gu0", "gu1", "turn", "y0", "y1"], steps=U), NR, ["y0", "y1"], U)
                AC = Timeline(sem("mo_act"), events(["woh", "si0", "wfh", "si1", "xh0", "xh1", "y0"], steps=U), NR, ["y0"], U)
                DV = Timeline(sem("mo_dve"), events(["z0", "wol", "wfl", "z1", "xl0", "xl1", "y1"], steps=U), NR, ["y1"], U)
                PO = Timeline(sem("mo_pool"), events(["to", "cols", "zh0", "zl0", "zh1", "zl1"], steps=U), NR, ["to0", "to1"], U)
                wf = [[w.rearrange("p (k n) -> p k n", k=KD) for w in (m.wf_h[p], m.wf_l[p])] for p in range(2)]
                wo = [[w.rearrange("p (k n) -> p k n", k=IB) for w in (m.wo_h[p], m.wo_l[p])] for p in range(2)]
                block = ctx.enter_context(nc.Block())

                @block.sync
                def _(sp):
                    for s in (s_rf[0], s_ro[0]):
                        sp.sem_inc(s, 16)
                    expert_weights(sp, m, 1, 1, s_rf[1], s_ro[1])
                    with sp.Fori(0, NR) as i:
                        for q in range(U):
                            st, tile = Step(i, q), i * U + q + 2
                            sp.wait_ge(DV.sem, DV.value("wfl", st, 1))
                            met(sp)
                            expert_weights(sp, m, tile, q, s_rf[q], None, outer=False)
                            sp.wait_ge(DV.sem, DV.value("wol", st))
                            met(sp)
                            expert_weights(sp, m, tile, q, None, s_ro[q], front=False)
                    for j in range(2):
                        sp.wait_ge(s_rf[j], 16 * (NR + 1))
                        sp.wait_ge(s_ro[j], 16 * (NR + 1))

                @block.gpsimd
                def _(pool):
                    s_zero = sem("mo_zero")
                    gather_rows(pool, m, [m.list[:, SH + h:SH + h + 1] for h in range(SH)], 1, s_rows[1])
                    pool.memset(zh[1][:], 0.0)
                    pool.memset(zl[1][:], 0.0).then_inc(s_zero, 1)
                    pool.memset(yo[0][:, :, :], 0.0)
                    pool.memset(yo[1][:, :, :], 0.0).then_inc(s_zero, 1)
                    pool.wait_ge(s_zero, 2)

                    def scatter(par, columns):
                        for h in range(SH):
                            pool.indirect_dma_start(ys[:, :], bass.IndirectOffsetOnAxis(columns[:, h:h + 1], 0), yo[par][:, h, :],
                                                    None).then_inc(s_yo[par], 16)

                    def store(st, par, first, evacuated):
                        pool.wait_ge(s_yo[par], (st.i if st.i is not None else NR) * (16 * SH) + 16 * SH)
                        met(pool)
                        name = "to" if st.i is not None else f"to{par}"
                        PO.mark(pool.tensor_copy(rows_to[par][:, :], m.to[:, bass.ds(first, SH)]), name, st)
                        pool.wait_ge(PO.sem, PO.value(name, st))
                        pool.wait_ge(AC.sem, AC.value("y0", st, evacuated))
                        pool.wait_ge(DV.sem, DV.value("y1", st, evacuated))
                        met(pool)
                        scatter(par, rows_to[par])
                    for par in range(2):
                        scatter(par, m.to[:, par * SH:(par + 1) * SH])
                    PO.start(pool)
                    with pool.Fori(0, NR) as i:
                        for q in range(U):
                            st = Step(i, q)
                            store(st, q, (i * U + q + 2) * SH, 1)
                            pool.wait_ge(PE.sem, PE.value("turn", st, 1))
                            met(pool)
                            PO.mark(pool.tensor_copy(cols[q][:, :], m.list[:, bass.ds((i * U + q + 2) * SH, SH)]), "cols", st)
                            pool.wait_ge(PO.sem, PO.value("cols", st))
                            met(pool)
                            gather_rows(pool, m, [cols[q][:, h:h + 1] for h in range(SH)], q, s_rows[q])
                            for n in range(IB):
                                pool.wait_ge(DV.sem, DV.value(f"z{n}", st))
                                pool.wait_ge(PE.sem, PE.value("y1", st, 1))
                                met(pool)
                                PO.mark(pool.tensor_copy(zh[q][:, n, :], z[:, n, :]), f"zh{n}", st)
                                pool.wait_ge(PO.sem, PO.value(f"zh{n}", st))
                                PO.mark(pool.tensor_tensor(zl[q][:, n, :], z[:, n, :], zh[q][:, n, :], ALU.subtract), f"zl{n}", st)
                    for par in range(2):
                        store(Step(None, 0), par, (NTILES + par + 2) * SH, 1 - par)
                    for j in range(2):
                        pool.wait_ge(s_rows[j], 16 * SH * (NR + j))
                        pool.wait_ge(s_yo[j], 16 * SH * (NR + 2))

                def stored(eng, st, i):
                    eng.wait_ge(s_yo[(st.q + 1) % 2], (i if st.i is not None else NR) * (16 * SH) + 16 * SH * (1 + st.q))

                @block.scalar
                def _(act):
                    AC.start(act)

                    def out_half(st, i):
                        act.wait_ge(PE.sem, PE.value("y0", st))
                        stored(act, st, i)
                        AC.mark(act.activation(yo[(st.q + 1) % 2][:, 0, :], bank[2][:, :], ACT.Copy), "y0", st)
                    with act.Fori(0, NR) as i:
                        for q in range(U):
                            st, nx = Step(i, q), (q + 1) % 2
                            act.wait_ge(s_ro[q], i * 16 + 16)
                            act.wait_ge(PE.sem, PE.value("y1", st, 1))
                            AC.mark(act.activation(m.wo_h[q], m.raw_o[q], ACT.Copy, scale=WS), "woh", st)
                            for n in range(IB):
                                act.wait_ge(PE.sem, PE.value(f"gu{n}", st))
                                act.wait_ge(DV.sem, DV.value(f"z{n}", st, 1))
                                AC.mark(act.activation(sg[:, n, :], bank[n][:, 0:ST], ACT.Silu, scale=1 / WS), f"si{n}", st)
                                if n == 0:
                                    act.wait_ge(s_rf[nx], i * 16 + 16 * (1 + (q + 1) // 2))
                                    act.wait_ge(PE.sem, PE.value("gu1", st, 1))
                                    AC.mark(act.activation(m.wf_h[nx], m.raw_f[nx], ACT.Copy, scale=WS), "wfh", st)
                            act.wait_ge(PE.sem, PE.value("turn", st))
                            for half in range(2):
                                dst, src = turned(m, nx, 0, half)
                                AC.mark(act.activation(dst, src, ACT.Copy), f"xh{half}", st)
                            out_half(st, i)
                    out_half(Step(None, 0), None)

                @block.vector
                def _(dve):
                    DV.start(dve)

                    def out_half(st, i):
                        dve.wait_ge(PE.sem, PE.value("y1", st))
                        stored(dve, st, i)
                        DV.mark(dve.tensor_copy(yo[(st.q + 1) % 2][:, 1, :], bank[3][:, :]), "y1", st)
                    with dve.Fori(0, NR) as i:
                        for q in range(U):
                            st, nx = Step(i, q), (q + 1) % 2

                            def product(n):
                                dve.wait_ge(AC.sem, AC.value(f"si{n}", st))
                                dve.wait_ge(PO.sem, PO.value(f"zl{n}", st, 1))
                                DV.mark(dve.scalar_tensor_tensor(z[:, n, :], bank[n][:, ST:2 * ST], OS / WS, sg[:, n, :],
                                                                 ALU.mult, ALU.mult), f"z{n}", st)
                            product(0)
                            dve.wait_ge(AC.sem, AC.value("woh", st))
                            DV.mark(dve.scalar_tensor_tensor(m.wo_l[q], m.raw_o[q], WS, m.wo_h[q], ALU.mult, ALU.subtract), "wol", st)
                            dve.wait_ge(AC.sem, AC.value("wfh", st))
                            DV.mark(dve.scalar_tensor_tensor(m.wf_l[nx], m.raw_f[nx], WS, m.wf_h[nx], ALU.mult, ALU.subtract), "wfl", st)
                            product(1)
                            dve.wait_ge(PE.sem, PE.value("turn", st))
                            for half in range(2):
                                dst, src = turned(m, nx, 1, half)
                                DV.mark(dve.tensor_copy(dst, src), f"xl{half}", st)
                            out_half(st, i)
                    out_half(Step(None, 0), None)

                @block.tensor
                def _(pe):
                    PE.start(pe)

                    def back_out(st):
                        par = (st.q + 1) % 2
                        pe.wait_ge(PO.sem, PO.value("zl1", st, 1))
                        pe.wait_ge(DV.sem, DV.value("wol", st, 1))
                        for h in range(SH):
                            if h == 0:
                                pe.wait_ge(AC.sem, AC.value("y0", st, 1))
                            else:
                                pe.wait_ge(DV.sem, DV.value("y1", st, 1))
                            tok = slice(h * P, (h + 1) * P)
                            PE.mark(three_pass(pe, bank[2 + h][:, :], [(zh[par][:, n, tok], zl[par][:, n, tok], wo[par][0][:, n, :],
                                                                        wo[par][1][:, n, :]) for n in range(IB)]), f"y{h}", st)

                    with pe.Fori(0, NR) as i:
                        for q in range(U):
                            st, nx = Step(i, q), (q + 1) % 2
                            pe.wait_ge(DV.sem, DV.value("xl1", st, 1))
                            pe.wait_ge(AC.sem, AC.value("xh1", st, 1))
                            for n in range(IB):
                                pe.wait_ge(DV.sem, DV.value(f"z{n}", st, 1))
                                for u in range(2):
                                    c = u * FI + n * P
                                    mm = three_pass(pe, bank[n][:, u * ST:(u + 1) * ST],
                                                    [(wf[q][0][:, k, c:c + P], wf[q][1][:, k, c:c + P], m.xth[q][:, k, :],
                                                      m.xtl[q][:, k, :]) for k in range(KD)])
                                PE.mark(mm, f"gu{n}", st)
                            pe.wait_ge(s_rows[nx], i * (16 * SH) + 16 * SH)
                            PE.mark(turn_rows(pe, m, nx), "turn", st)
                            back_out(st)
                    back_out(Step(None, 0))

        def combine_and_normalise(m):
            with ExitStack() as ctx:
                rows = [sb(f"co_rows{q}", [P, TOPK, D], F32, ctx) for q in range(TQ)]
                st_ = [sb(f"co_st{q}", [P, 6], F32, ctx) for q in range(TQ)]
                mv_ = [sb(f"co_mv{q}", [P, 2], F32, ctx) for q in range(TQ)]
                rs_ = [sb(f"co_rs{q}", [P, 1], F32, ctx) for q in range(TQ)]
                part = [[sb(f"co_part{h}_{q}", [P, D], F32, ctx) for q in range(2)] for h in range(2)]
                res = [sb(f"co_res{q}", [P, D], F32, ctx) for q in range(TQ)]
                s_rows, s_out = [sem(f"co_rows{q}") for q in range(TQ)], [sem(f"co_out{q}") for q in range(TQ)]
                DV = Timeline(sem("co_dve"), events(["add0", "stats", "add1", "agg", "add2", "inv", "norm"]), NQ, ["stats", "agg", "inv", "norm"])
                AC = Timeline(sem("co_act"), events(["part0", "part1", "sqrt"]), NQ, ["sqrt"])
                PO = Timeline(sem("co_pool"), events(["sum"]), NQ)
                block = ctx.enter_context(nc.Block())

                @block.sync
                def _(sp):
                    def load(q, tile):
                        sp.dma_start(rows[q][:, :, :], ys[0:PICKS, :].rearrange("(j t) d -> t j d", j=TOPK)[bass.ds(tile * P, P), :, :]
                                     ).then_inc(s_rows[q], 16)

                    def store(st, tile):
                        q = (st.q - 1) % TQ if st.i is not None else TQ - 1
                        sp.wait_ge(DV.sem, DV.value("norm", st))
                        met(sp)
                        sp.dma_start(out[bass.ds(tile * P, P), :], res[q][:, :]).then_inc(s_out[q], 16)
                    for q in range(TQ):
                        load(q, q)
                        sp.sem_inc(s_out[q], 16)
                    with sp.Fori(0, NQ) as i:
                        for q in range(TQ):
                            st = Step(i, q)
                            sp.wait_ge(DV.sem, DV.value("add1", st))
                            met(sp)
                            sp.wait_ge(AC.sem, AC.value("part1", st))
                            met(sp)
                            load(q, (i * TQ + q + TQ) % NT)
                            store(st, (i * TQ + q + NT - 1) % NT)
                    store(Step(None, 0), NT - 1)
                    for q in range(TQ):
                        sp.wait_ge(s_rows[q], 16 * (NQ + 1))
                        sp.wait_ge(s_out[q], 16 * (NQ + 1 + (q == TQ - 1)))

                @block.gpsimd
                def _(pool):
                    PO.start(pool)
                    with pool.Fori(0, NQ) as i:
                        for q in range(TQ):
                            st = Step(i, q)
                            pool.wait_ge(AC.sem, AC.value("part1", st))
                            PO.mark(pool.tensor_tensor(part[0][q % 2][:, :], part[0][q % 2][:, :], part[1][q % 2][:, :], ALU.add), "sum", st)

                @block.scalar
                def _(act):
                    def root(st):
                        q = (st.q - 1) % TQ if st.i is not None else TQ - 1
                        act.wait_ge(DV.sem, DV.value("agg", st))
                        AC.mark(act.activation(rs_[q][:, :], mv_[q][:, 1:2], ACT.Sqrt, bias=eps[:, :]), "sqrt", st)
                    AC.start(act)
                    with act.Fori(0, NQ) as i:
                        for q in range(TQ):
                            st = Step(i, q)
                            act.wait_ge(s_rows[q], i * 16 + 16)
                            act.wait_ge(DV.sem, DV.value("add2", st, 2))
                            act.wait_ge(PO.sem, PO.value("sum", st, 2))
                            for h in range(2):
                                AC.mark(act.activation(part[h][q % 2][:, :], rows[q][:, 2 + h, :], ACT.Copy,
                                                       scale=m.w4[:, i * TQ + q, 2 + h:3 + h]), f"part{h}", st)
                            root(st)
                    root(Step(None, 0))

                @block.vector
                def _(dve):
                    DV.start(dve)

                    def own(name, st, back=0):
                        dve.wait_ge(DV.sem, DV.value(name, st, back))

                    def before(st):
                        return (st.q - 1) % TQ if st.i is not None else TQ - 1

                    def stats(st, tile):
                        own("add2", st, 1)
                        met(dve)
                        DV.mark(dve.bn_stats(st_[before(st)][:, :], acc[:, tile, :]), "stats", st)

                    def aggregate(st):
                        own("stats", st)
                        met(dve)
                        DV.mark(dve.bn_aggr(mv_[before(st)][:, :], st_[before(st)][:, :]), "agg", st)

                    def normalise(st, tile):
                        q = before(st)
                        dve.wait_ge(AC.sem, AC.value("sqrt", st))
                        DV.mark(dve.reciprocal(rs_[q][:, :], rs_[q][:, :]), "inv", st)
                        own("inv", st)
                        dve.wait_ge(s_out[q], st.i * 16 + 16 if st.i is not None else 16 * (NQ + 1))
                        DV.mark(dve.tensor_scalar(res[q][:, :], acc[:, tile, :], mv_[q][:, 0:1], rs_[q][:, 0:1],
                                                  ALU.subtract, ALU.mult), "norm", st)
                    with dve.Fori(0, NQ) as i:
                        for q in range(TQ):
                            st, tile, last_tile = Step(i, q), i * TQ + q, (i * TQ + q + NT - 1) % NT

                            def add(j):
                                DV.mark(dve.scalar_tensor_tensor(acc[:, tile, :], rows[q][:, j, :], m.w4[:, tile, j:j + 1], acc[:, tile, :],
                                                                 ALU.mult, ALU.add), f"add{j}", st)
                            dve.wait_ge(s_rows[q], i * 16 + 16)
                            add(0)
                            stats(st, last_tile)
                            own("add0", st)
                            add(1)
                            aggregate(st)
                            own("add1", st)
                            dve.wait_ge(PO.sem, PO.value("sum", st))
                            DV.mark(dve.tensor_tensor(acc[:, tile, :], acc[:, tile, :], part[0][q % 2][:, :], ALU.add), "add2", st)
                            normalise(st, last_tile)
                    done = Step(None, 0)
                    stats(done, NT - 1)
                    aggregate(done)
                    normalise(done, NT - 1)

        def first_group(tag, loads, front):
            s_w, s_c = sem(f"{tag}_w0"), sem(f"{tag}_w0_chain")

            def prefetch(sp):
                for dst, src in loads:
                    sp.dma_start(dst, src).then_inc(s_w, 16)

            def prepare(pool):
                chain = chained(pool, s_c)
                pool.memset(out_h[:, :], 0.0)
                chain(pool.memset(out_l[:, :], 0.0))
                pool.wait_ge(s_w, 16 * len(loads))
                split_on_pool(pool, chain, raw_front[:, 0:front], front_h[:, 0:front], front_l[:, 0:front], WS)
            return prefetch, prepare

        with ExitStack() as held:
            ch, cl = sb("ch", [P, KD, T], F16, held), sb("cl", [P, KD, T], F16, held)
            bound = sb("bound", [P, B, S], F32, held)

            def mask_bound(pool):
                s_m, chain = sem("mask_in"), chained(pool, sem("mask_chain"))
                for h in range(2):
                    pool.dma_start(bound[64 * h:64 * h + 64, :, :], maskf.rearrange("b q k -> q b k")).then_inc(s_m, 16)
                pool.wait_ge(s_m, 32)
                bd = bound[:, :, :].rearrange("p b k -> p (b k)")
                chain(pool.tensor_scalar(bd, bd, 0.0, 0.0, ALU.is_equal, ALU.is_equal))
                chain(pool.tensor_scalar(bd, bd, BIG, -1e9 * float(HD2) ** 0.5, ALU.mult, ALU.add))

            self_attention(mask_bound)
            fw = (GQ + 2) * HD2
            wf = blocks(raw_front, KD)(fw)
            loads, c = [], 0
            for w, n in ((xwq, GQ * HD2), (xwk, HD2), (xwv, HD2)):
                loads.append((wf[:, :, c:c + n], w.rearrange("(k p) n -> p k n", p=P)[:, :, 0:n]))
                c += n
            layernorm("ln1", *first_group("xa", loads, KD * fw))
            cross_attention()
        with ExitStack() as held:
            shared = moe_buffers(held)
            layernorm("ln2", *shared_weights(shared))
            route_and_shared(shared)
            experts(shared)
            combine_and_normalise(shared)


def kernel(**inputs):
    import numpy as np
    import concourse.bacc as bacc
    from concourse.bass_utils import run_bass_kernel_spmd

    f = {k: np.asarray(v) for k, v in inputs.items()}
    x = f["x"].reshape(T, D)
    half = HD2 // 2
    inv = (np.float32(1.0) / np.power(np.float32(10000.0), np.arange(0, HD2, 2, dtype=np.float32) / np.float32(HD2))).astype(np.float32)
    ang = (np.arange(S, dtype=np.float32)[None, :] * inv[:, None]).astype(np.float32)
    cos, sin = np.cos(ang) / np.float32(WS), np.sin(ang) / np.float32(WS)
    pos = np.arange(P) % S
    arrays = {
        "x": x,
        "xT": x.T,
        "cT": f["ctx_4096"].reshape(T, D).T,
        "maskf": f["mask_BxSxS2_ff1"],
        "wqT": f["L0_attn_Wq"].T, "bq": f["L0_attn_bq"],
        "wkT": f["L0_attn_Wk"].T, "bk": f["L0_attn_bk"],
        "wvT": f["L0_attn_Wv"].T, "bv": f["L0_attn_bv"],
        "woT": f["L0_attn_Wo"].T, "bo": f["L0_attn_bo"],
        "xwq": f["L0_xattn_wq"], "xwk": f["L0_xattn_wk"], "xwv": f["L0_xattn_wv"], "xwo": f["L0_xattn_wo"],
        "gwT": f["L0_ffn_gate_w"].T, "gbias": f["L0_ffn_bias"],
        "egu": np.concatenate([np.concatenate([f["L0_ffn_Wg"], f["L0_ffn_Sg"][None]]).transpose(0, 2, 1),
                               np.concatenate([f["L0_ffn_Wu"], f["L0_ffn_Su"][None]]).transpose(0, 2, 1)], axis=2)
        .reshape((NE + 1) * D, 2 * FI),
        "ed": np.concatenate([f["L0_ffn_Wd"], f["L0_ffn_Sd"][None]]).transpose(0, 2, 1).reshape((NE + 1) * FI, D),
        "causal": np.where(np.arange(S)[None, :] <= pos[:, None], np.float32(BIG), np.float32(-1e30)).astype(np.float32),
        "cosT": np.concatenate([cos, cos]).astype(np.float32),
        "sinT": np.concatenate([-sin, sin]).astype(np.float32),
        "parity": np.stack([(np.arange(P) // HD1) % 2 == e for e in range(2)], axis=1).astype(np.float32),
        "eye": np.eye(P, dtype=np.float32),
        "iota": np.broadcast_to(np.arange(P, dtype=np.float32), (P, P)),
        "tileno": np.broadcast_to(P * np.arange(TOPK * NT, dtype=np.float32), (P, TOPK * NT)),
        "partno": 1 + np.arange(P, dtype=np.float32)[:, None],
        "spare": (PICKS + np.arange(P)[:, None] + P * np.arange(COLS + DUMMY)[None, :]).astype(np.float32),
        "limits": np.broadcast_to(np.arange(T // ST, dtype=np.float32) * ST, (P, T // ST)),
        "below": np.broadcast_to(np.tril(np.ones((NE, NE), np.float32), -1), (P, NE, NE)),
        "ones": np.ones((P, P), np.float16),
        "lower": np.triu(np.ones((P, P), np.float16), 1),
    }
    nc = bacc.Bacc("TRN2", target_bir_lowering=False, num_devices=1)
    given, args = {}, []
    for name, a in arrays.items():
        a = np.ascontiguousarray(a)
        given[f"in_{name}"] = a
        args.append(nc.dram_tensor(f"in_{name}", a.shape, mybir.dt.from_np(a.dtype), kind="ExternalInput").ap())
    args.append(nc.dram_tensor("scratch_x", (T, 2 * D), F16, kind="Internal").ap())
    args.append(nc.dram_tensor("scratch_y", (PICKS + (COLS + DUMMY) * P, D), F32, kind="Internal").ap())
    out = nc.dram_tensor("out_0", (T, D), F32, kind="ExternalOutput").ap()
    build(nc, *args, out)
    r = run_bass_kernel_spmd(nc, [given], core_ids=[0])
    return r.results[0]["out_0"].reshape(B, S, D)
```
